# Optimizing a Trainium2 kernel written in Bass

```python
import numpy as np
import jax
import jax.numpy as jnp

def _softmax(x, axis=-1):
    return jax.nn.softmax(x, axis=axis)

def _gelu(x):
    return jax.nn.gelu(x, approximate=True)

def _silu(x):
    return jax.nn.silu(x)

def _sigmoid(x):
    return jax.nn.sigmoid(x)

def _layernorm(x, axis=-1, eps=1e-05):
    m = jnp.mean(x, axis=axis, keepdims=True)
    v = jnp.var(x, axis=axis, keepdims=True)
    return (x - m) / jnp.sqrt(v + eps)

def _scatter_add(tgt, idx, src, axis=0):
    return tgt.at[idx].add(src)

def _segment_sum(src, seg, n):
    return jax.ops.segment_sum(src, seg, n)
kernel_name = 'mk_gnn_resnorm_d4_gnn_r64_5554bc'

def setup_inputs(seed: int=0):
    np.random.seed(seed)
    _w = jnp.asarray

    def _rec_inputs():
        import jax
        import jax.numpy as jnp
        _gk = jax.random.key(seed)
        x = -0.000202 + 1 * jax.random.normal(jax.random.fold_in(_gk, 1), (100000, 128), jnp.float32)
        src = jax.random.randint(jax.random.fold_in(_gk, 2), (50000,), 0, 100000, jnp.int32)
        dst = jnp.minimum((100000 * jax.random.uniform(jax.random.fold_in(_gk, 3), (50000,)) ** 2.0).astype(jnp.int32), 99999)
        _o = jnp.argsort(dst, stable=True)
        src = src[_o]
        dst = dst[_o]
        edge_attr_10 = 0.000254407 + 0.99978 * jax.random.normal(jax.random.fold_in(_gk, 12), (50000, 10), jnp.float32)
        edge_weight = jax.random.uniform(jax.random.fold_in(_gk, 14), (50000,), jnp.float32, 0.0, 1)
        return (x, src, dst, edge_attr_10, edge_weight)
    x, src, dst, edge_attr_10, edge_weight = _rec_inputs()

    def _L0_gnn_setup():
        import jax, jax.numpy as jnp
        import numpy as np
        N_NODES = 50000
        N_EDGES = 12500
        D = 128
        H = 128

        def _sage_conv(x, src, dst, W_l, b_l, W_r, n_nodes):
            agg = jax.ops.segment_sum(x[src], dst, num_segments=n_nodes)
            cnt = jax.ops.segment_sum(jnp.ones((src.shape[0],), x.dtype), dst, num_segments=n_nodes)
            mean = agg / jnp.maximum(cnt, 1.0)[:, None]
            out = mean @ W_l + b_l + x @ W_r
            norm = jnp.linalg.norm(out, axis=-1, keepdims=True)
            return out / jnp.maximum(norm, 1e-12)
        key = jax.random.key(seed)
        ks = jax.random.split(key, 8)
        s = 1.0 / np.sqrt(D)
        return {'x': jax.random.normal(ks[0], (N_NODES, D), dtype=jnp.float32), 'edge_index': jax.random.randint(ks[1], (2, N_EDGES), 0, N_NODES, dtype=jnp.int64), 'W1_l': jax.random.normal(ks[2], (D, H), dtype=jnp.float32) * s, 'b1_l': jax.random.normal(ks[3], (H,), dtype=jnp.float32) * s, 'W1_r': jax.random.normal(ks[4], (D, H), dtype=jnp.float32) * s, 'W2_l': jax.random.normal(ks[5], (H, H), dtype=jnp.float32) * s, 'b2_l': jax.random.normal(ks[6], (H,), dtype=jnp.float32) * s, 'W2_r': jax.random.normal(ks[7], (H, H), dtype=jnp.float32) * s}
    _L0_gnn_all = _L0_gnn_setup()
    _L0_gnn_in = {k: v for k, v in _L0_gnn_all.items() if k in ('W1_l', 'b1_l', 'W1_r', 'W2_l', 'b2_l', 'W2_r')}
    del _L0_gnn_all

    def _L1_gnn_setup():
        import jax, jax.numpy as jnp
        import numpy as np
        N_NODES = 50000
        N_EDGES = 9375
        DIM = 128
        N_LAYERS = 4
        key = jax.random.key(seed)
        k_x, k_e, k_wl, k_wr = jax.random.split(key, 4)
        scale = 1.0 / np.sqrt(DIM)
        x = jax.random.normal(k_x, (N_NODES, DIM), dtype=jnp.float32)
        edge_index = jax.random.randint(k_e, (2, N_EDGES), 0, N_NODES, dtype=jnp.int64)
        Wl = jax.random.normal(k_wl, (N_LAYERS, DIM, DIM), dtype=jnp.float32) * scale
        Wr = jax.random.normal(k_wr, (N_LAYERS, DIM, DIM), dtype=jnp.float32) * scale
        b = jnp.zeros((N_LAYERS, DIM), dtype=jnp.float32)
        return {'x': x, 'Wl': Wl, 'Wr': Wr, 'b': b, 'edge_index': edge_index}
    _L1_gnn_all = _L1_gnn_setup()
    _L1_gnn_in = {k: v for k, v in _L1_gnn_all.items() if k in ('Wl', 'Wr', 'b')}
    del _L1_gnn_all

    def _L2_gnn_setup():
        import jax, jax.numpy as jnp
        import numpy as np
        N = 100000
        E = 25000
        DIN = 128
        DOUT = 128
        H = 4
        DS = DOUT // H
        key = jax.random.key(seed)
        ks = jax.random.split(key, 8)
        x = jax.random.normal(ks[0], (N, DIN), dtype=jnp.float32)
        rows = jax.random.randint(ks[1], (E,), 0, N, dtype=jnp.int32)
        cols = jax.random.randint(ks[2], (E,), 0, N, dtype=jnp.int32)
        vals = jnp.ones((E,), dtype=jnp.float32)
        W0 = jax.random.normal(ks[3], (DOUT, DIN), dtype=jnp.float32) * 0.05
        b0 = jax.random.normal(ks[4], (DOUT,), dtype=jnp.float32) * 0.05
        W1 = jax.random.normal(ks[5], (DOUT, DIN), dtype=jnp.float32) * 0.05
        b1 = jax.random.normal(ks[6], (DOUT,), dtype=jnp.float32) * 0.05
        att = jax.random.normal(ks[7], (H, DS), dtype=jnp.float32) * 0.05
        scale = jnp.ones((DOUT,), dtype=jnp.float32)
        offset = jnp.zeros((DOUT,), dtype=jnp.float32)
        return {'x': x, 'rows': rows, 'cols': cols, 'vals': vals, 'W0': W0, 'b0': b0, 'W1': W1, 'b1': b1, 'att': att, 'scale': scale, 'offset': offset}
    _L2_gnn_all = _L2_gnn_setup()
    _L2_gnn_in = {k: v for k, v in _L2_gnn_all.items() if k in ('W0', 'b0', 'W1', 'b1', 'att', 'scale', 'offset')}
    del _L2_gnn_all

    def _L3_gnn_setup():
        import jax, jax.numpy as jnp
        import numpy as np
        N_NODES = 50000
        N_EDGES = 12500
        IN_DIM = 128
        HID = 128
        EDGE_DIM = 10
        BN_EPS = 1e-05
        key = jax.random.key(seed)
        ks = jax.random.split(key, 12)
        s = 0.05
        return {'x': jax.random.normal(ks[0], (N_NODES, IN_DIM), dtype=jnp.float32), 'edge_index': jax.random.randint(ks[1], (2, N_EDGES), 0, N_NODES, dtype=jnp.int32), 'edge_attr': jax.random.normal(ks[2], (N_EDGES, EDGE_DIM), dtype=jnp.float32), 'Wq': jax.random.normal(ks[3], (HID, IN_DIM), dtype=jnp.float32) * s, 'bq': jnp.zeros((HID,), dtype=jnp.float32), 'Wk': jax.random.normal(ks[4], (HID, IN_DIM), dtype=jnp.float32) * s, 'bk': jnp.zeros((HID,), dtype=jnp.float32), 'Wv': jax.random.normal(ks[5], (HID, IN_DIM), dtype=jnp.float32) * s, 'bv': jnp.zeros((HID,), dtype=jnp.float32), 'We': jax.random.normal(ks[6], (HID, EDGE_DIM), dtype=jnp.float32) * s, 'Wskip': jax.random.normal(ks[7], (HID, IN_DIM), dtype=jnp.float32) * s, 'bskip': jnp.zeros((HID,), dtype=jnp.float32), 'gamma': jnp.ones((HID,), dtype=jnp.float32), 'beta': jnp.zeros((HID,), dtype=jnp.float32)}
    _L3_gnn_all = _L3_gnn_setup()
    _L3_gnn_in = {k: v for k, v in _L3_gnn_all.items() if k in ('Wq', 'bq', 'Wk', 'bk', 'Wv', 'bv', 'We', 'Wskip', 'bskip', 'gamma', 'beta')}
    del _L3_gnn_all
    return {'x': x, 'src': src, 'dst': dst, 'edge_attr_10': edge_attr_10, 'edge_weight': edge_weight, 'L0_gnn_W1_l': _L0_gnn_in['W1_l'], 'L0_gnn_b1_l': _L0_gnn_in['b1_l'], 'L0_gnn_W1_r': _L0_gnn_in['W1_r'], 'L0_gnn_W2_l': _L0_gnn_in['W2_l'], 'L0_gnn_b2_l': _L0_gnn_in['b2_l'], 'L0_gnn_W2_r': _L0_gnn_in['W2_r'], 'L1_gnn_Wl': _L1_gnn_in['Wl'], 'L1_gnn_Wr': _L1_gnn_in['Wr'], 'L1_gnn_b': _L1_gnn_in['b'], 'L2_gnn_W0': _L2_gnn_in['W0'], 'L2_gnn_b0': _L2_gnn_in['b0'], 'L2_gnn_W1': _L2_gnn_in['W1'], 'L2_gnn_b1': _L2_gnn_in['b1'], 'L2_gnn_att': _L2_gnn_in['att'], 'L2_gnn_scale': _L2_gnn_in['scale'], 'L2_gnn_offset': _L2_gnn_in['offset'], 'L3_gnn_Wq': _L3_gnn_in['Wq'], 'L3_gnn_bq': _L3_gnn_in['bq'], 'L3_gnn_Wk': _L3_gnn_in['Wk'], 'L3_gnn_bk': _L3_gnn_in['bk'], 'L3_gnn_Wv': _L3_gnn_in['Wv'], 'L3_gnn_bv': _L3_gnn_in['bv'], 'L3_gnn_We': _L3_gnn_in['We'], 'L3_gnn_Wskip': _L3_gnn_in['Wskip'], 'L3_gnn_bskip': _L3_gnn_in['bskip'], 'L3_gnn_gamma': _L3_gnn_in['gamma'], 'L3_gnn_beta': _L3_gnn_in['beta']}

def reference(x, src, dst, edge_attr_10, edge_weight, L0_gnn_W1_l, L0_gnn_b1_l, L0_gnn_W1_r, L0_gnn_W2_l, L0_gnn_b2_l, L0_gnn_W2_r, L1_gnn_Wl, L1_gnn_Wr, L1_gnn_b, L2_gnn_W0, L2_gnn_b0, L2_gnn_W1, L2_gnn_b1, L2_gnn_att, L2_gnn_scale, L2_gnn_offset, L3_gnn_Wq, L3_gnn_bq, L3_gnn_Wk, L3_gnn_bk, L3_gnn_Wv, L3_gnn_bv, L3_gnn_We, L3_gnn_Wskip, L3_gnn_bskip, L3_gnn_gamma, L3_gnn_beta):
    import jax
    import jax.numpy as jnp

    def _L0_gnn_ref(x, edge_index, W1_l, b1_l, W1_r, W2_l, b2_l, W2_r):
        import jax, jax.numpy as jnp
        import numpy as np
        N_NODES = 50000
        N_EDGES = 12500
        D = 128
        H = 128

        def _sage_conv(x, src, dst, W_l, b_l, W_r, n_nodes):
            agg = jax.ops.segment_sum(x[src], dst, num_segments=n_nodes)
            cnt = jax.ops.segment_sum(jnp.ones((src.shape[0],), x.dtype), dst, num_segments=n_nodes)
            mean = agg / jnp.maximum(cnt, 1.0)[:, None]
            out = mean @ W_l + b_l + x @ W_r
            norm = jnp.linalg.norm(out, axis=-1, keepdims=True)
            return out / jnp.maximum(norm, 1e-12)
        src, dst = (edge_index[0], edge_index[1])
        n = x.shape[0]
        h = jax.nn.relu(_sage_conv(x, src, dst, W1_l, b1_l, W1_r, n))
        h = jax.nn.relu(_sage_conv(h, src, dst, W2_l, b2_l, W2_r, n))
        return h

    def _L1_gnn_ref(x, Wl, Wr, b, edge_index):
        import jax, jax.numpy as jnp
        import numpy as np
        N_NODES = 50000
        N_EDGES = 9375
        DIM = 128
        N_LAYERS = 4
        src, dst = (edge_index[0], edge_index[1])
        n = x.shape[0]
        ones = jnp.ones((src.shape[0],), dtype=x.dtype)
        deg = jax.ops.segment_sum(ones, dst, num_segments=n)
        inv_deg = 1.0 / jnp.maximum(deg, 1.0)

        def sage_conv(h, W_l, W_r, bias):
            agg = jax.ops.segment_sum(h[src], dst, num_segments=n) * inv_deg[:, None]
            return jax.nn.relu(agg @ W_l + h @ W_r + bias)
        h = x
        for i in range(Wl.shape[0]):
            h = sage_conv(h, Wl[i], Wr[i], b[i])
        return h

    def _L2_gnn_ref(x, rows, cols, vals, W0, b0, W1, b1, att, scale, offset):
        import jax, jax.numpy as jnp
        import numpy as np
        N = 100000
        E = 25000
        DIN = 128
        DOUT = 128
        H = 4
        DS = DOUT // H
        n = x.shape[0]
        feat_src = (x @ W0.T + b0).reshape(n, H, DS)
        el = jax.nn.leaky_relu(jnp.einsum('nhd,hd->nh', feat_src, att), 0.2)
        el_e = el[cols]
        mx = jax.ops.segment_max(el_e, rows, num_segments=n)
        ev = jnp.exp(el_e - mx[rows]) * vals[:, None]
        denom = jnp.clip(jax.ops.segment_sum(ev, rows, num_segments=n), 1e-10)
        num = jax.ops.segment_sum(ev[:, :, None] * feat_src[cols], rows, num_segments=n)
        feat_aggr = (num / denom[:, :, None]).reshape(n, H * DS)
        feat_self = x @ W1.T + b1
        h = jax.nn.relu(feat_aggr + feat_self)
        mean = h.mean(axis=1, keepdims=True)
        var = h.var(axis=1, keepdims=True)
        return (h - mean) * jax.lax.rsqrt(var + 1e-09) * scale[None, :] + offset[None, :]

    def _L3_gnn_ref(x, edge_index, edge_attr, Wq, bq, Wk, bk, Wv, bv, We, Wskip, bskip, gamma, beta):
        import jax, jax.numpy as jnp
        import numpy as np
        N_NODES = 50000
        N_EDGES = 12500
        IN_DIM = 128
        HID = 128
        EDGE_DIM = 10
        BN_EPS = 1e-05
        N = x.shape[0]
        d = Wq.shape[0]
        src, dst = (edge_index[0], edge_index[1])
        q_all = x @ Wq.T + bq
        k_all = x @ Wk.T + bk
        v_all = x @ Wv.T + bv
        e = edge_attr @ We.T
        q = q_all[dst]
        k = k_all[src] + e
        v = v_all[src] + e
        scale = 1.0 / jnp.sqrt(jnp.asarray(d, dtype=x.dtype))
        alpha = (q * k).sum(-1) * scale
        amax = jax.ops.segment_max(alpha, dst, num_segments=N)
        ex = jnp.exp(alpha - amax[dst])
        denom = jax.ops.segment_sum(ex, dst, num_segments=N)
        w = ex / denom[dst]
        agg = jax.ops.segment_sum(v * w[:, None], dst, num_segments=N)
        out = agg + x @ Wskip.T + bskip
        h = jax.nn.relu(out)
        mean = h.mean(0)
        var = ((h - mean) ** 2).mean(0)
        return gamma * (h - mean) * jax.lax.rsqrt(var + BN_EPS) + beta
    edge_index = jnp.stack([src, dst])
    x = _layernorm(x + _L0_gnn_ref(x, edge_index, L0_gnn_W1_l, L0_gnn_b1_l, L0_gnn_W1_r, L0_gnn_W2_l, L0_gnn_b2_l, L0_gnn_W2_r), axis=-1)
    x = _layernorm(x + _L1_gnn_ref(x, L1_gnn_Wl, L1_gnn_Wr, L1_gnn_b, edge_index), axis=-1)
    x = _layernorm(x + _L2_gnn_ref(x, src, dst, edge_weight, L2_gnn_W0, L2_gnn_b0, L2_gnn_W1, L2_gnn_b1, L2_gnn_att, L2_gnn_scale, L2_gnn_offset), axis=-1)
    x = _layernorm(x + _L3_gnn_ref(x, edge_index, edge_attr_10, L3_gnn_Wq, L3_gnn_bq, L3_gnn_Wk, L3_gnn_bk, L3_gnn_Wv, L3_gnn_bv, L3_gnn_We, L3_gnn_Wskip, L3_gnn_bskip, L3_gnn_gamma, L3_gnn_beta), axis=-1)
    return x

_drawn_inputs = setup_inputs


def setup_inputs(seed=0):
    import zlib

    import numpy as np

    out = dict(_drawn_inputs(seed))
    spreads = {'L1_gnn_b': (0.0, 0.1),
     'L2_gnn_scale': (1.0, 0.2),
     'L2_gnn_offset': (0.0, 0.1),
     'L3_gnn_bq': (0.0, 0.8),
     'L3_gnn_bk': (0.0, 0.8),
     'L3_gnn_bv': (0.0, 0.1),
     'L3_gnn_bskip': (0.0, 0.1),
     'L3_gnn_gamma': (1.0, 0.2),
     'L3_gnn_beta': (0.0, 0.1)}
    factors = {'L0_gnn_W1_l': 3.781, 'L0_gnn_b1_l': 8.0, 'L2_gnn_att': 4.931}
    for name, (base, spread) in spreads.items():
        noise = np.random.default_rng([zlib.crc32(name.encode()), seed]).standard_normal(out[name].shape)
        drawn = base * np.exp(spread * noise) if base else spread * noise
        out[name] = jnp.asarray(drawn.astype(out[name].dtype))
    for name, factor in factors.items():
        out[name] = (out[name] * factor).astype(out[name].dtype)
    return out
```

```python
from contextlib import ExitStack

import concourse.bass as bass
from concourse import mybir

F32 = mybir.dt.float32
I32 = mybir.dt.int32
U8 = mybir.dt.uint8
BF16 = mybir.dt.bfloat16
ALU = mybir.AluOpType
ACT = mybir.ActivationFunctionType
AX_X = mybir.AxisListType.X

P = 128
RPP = 4
GROUP = P * RPP
UNIT = 2 * GROUP
CPB = 4
BLOCK = P * CPB
BIG = 1e30
LN_EPS = 1e-5
LOW_BITS = 9
DIGITS = 1 << LOW_BITS
REC = 4


class Stage:

    def __init__(self, sems, rounds, per_round, step=1):
        self.sems, self.rounds, self.per_round, self.step = sems, rounds, per_round, step

    def __getitem__(self, slot):
        return self.sems[slot]

    def at(self, r, n):
        before = len([x for x in self.rounds if x < r]) * self.per_round
        return (n + before) * self.step


def gnn_kernel(nc, io, out):
    N = io["x"].shape[0]
    E = io["src"].shape[0]
    D = io["x"].shape[1]
    EDIM = io["edge_attr_10"].shape[1]
    HEADS, HDIM = io["L2_gnn_att"].shape
    assert D == P and HEADS * HDIM == D
    UNITS = N // UNIT
    TAILP = (N - UNITS * UNIT - GROUP) // RPP
    assert UNITS * UNIT + GROUP + TAILP * RPP == N and 0 < TAILP <= P
    BLOCKS = -(-E // BLOCK)
    BLOCKS += BLOCKS % 2
    PAIRS = BLOCKS // 2
    EPAD = BLOCKS * BLOCK
    FULLB = E // BLOCK
    RESTE = E - FULLB * BLOCK
    assert FULLB == BLOCKS - 1 and 1 < RESTE < BLOCK
    NOWHERE = 1 << 17
    assert N <= NOWHERE and NOWHERE >> LOW_BITS < DIGITS
    SHIFT = UNIT.bit_length() - 1

    SAGE, GAT, TR = "sage", "gat", "tr"
    dram = {n: nc.dram_tensor(n, [N, D], F32).ap() for n in ("node_a", "node_b", "node_x", "agg0", "agg1")}
    x_in, node_a, node_b, node_x = io["x"], dram["node_a"], dram["node_b"], dram["node_x"]
    agg = [dram["agg0"], dram["agg1"]]
    w1 = [io["L1_gnn_Wl"][k] for k in range(4)]
    v1 = [io["L1_gnn_Wr"][k] for k in range(4)]
    c1 = [io["L1_gnn_b"][k:k + 1, :] for k in range(4)]

    def row(v):
        return v.unsqueeze(0)

    ROUNDS = [
        (SAGE, "norm", x_in, None, node_a, io["L0_gnn_W1_l"], io["L0_gnn_W1_r"], row(io["L0_gnn_b1_l"])),
        (SAGE, "norm_ln", node_a, x_in, node_x, io["L0_gnn_W2_l"], io["L0_gnn_W2_r"], row(io["L0_gnn_b2_l"])),
        (SAGE, "relu", node_x, None, node_a, w1[0], v1[0], c1[0]),
        (SAGE, "relu", node_a, None, node_b, w1[1], v1[1], c1[1]),
        (SAGE, "relu", node_b, None, node_a, w1[2], v1[2], c1[2]),
        (SAGE, "relu_ln", node_a, node_x, node_b, w1[3], v1[3], c1[3]),
        (GAT, "gat", node_b, None, node_x, None, io["L2_gnn_W1"], row(io["L2_gnn_b1"])),
        (TR, "tr", node_x, None, node_a, None, io["L3_gnn_Wskip"], row(io["L3_gnn_bskip"])),
    ]
    NR = len(ROUNDS)
    R_GAT, R_TR, R_OUT = 6, 7, 8
    sage_rounds = [r for r in range(NR) if ROUNDS[r][0] == SAGE]
    soft_rounds = [R_GAT, R_TR]
    all_edges = list(range(NR))
    all_dense = list(range(NR))
    all_store = list(range(NR + 1))
    tails = {k: [r for r in range(NR) if ROUNDS[r][1] == k] for k in ("norm", "norm_ln", "relu", "relu_ln", "gat", "tr")}
    norm_rounds = tails["norm"] + tails["norm_ln"]
    t1_rounds = tails["norm_ln"] + tails["gat"]
    ln_rounds = sorted(tails["norm_ln"] + tails["relu_ln"] + tails["gat"] + [R_OUT])
    res_rounds = tails["norm_ln"] + tails["relu_ln"]

    with ExitStack() as ctx:
        def sb(name, shape, dt=F32):
            return ctx.enter_context(nc.sbuf_tensor(name, shape, dt))

        def sb2(name, shape, dt=F32):
            return [sb(f"{name}{k}", shape, dt) for k in range(2)]

        def sem(name):
            return ctx.enter_context(nc.semaphore(name))

        def edge_stage(name, rounds, step=1):
            return Stage([sem(f"{name}{k}") for k in range(2)], rounds, PAIRS, step)

        def unit_stage(name, rounds, step=1):
            return Stage([sem(f"{name}{k}") for k in range(2)], rounds, UNITS + 1, step)

        keep_dram = [nc.dram_tensor(f"keep_dram{t}", [EPAD], U8).ap() for t in range(2)]
        weight_dram = nc.dram_tensor("weight_dram", [EPAD], F32).ap()
        rec_dram = [nc.dram_tensor(f"rec_dram{t}", [EPAD, REC], F32).ap() for t in range(2)]
        attr_dram = nc.dram_tensor("attr_dram", [EPAD, EDIM], F32).ap()

        ident = sb("ident", [P, P])
        ones_row = sb("ones_row", [1, P])
        score_ones = sb("score_ones", [P, P])
        head_mask = sb("head_mask", [P, P])
        head_pick = sb("head_pick", [P, HEADS])
        keep = sb("keep", [P, EPAD], U8)
        idx = [sb(f"idx{t}", [P, BLOCKS + 2, 3 * CPB], I32) for t in range(2)]
        inv = sb("inv", [P, BLOCKS, CPB])
        unit_end = [sb(f"unit_end{t}", [1, PAIRS + 1], I32) for t in range(2)]
        zeros = sb("zeros", [P, 16 * P])
        w_l = {r: sb(f"w_l{r}", [P, P]) for r in sage_rounds}
        w_r = {r: sb(f"w_r{r}", [P, P]) for r in range(NR)}
        b_row = {r: sb(f"b_row{r}", [1, P]) for r in range(NR)}
        natural = {n: sb(f"nat_{n}", [P, P]) for n in ("W0", "W1", "Wq", "Wk", "Wv", "Wskip")}
        we_nat = sb("we_nat", [P, EDIM])
        w0_t, wq_t, wk_t, wv_t = sb("w0_t", [P, P]), sb("wq_t", [P, P]), sb("wk_t", [P, P]), sb("wv_t", [P, P])
        we_t = sb("we_t", [EDIM, P])
        att_rep = sb("att_rep", [P, P])
        w_att = sb("w_att", [P, P])
        cols = sb("cols", [P, 8])
        C_ATT, C_B0, C_BQ, C_BK, C_BV, C_GAMMA, C_BETA, C_BATT = range(8)
        scale_bc, offset_bc = sb("scale_bc", [P, P]), sb("offset_bc", [P, P])
        bn_stat = sb("bn_stat", [P, 2 * (UNITS + 1), 6])
        bn_work = sb("bn_work", [P, 8])
        bn_a, bn_b = sb("bn_a", [P, P]), sb("bn_b", [P, P])
        arena_at = [0]

        def in_arena(parts, shape, dt=F32):
            count = 1
            for size in shape:
                count *= size
            nbytes = count * mybir.dt.size(dt)
            at = arena_at[0]
            arena_at[0] += -(-nbytes // 32) * 32
            assert arena_at[0] <= EPAD
            t = keep[0:parts, at:at + nbytes].bitcast(dt)
            if len(shape) == 2:
                t = t.rearrange("p (a b) -> p a b", a=shape[0])
            if len(shape) == 3:
                t = t.rearrange("p (a b c) -> p a b c", a=shape[0], b=shape[1])
            return t

        def block_table(dt=F32):
            return in_arena(BLOCKS, [BLOCK], dt)

        src_i, digit_i, keep_u = block_table(I32), block_table(I32), block_table(U8)
        key_f, other_f, wt_f, keep_f, scat_f, keyc_f, otherc_f = (block_table() for _ in range(7))
        inv_f = digit_f = block_table()
        arena_rec = arena_at[0]
        dst_i, place_i, pos_f, start_f = block_table(I32), block_table(I32), block_table(), block_table()
        arena_at[0] = arena_rec
        rec_f = in_arena(BLOCKS, [BLOCK, REC])
        before_f, after_f = sb("before_f", [BLOCKS, 1]), sb("after_f", [BLOCKS, 1])
        carry_col, carry_row = sb("carry_col", [BLOCKS, 1]), sb("carry_row", [1, BLOCKS + 1])
        rec_t = in_arena(P, [BLOCKS, CPB, REC])
        digit_t = in_arena(P, [BLOCKS, CPB])
        iota_i, iota_f = in_arena(P, [DIGITS], I32), in_arena(P, [DIGITS])
        onehot = [in_arena(P, [DIGITS], BF16) for k in range(CPB)]
        picked = in_arena(P, [DIGITS])
        before_ones, rest_ones = sb("before_ones", [P, P], BF16), sb("rest_ones", [P, P], BF16)
        all_ones, no_ones = sb("all_ones", [P, P], BF16), sb("no_ones", [P, P], BF16)
        place_f = sb("place_f", [P, CPB])
        place_idx, rec_rows = sb2("place_idx", [P, CPB], I32), sb2("rec_rows", [P, CPB, REC])
        g_idx = sb2("g_idx", [P, 2 * CPB], I32)
        s_idx = sb2("s_idx", [P, CPB], I32)
        gath = sb2("gath", [P, CPB, P])
        gath_d = sb2("gath_d", [P, CPB, P])
        run = sb2("run", [P, BLOCK])
        y_rows = sb2("y_rows", [P, CPB, P])
        seg_max, den, num = sb2("seg_max", [P, BLOCK]), sb2("den", [P, BLOCK]), run
        gsrc_t, gdst_t = sb("gsrc_t", [P, BLOCK]), sb("gdst_t", [P, BLOCK])
        attr = sb2("attr", [P, CPB, EDIM])
        attr_t = sb("attr_t", [EDIM, BLOCK])
        wt_bc = sb2("wt_bc", [P, BLOCK])
        start_neg = sb("start_neg", [P, BLOCK + 1])
        logit_raw, logit, full_max, shifted, expd, weighted, msg = (
            sb(n, [P, BLOCK]) for n in ("logit_raw", "logit", "full_max", "shifted", "expd", "weighted", "msg"))
        prod = logit
        carry = sb("carry", [P, 4])
        den_inv = sb("den_inv", [P, 2, CPB * HEADS])
        h_in, agg_in, res_in = sb2("h_in", [P, RPP, P]), sb2("agg_in", [P, RPP, P]), sb2("res_in", [P, RPP, P])
        h_t = sb2("h_t", [P, RPP, P])
        total, t1, t2 = sb2("total", [P, RPP, P]), sb2("t1", [P, RPP, P]), sb2("t2", [P, RPP, P])
        h_out = sb2("h_out", [P, RPP, P])
        sq = sb2("sq", [P, RPP, P])
        small = sb2("small", [P, 6, RPP])
        st6, mv = sb2("st6", [P, RPP, 6]), sb2("mv", [P, RPP, 2])
        pe_bank = [ctx.enter_context(nc.psum_tensor(f"edge_bank{k}", [P, BLOCK], F32)) for k in range(4)]
        ht_bank = [ctx.enter_context(nc.psum_tensor(f"ht_bank{k}", [P, GROUP], F32)) for k in range(2)]
        o_bank = [ctx.enter_context(nc.psum_tensor(f"o_bank{k}", [P, GROUP], F32)) for k in range(2)]

        filled, loaded, prep, prep_pe, prep_act, prep_pool = (sem(n) for n in ("filled", "loaded", "prep", "prep_pe", "prep_act", "prep_pool"))
        zeroed, keep_out, keep_in, padded, tables_done = (sem(n) for n in ("zeroed", "keep_out", "keep_in", "padded", "tables_done"))
        key_ready = sem("key_ready")
        ends_in = sem("ends_in")
        keep_ready = sem("keep_ready")
        att_ready = sem("att_ready")
        last_start, first_start = sem("last_start"), sem("first_start")
        last_start_t, first_start_t = sem("last_start_t"), sem("first_start_t")
        tab_ready, tab_t = sem("tab_ready"), sem("tab_t")
        tab_used = sem("tab_used")
        sort_ready, sort_t, sort_used = sem("sort_ready"), sem("sort_t"), sem("sort_used")
        hot = sem("hot")
        counted = [sem(f"counted{k}") for k in range(CPB)]
        ranked, placed = sem("ranked"), sem("placed")
        slot_ready = [sem(f"slot_ready{q}") for q in range(2)]
        rec_out = [sem(f"rec_out{q}") for q in range(2)]
        rec_in = sem("rec_in")
        bn_var, bn_coef = sem("bn_var"), sem("bn_coef")
        pool_turn, sp_turn, dve_turn = sem("pool_turn"), sem("sp_turn"), sem("dve_turn")
        gidx_ready = Stage([sem(f"gidx_ready{q}") for q in range(2)], all_edges, PAIRS + 1)
        sidx_ready = edge_stage("sidx_ready", all_edges)
        gathered = edge_stage("gathered", all_edges, 16 * CPB)
        gathered_d = edge_stage("gathered_d", [R_TR], 16 * CPB)
        scattered = edge_stage("scattered", all_edges, 16 * CPB)
        gt_ready = edge_stage("gt_ready", all_edges)
        run_ready = edge_stage("run_ready", sage_rounds)
        yp_ready = edge_stage("yp_ready", all_edges)
        y_ready = edge_stage("y_ready", all_edges)
        gts_ready = edge_stage("gts_ready", soft_rounds)
        lin_ready = edge_stage("lin_ready", soft_rounds)
        raw_ready = edge_stage("raw_ready", soft_rounds)
        neg_ready = edge_stage("neg_ready", soft_rounds)
        prod_ready = edge_stage("prod_ready", [R_TR])
        score_ready = edge_stage("score_ready", [R_TR])
        shift_ready = edge_stage("shift_ready", soft_rounds)
        exp_ready = edge_stage("exp_ready", soft_rounds)
        sums_ready = edge_stage("sums_ready", soft_rounds)
        extra_in = edge_stage("extra_in", soft_rounds, 16)
        h_loaded = unit_stage("h_loaded", all_store, 16)
        agg_loaded = unit_stage("agg_loaded", all_store, 16)
        res_loaded = unit_stage("res_loaded", res_rounds, 16)
        htp_ready = unit_stage("htp_ready", all_dense)
        ht_ready = unit_stage("ht_ready", all_dense)
        mm_ready = unit_stage("mm_ready", all_dense)
        sum_ready = unit_stage("sum_ready", all_dense)
        sq_ready = unit_stage("sq_ready", norm_rounds)
        ss_ready = unit_stage("ss_ready", norm_rounds)
        nrm_ready = unit_stage("nrm_ready", norm_rounds)
        t1_ready = unit_stage("t1_ready", t1_rounds)
        t2_ready = unit_stage("t2_ready", ln_rounds)
        var_ready = unit_stage("var_ready", ln_rounds)
        sd_ready = unit_stage("sd_ready", ln_rounds)
        gvar_ready = unit_stage("gvar_ready", tails["gat"])
        gat_off = unit_stage("gat_off", tails["gat"])
        gsd_ready = unit_stage("gsd_ready", tails["gat"])
        out_ready = unit_stage("out_ready", all_store)
        stored = unit_stage("stored", all_store, 16)
        hot_ready = unit_stage("hot_ready", [R_TR])
        bn_ready = unit_stage("bn_ready", [R_TR])
        edge_steps = sem("edge_steps")
        unit_steps = sem("unit_steps")

        class Steps:

            def __init__(self, dve, semaphore, base, per, iteration):
                self.dve, self.sem, self.value, self.n, self.per = dve, semaphore, base + iteration * per, 0, per

            def mark(self, instruction):
                instruction.then_inc(self.sem, 1)
                self.n += 1

            def wait(self):
                self.dve.wait_ge(self.sem, self.value + self.n)

            def done(self, instruction):
                self.mark(instruction)
                self.wait()

            def end(self):
                assert self.n == self.per

        def unit_rows(t):
            return t[0:UNITS * UNIT].rearrange("(u h p j) f -> u h p (j f)", h=2, p=P, j=RPP)

        def group_dram(t, u, s):
            if isinstance(u, int):
                assert u == UNITS
                first = UNITS * UNIT + s * GROUP
                p = P if s == 0 else TAILP
                return t[first:first + p * RPP].rearrange("(p j) f -> p (j f)", j=RPP)
            return unit_rows(t)[bass.ds(u, 1), s].rearrange("o p f -> (o p) f")

        def width(u, s):
            return TAILP if isinstance(u, int) and s == 1 else P

        def flat(t, p=P):
            return t[0:p].rearrange("p j f -> p (j f)")

        def bc_rows(t, p):
            return t[0:p].unsqueeze(1).to_broadcast([p, RPP, P])

        def order(r):
            return 1 if ROUNDS[r][0] == GAT else 0

        def schedule(eng, r, edge_pair, before_units, unit):
            end = unit_end[order(r)]
            with eng.Fori(0, PAIRS) as i:
                edge_pair(i)
                before_units(i)
                lo = eng.value_load(end[0:1, bass.ds(i, 1)], min_val=0, max_val=UNITS - 1)
                hi = eng.value_load(end[0:1, bass.ds(i + 1, 1)], min_val=0, max_val=UNITS - 1)
                with eng.If(lo < hi):
                    with eng.Fori(lo, hi) as u:
                        unit(u)
            before_units(PAIRS)
            lo = eng.value_load(end[0:1, PAIRS:PAIRS + 1], min_val=0, max_val=UNITS - 1)
            with eng.Fori(lo, UNITS) as u:
                unit(u)
            unit(UNITS)

        PREP_W = [("W0", pe_bank[0], 0), ("W1", pe_bank[0], P), ("Wq", pe_bank[1], 0), ("Wk", pe_bank[1], P),
                  ("Wv", pe_bank[2], 0), ("Wskip", pe_bank[2], P)]
        big_zero = [(n * P * 16, P, 16) for n in range(N // (P * 16))]
        at_zero = len(big_zero) * P * 16
        while at_zero < N:
            big_zero.append((at_zero, min(P, (N - at_zero) // RPP), RPP))
            at_zero += big_zero[-1][1] * RPP
        ZERO_DMAS = 2 * len(big_zero)

        ctx.enter_context(nc.allow_non_contiguous_dma(reason="vectors as columns and every 1024th destination, once"))
        block = ctx.enter_context(nc.Block())

        FILLS = 9
        LOADS = []
        keep_loads = [r for r in range(NR) if r == 0 or order(r) != order(r - 1)]

        @block.sync
        def _(sp):
            sp.wait_ge(filled, FILLS)
            dst, src = io["dst"], io["src"]

            def load(to, of):
                sp.dma_start(to, of).then_inc(loaded, 16)
                LOADS.append(1)

            load(dst_i[0:FULLB], dst[0:FULLB * BLOCK].rearrange("(p j) -> p j", j=BLOCK))
            load(dst_i[FULLB:FULLB + 1, 0:RESTE], row(dst[FULLB * BLOCK:E]))
            load(src_i[0:FULLB], src[0:FULLB * BLOCK].rearrange("(p j) -> p j", j=BLOCK))
            load(src_i[FULLB:FULLB + 1, 0:RESTE], row(src[FULLB * BLOCK:E]))
            load(wt_f[0:FULLB], io["edge_weight"][0:FULLB * BLOCK].rearrange("(p j) -> p j", j=BLOCK))
            load(wt_f[FULLB:FULLB + 1, 0:RESTE], row(io["edge_weight"][FULLB * BLOCK:E]))
            for r in range(NR):
                _, _, _, _, _, wl, wr, b = ROUNDS[r]
                if wl is not None:
                    load(w_l[r][:], wl)
                    load(w_r[r][:], wr)
                load(b_row[r][:], b)
            for n, t in (("W0", "L2_gnn_W0"), ("W1", "L2_gnn_W1"), ("Wq", "L3_gnn_Wq"), ("Wk", "L3_gnn_Wk"),
                         ("Wv", "L3_gnn_Wv"), ("Wskip", "L3_gnn_Wskip")):
                load(natural[n][:], io[t])
            load(we_nat[:], io["L3_gnn_We"])
            load(cols[:, C_ATT:C_ATT + 1], io["L2_gnn_att"].rearrange("h d -> (h d)").unsqueeze(1))
            for c, t in ((C_B0, "L2_gnn_b0"), (C_BQ, "L3_gnn_bq"), (C_BK, "L3_gnn_bk"), (C_BV, "L3_gnn_bv"),
                         (C_GAMMA, "L3_gnn_gamma"), (C_BETA, "L3_gnn_beta")):
                load(cols[:, c:c + 1], io[t].unsqueeze(1))
            load(scale_bc[:], row(io["L2_gnn_scale"]).to_broadcast([P, P]))
            load(offset_bc[:], row(io["L2_gnn_offset"]).to_broadcast([P, P]))
            sp.dma_start(attr_dram[0:E].rearrange("(a b) f -> a (b f)", a=16),
                         io["edge_attr_10"].rearrange("(a b) f -> a (b f)", a=16)).then_inc(padded, 16)
            sp.dma_start(row(attr_dram[E:EPAD].rearrange("a f -> (a f)")),
                         zeros[0:1, 0:(EPAD - E) * EDIM]).then_inc(padded, 16)
            for t in range(2):
                if t == 1:
                    for n in range(2):
                        for q in range(2):
                            sp.wait_ge(rec_out[q], (n + 1) * PAIRS * CPB * 16)
                        if n == 1:
                            sp.wait_ge(sort_ready, 2)
                        sp.dma_start(rec_f[:].rearrange("p j c -> p (j c)"),
                                     rec_dram[n].rearrange("(p j) c -> p (j c)", j=BLOCK)).then_inc(rec_in, 16)
                sp.wait_ge(key_ready, t + 1)
                sp.dma_start(before_f[1:BLOCKS], key_f[0:BLOCKS - 1, BLOCK - 1:BLOCK]).then_inc(ends_in, 16)
                sp.dma_start(after_f[0:BLOCKS - 1], key_f[1:BLOCKS, 0:1]).then_inc(ends_in, 16)
                sp.wait_ge(keep_ready, t + 1)
                sp.dma_start(keep_dram[t].rearrange("(p j) -> p j", j=BLOCK), keep_u[:]).then_inc(keep_out, 16)
            sp.dma_start(weight_dram.rearrange("(p j) -> p j", j=BLOCK), wt_f[:]).then_inc(padded, 16)
            sp.wait_ge(keep_out, 32)
            sp.wait_ge(padded, 48)
            sp.wait_ge(tables_done, 1)

            weight_v = weight_dram.rearrange("(i q e) -> i q e", q=2, e=BLOCK)
            attr_v = attr_dram.rearrange("(i q k p) f -> i q p k f", q=2, k=CPB, p=P)
            for r in range(NR):
                kind, tail, h_of, res_of, _, _, _, _ = ROUNDS[r]
                if r > 0:
                    for s in range(2):
                        sp.wait_ge(stored[s], stored.at(r, 0))
                        sp.sem_inc(sp_turn, 1)
                if r in keep_loads:
                    sp.dma_start(keep[:], row(keep_dram[order(r)]).to_broadcast([P, EPAD])).then_inc(keep_in, 16)

                def edge_pair(i, r=r, kind=kind):
                    if kind == GAT:
                        for q in range(2):
                            sp.wait_ge(sums_ready[q], sums_ready.at(r, i))
                            sp.sem_inc(sp_turn, 1)
                            sp.dma_start(wt_bc[q][:], weight_v[bass.ds(i, 1), q].to_broadcast([P, BLOCK])).then_inc(extra_in[q], 16)
                    if kind == TR:
                        for q in range(2):
                            sp.wait_ge(sums_ready[q], sums_ready.at(r, i))
                            sp.sem_inc(sp_turn, 1)
                            sp.dma_start(attr[q][:], attr_v[bass.ds(i, 1), q].rearrange("o p k f -> (o p) k f")).then_inc(extra_in[q], 16)

                def before_units(i, r=r):
                    for q in range(2):
                        sp.wait_ge(scattered[q], scattered.at(r, i))
                    sp.sem_inc(sp_turn, 1)

                def unit(u, r=r, tail=tail, h_of=h_of, res_of=res_of):
                    for s in range(2):
                        p = width(u, s)
                        sp.wait_ge(htp_ready[s], htp_ready.at(r, u))
                        sp.sem_inc(sp_turn, 1)
                        if tail == "gat":
                            sp.wait_ge(t2_ready[s], t2_ready.at(r, u))
                        sp.sem_inc(sp_turn, 1)
                        sp.dma_start(flat(h_in[s], p), group_dram(h_of, u, s)).then_inc(h_loaded[s], 16)
                        sp.wait_ge(sum_ready[s], sum_ready.at(r, u))
                        sp.sem_inc(sp_turn, 1)
                        sp.dma_start(flat(agg_in[s], p), group_dram(agg[order(r)], u, s)).then_inc(agg_loaded[s], 16)
                        if res_of is not None:
                            sp.wait_ge(t2_ready[s], t2_ready.at(r, u))
                            sp.sem_inc(sp_turn, 1)
                            sp.dma_start(flat(res_in[s], p), group_dram(res_of, u, s)).then_inc(res_loaded[s], 16)

                schedule(sp, r, edge_pair, before_units, unit)

            r = R_OUT
            for s in range(2):
                sp.wait_ge(stored[s], stored.at(r, 0))
                sp.sem_inc(sp_turn, 1)

            def out_unit(u):
                for s in range(2):
                    p = width(u, s)
                    sp.wait_ge(t2_ready[s], t2_ready.at(r, u))
                    sp.sem_inc(sp_turn, 1)
                    sp.dma_start(flat(h_in[s], p), group_dram(node_x, u, s)).then_inc(h_loaded[s], 16)
                    sp.sem_inc(sp_turn, 1)
                    sp.dma_start(flat(agg_in[s], p), group_dram(node_a, u, s)).then_inc(agg_loaded[s], 16)

            with sp.Fori(0, UNITS) as u:
                out_unit(u)
            out_unit(UNITS)

        @block.gpsimd
        def _(pool):
            pool.memset(ident[:], 0.0).then_inc(prep_pool, 1)
            pool.memset(before_ones[:], 0.0).then_inc(prep_pool, 1)
            pool.memset(rest_ones[:], 1.0).then_inc(prep_pool, 1)
            pool.iota(place_i[:], pattern=[[1, BLOCK]], base=0, channel_multiplier=BLOCK).then_inc(prep_pool, 1)
            pool.iota(iota_i[:], pattern=[[1, DIGITS]], base=0, channel_multiplier=0).then_inc(prep_pool, 1)
            pool.wait_ge(prep_pool, 5)
            pool.affine_select(out=ident[:], in_=ident[:], compare_op=ALU.not_equal, fill=1.0, base=0,
                               pattern=[[-1, P]], channel_multiplier=1).then_inc(prep_pool, 1)
            pool.affine_select(out=before_ones[:], in_=before_ones[:], compare_op=ALU.is_ge, fill=1.0, base=0,
                               pattern=[[-1, P]], channel_multiplier=1).then_inc(prep_pool, 1)
            pool.affine_select(out=rest_ones[:], in_=rest_ones[:], compare_op=ALU.is_ge, fill=0.0, base=0,
                               pattern=[[-1, P]], channel_multiplier=1).then_inc(prep_pool, 1)
            for n in range(2):
                with pool.Fori(0, PAIRS) as i:
                    for q in range(2):
                        pool.wait_ge(slot_ready[q], n * PAIRS + i + 1)
                        pool.sem_inc(pool_turn, 1)
                        for k in range(CPB):
                            pool.indirect_dma_start(rec_dram[n], bass.IndirectOffsetOnAxis(place_idx[q][:, k:k + 1], 0),
                                                    rec_rows[q][:, k, :], None).then_inc(rec_out[q], 16)
            pool.wait_ge(tables_done, 1)
            pool.wait_ge(zeroed, ZERO_DMAS * 16)
            for r in range(NR):
                kind, _, h_of, _, _, _, _, _ = ROUNDS[r]
                if r > 0:
                    for s in range(2):
                        pool.wait_ge(stored[s], stored.at(r, 0))

                def gathers(q, r=r, kind=kind, h_of=h_of):
                    for k in range(CPB):
                        pool.indirect_dma_start(gath[q][:, k, :], None, h_of,
                                                bass.IndirectOffsetOnAxis(g_idx[q][:, k:k + 1], 0)).then_inc(gathered[q], 16)
                    if kind == TR:
                        for k in range(CPB):
                            pool.indirect_dma_start(gath_d[q][:, k, :], None, h_of,
                                                    bass.IndirectOffsetOnAxis(g_idx[q][:, CPB + k:CPB + k + 1], 0)).then_inc(gathered_d[q], 16)

                def scatters(q, r=r):
                    for k in range(CPB):
                        pool.indirect_dma_start(agg[order(r)], bass.IndirectOffsetOnAxis(s_idx[q][:, k:k + 1], 0), y_rows[q][:, k, :],
                                                None, bounds_check=N - 1, oob_is_err=False).then_inc(scattered[q], 16)

                for q in range(2):
                    pool.wait_ge(gidx_ready[q], gidx_ready.at(r, 1))
                    gathers(q)
                with pool.Fori(0, PAIRS - 1) as i:
                    for q in range(2):
                        pool.wait_ge(gt_ready[q], gt_ready.at(r, i + 1))
                        pool.wait_ge(gidx_ready[q], gidx_ready.at(r, i + 2))
                        pool.sem_inc(pool_turn, 1)
                        gathers(q)
                        pool.wait_ge(sidx_ready[q], sidx_ready.at(r, i + 1))
                        pool.wait_ge(y_ready[q], y_ready.at(r, i + 1))
                        pool.sem_inc(pool_turn, 1)
                        scatters(q)
                for q in range(2):
                    pool.wait_ge(sidx_ready[q], sidx_ready.at(r, PAIRS))
                    pool.wait_ge(y_ready[q], y_ready.at(r, PAIRS))
                    scatters(q)

        @block.tensor
        def _(pe):
            pe.wait_ge(prep_pool, 8)
            pe.wait_ge(loaded, 16 * len(LOADS))
            for name, bank, col in PREP_W:
                pe.transpose(bank[:, col:col + P], natural[name][:], ident[:]).then_inc(prep_pe, 1)
            pe.transpose(pe_bank[3][0:EDIM, 0:P], we_nat[:], ident[:]).then_inc(prep_pe, 1)
            pe.wait_ge(att_ready, 1)
            pe.matmul(o_bank[0][:, 0:P], natural["W0"][:], att_rep[:], start=True, stop=True)
            pe.matmul(o_bank[0][:, P:P + 1], att_rep[:], cols[:, C_B0:C_B0 + 1], start=True, stop=True,
                      skip_group_check=True).then_inc(prep_pe, 1)
            pe.wait_ge(prep_act, 9)

            def transposed(tables, semaphore):
                for t, bank in tables:
                    for k in range(CPB):
                        last = pe.transpose(bank[:, k * BLOCKS:(k + 1) * BLOCKS], t[:, k * P:(k + 1) * P],
                                            ident[0:BLOCKS, 0:BLOCKS])
                last.then_inc(semaphore, 1)

            pe.wait_ge(last_start, 1)
            pe.transpose(pe_bank[0][0:1, 0:BLOCKS], carry_col[:], ident[0:BLOCKS, 0:BLOCKS]).then_inc(last_start_t, 1)
            pe.wait_ge(first_start, 1)
            pe.transpose(pe_bank[1][0:BLOCKS, 0:1], carry_row[:, 0:BLOCKS], ident[0:1, 0:1]).then_inc(first_start_t, 1)
            for t in range(2):
                pe.wait_ge(tab_ready, t + 1)
                pe.transpose(pe_bank[1][0:1, 0:BLOCKS], key_f[:, 0:1], ident[0:BLOCKS, 0:BLOCKS])
                transposed([(otherc_f, ht_bank[0]), (keyc_f, ht_bank[1]), (scat_f, o_bank[1])]
                           + ([(inv_f, pe_bank[0])] if t == 0 else []), tab_t)
                if t == 1:
                    break
                for n in range(2):
                    pe.wait_ge(sort_ready, n + 1)
                    pe.wait_ge(tab_used, 1)
                    transposed([(rec_f[:, :, 0] if n else other_f, ht_bank[0]), (rec_f[:, :, 1] if n else key_f, ht_bank[1]),
                                (rec_f[:, :, 2] if n else wt_f, o_bank[1]), (digit_f, pe_bank[0])], sort_t)
                    pe.wait_ge(sort_used, n + 1)
                    rank = pe_bank[2]
                    loop = 2 * n * BLOCKS
                    for k in range(DIGITS // P):
                        pe.matmul(rank[:, k * P:(k + 1) * P], no_ones[:], no_ones[:], start=k == 0, stop=False,
                                  skip_group_check=True)
                    with pe.Fori(0, BLOCKS) as b:
                        for k in range(CPB):
                            pe.wait_ge(hot, (b + loop) * CPB + k + 1)
                            pe.matmul(rank[:], all_ones[:], onehot[k][:], start=False, stop=False,
                                      skip_group_check=True).then_inc(counted[k], 1)
                    loop += BLOCKS
                    with pe.Fori(0, BLOCKS) as b:
                        for k in range(CPB):
                            pe.wait_ge(hot, (b + loop) * CPB + k + 1)
                            pe.matmul(rank[:], before_ones[:], onehot[k][:], start=False, stop=False,
                                      skip_group_check=True).then_inc(ranked, 1)
                            pe.wait_ge(placed, (b + n * BLOCKS) * CPB + k + 1)
                            pe.matmul(rank[:], rest_ones[:], onehot[k][:], start=False, stop=False,
                                      skip_group_check=True).then_inc(counted[k], 1)
            pe.wait_ge(tables_done, 1)

            for r in range(NR):
                kind, tail = ROUNDS[r][0:2]

                def sage_pair(i, r=r):
                    for q in range(2):
                        pe.wait_ge(gathered[q], gathered.at(r, i + 1))
                        pe.wait_ge(run_ready[q], run_ready.at(r, i))
                        for k in range(CPB):
                            last = pe.transpose(pe_bank[q][:, k * P:(k + 1) * P], gath[q][:, k, :], ident[:])
                        last.then_inc(gt_ready[q], 1)
                    for q in range(2):
                        pe.wait_ge(run_ready[q], run_ready.at(r, i + 1))
                        pe.wait_ge(y_ready[q], y_ready.at(r, i))
                        for k in range(CPB):
                            last = pe.matmul(pe_bank[2 + q][:, k * P:(k + 1) * P], run[q][:, k * P:(k + 1) * P],
                                             w_l[r][:], start=True, stop=True, skip_group_check=True)
                        last.then_inc(yp_ready[q], 1)

                def rows_out(i, q, r, bank, den_bank):
                    pe.wait_ge(sums_ready[q], sums_ready.at(r, i + 1))
                    for k in range(CPB):
                        pe.transpose(bank[:, k * P:(k + 1) * P], num[q][:, k * P:(k + 1) * P], ident[:])
                    for k in range(CPB):
                        last = pe.matmul(den_bank[:, k * HEADS:(k + 1) * HEADS], den[q][:, k * P:(k + 1) * P],
                                         head_pick[:], start=True, stop=True, skip_group_check=True)
                    last.then_inc(yp_ready[q], 1)

                def gat_pair(i, r=r):
                    for q in range(2):
                        pe.wait_ge(gathered[q], gathered.at(r, i + 1))
                        pe.wait_ge(y_ready[1 - q], y_ready.at(r, i + q))
                        for k in range(CPB):
                            last = pe.transpose(pe_bank[0][:, k * P:(k + 1) * P], gath[q][:, k, :], ident[:])
                        last.then_inc(gt_ready[q], 1)
                        pe.wait_ge(gts_ready[q], gts_ready.at(r, i + 1))
                        pe.matmul(pe_bank[1][:], w_att[:], gsrc_t[:], start=True, stop=True)
                        pe.matmul(pe_bank[2][:], w0_t[:], gsrc_t[:], start=True, stop=True).then_inc(lin_ready[q], 1)
                        rows_out(i, q, r, pe_bank[0], pe_bank[3])

                def tr_pair(i, r=r):
                    for q in range(2):
                        pe.wait_ge(gathered[q], gathered.at(r, i + 1))
                        pe.wait_ge(gathered_d[q], gathered_d.at(r, i + 1))
                        pe.wait_ge(extra_in[q], extra_in.at(r, i + 1))
                        pe.wait_ge(y_ready[1 - q], y_ready.at(r, i + q))
                        for k in range(CPB):
                            pe.transpose(pe_bank[0][:, k * P:(k + 1) * P], gath[q][:, k, :], ident[:])
                        for k in range(CPB):
                            pe.transpose(pe_bank[1][:, k * P:(k + 1) * P], gath_d[q][:, k, :], ident[:])
                        for k in range(CPB):
                            last = pe.transpose(pe_bank[3][0:EDIM, k * P:(k + 1) * P], attr[q][:, k, :], ident[:])
                        last.then_inc(gt_ready[q], 1)
                        pe.wait_ge(gts_ready[q], gts_ready.at(r, i + 1))
                        pe.matmul(pe_bank[2][:], wk_t[:], gsrc_t[:], start=True, stop=False)
                        pe.matmul(pe_bank[2][:], we_t[:], attr_t[:], start=False, stop=True)
                        pe.matmul(pe_bank[0][:], wq_t[:], gdst_t[:], start=True, stop=True)
                        pe.matmul(pe_bank[1][:], wv_t[:], gsrc_t[:], start=True, stop=False)
                        pe.matmul(pe_bank[1][:], we_t[:], attr_t[:], start=False, stop=True).then_inc(lin_ready[q], 1)
                        pe.wait_ge(prod_ready[q], prod_ready.at(r, i + 1))
                        pe.matmul(pe_bank[3][:], score_ones[:], prod[:], start=True, stop=True).then_inc(score_ready[q], 1)
                        rows_out(i, q, r, pe_bank[2], pe_bank[3])

                def unit(u, r=r, tail=tail):
                    for s in range(2):
                        p = width(u, s)
                        pe.wait_ge(h_loaded[s], h_loaded.at(r, u + 1))
                        pe.wait_ge(ht_ready[s], ht_ready.at(r, u))
                        if tail == "tr":
                            pe.wait_ge(bn_ready[s], bn_ready.at(r, u))
                        for j in range(RPP):
                            last = pe.transpose(ht_bank[s][:, j * P:j * P + p], h_in[s][0:p, j, :], ident[0:p, 0:p])
                        last.then_inc(htp_ready[s], 1)
                    for s in range(2):
                        p = width(u, s)
                        pe.wait_ge(ht_ready[s], ht_ready.at(r, u + 1))
                        pe.wait_ge(sum_ready[s], sum_ready.at(r, u))
                        pe.matmul(o_bank[s][0:p, :], ones_row[:, 0:p], b_row[r][:].unsqueeze(1).to_broadcast([1, RPP, P]),
                                  start=True, stop=False, skip_group_check=True)
                        for j in range(RPP):
                            last = pe.matmul(o_bank[s][0:p, j * P:(j + 1) * P], h_t[s][:, j, 0:p], w_r[r][:],
                                             start=False, stop=j == RPP - 1, skip_group_check=True)
                        last.then_inc(mm_ready[s], 1)
                    if tail == "tr":
                        for s in range(2):
                            p = width(u, s)
                            pe.wait_ge(out_ready[s], out_ready.at(r, u + 1))
                            for j in range(RPP):
                                last = pe.transpose(ht_bank[s][:, j * P:j * P + p], h_out[s][0:p, j, :], ident[0:p, 0:p])
                            last.then_inc(hot_ready[s], 1)

                schedule(pe, r, {SAGE: sage_pair, GAT: gat_pair, TR: tr_pair}[kind], lambda i: None, unit)

            pe.wait_ge(bn_coef, 1)
            for bank, c in ((o_bank[0], 4), (o_bank[1], 5)):
                last = pe.matmul(bank[:, 0:P], bn_work[:, c:c + 1].to_broadcast([P, P]), ident[:], start=True, stop=True)
            last.then_inc(prep_pe, 1)

        @block.scalar
        def _(act):
            act.wait_ge(filled, FILLS)
            for t, first, p, j in [(t, *z) for t in range(2) for z in big_zero]:
                act.dma_start(agg[t][first:first + p * j].rearrange("(p j) f -> p (j f)", j=j),
                              zeros[0:p, 0:j * P]).then_inc(zeroed, 16)
            for to, bank, col in ([(w0_t, pe_bank[0], 0), (w_r[R_GAT], pe_bank[0], P), (wq_t, pe_bank[1], 0),
                                                 (wk_t, pe_bank[1], P), (wv_t, pe_bank[2], 0), (w_r[R_TR], pe_bank[2], P)]):
                act.wait_ge(prep_pe, 7)
                act.activation(to[:], bank[:, col:col + P], ACT.Copy).then_inc(prep_act, 1)
            act.activation(we_t[:], pe_bank[3][0:EDIM, 0:P], ACT.Copy).then_inc(prep_act, 1)
            act.wait_ge(prep_pe, 8)
            act.activation(w_att[:], o_bank[0][:, 0:P], ACT.Copy).then_inc(prep_act, 1)
            act.activation(cols[:, C_BATT:C_BATT + 1], o_bank[0][:, P:P + 1], ACT.Copy).then_inc(prep_act, 1)
            act.wait_ge(tables_done, 1)

            for r in range(NR):
                kind, tail, _, _, h_to, _, _, _ = ROUNDS[r]
                act.wait_ge(keep_in, 16 * len([x for x in keep_loads if x <= r]))

                def sage_pair(i, r=r):
                    for q in range(2):
                        act.wait_ge(yp_ready[q], yp_ready.at(r, i + 1))
                        act.wait_ge(scattered[q], scattered.at(r, i))
                        for k in range(CPB):
                            last = act.activation(y_rows[q][:, k, :], pe_bank[2 + q][:, k * P:(k + 1) * P], ACT.Copy,
                                                  scale=inv[:, bass.ds(2 * i + q, 1), k])
                        last.then_inc(y_ready[q], 1)

                def start_marks(i, q, r):
                    act.wait_ge(shift_ready[1 - q], shift_ready.at(r, i + q))
                    act.activation(start_neg[:, 0:BLOCK], keep[:, bass.ds((2 * i + q) * BLOCK, BLOCK)], ACT.Copy,
                                   scale=BIG, bias=-BIG).then_inc(neg_ready[q], 1)

                def exponentials(i, q, r):
                    act.wait_ge(shift_ready[q], shift_ready.at(r, i + 1))
                    act.wait_ge(sums_ready[1 - q], sums_ready.at(r, i + q))
                    act.activation(carry[:, 1:2], carry[:, 0:1], ACT.Exp)
                    act.activation(expd[:], shifted[:], ACT.Exp).then_inc(exp_ready[q], 1)

                def gat_pair(i, r=r):
                    for q in range(2):
                        start_marks(i, q, r)
                        act.wait_ge(gt_ready[q], gt_ready.at(r, i + 1))
                        act.wait_ge(lin_ready[1 - q], lin_ready.at(r, i + q))
                        act.activation(gsrc_t[:], pe_bank[0][:], ACT.Copy).then_inc(gts_ready[q], 1)
                        act.wait_ge(lin_ready[q], lin_ready.at(r, i + 1))
                        act.activation(logit_raw[:], pe_bank[1][:], ACT.Identity,
                                       bias=cols[:, C_BATT:C_BATT + 1]).then_inc(raw_ready[q], 1)
                        exponentials(i, q, r)

                def tr_pair(i, r=r):
                    for q in range(2):
                        start_marks(i, q, r)
                        act.wait_ge(gt_ready[q], gt_ready.at(r, i + 1))
                        act.wait_ge(lin_ready[1 - q], lin_ready.at(r, i + q))
                        act.activation(gsrc_t[:], pe_bank[0][:], ACT.Copy)
                        act.activation(gdst_t[:], pe_bank[1][:], ACT.Copy)
                        act.activation(attr_t[:], pe_bank[3][0:EDIM, :], ACT.Copy).then_inc(gts_ready[q], 1)
                        act.wait_ge(lin_ready[q], lin_ready.at(r, i + 1))
                        act.activation(logit_raw[:], pe_bank[2][:], ACT.Identity,
                                       bias=cols[:, C_BK:C_BK + 1]).then_inc(raw_ready[q], 1)
                        exponentials(i, q, r)

                def store(u, s, r, h_to):
                    act.wait_ge(out_ready[s], out_ready.at(r, u + 1))
                    act.dma_start(group_dram(h_to, u, s), flat(h_out[s], width(u, s))).then_inc(stored[s], 16)

                def unit(u, r=r, tail=tail, h_to=h_to):
                    for s in range(2):
                        p = width(u, s)
                        act.wait_ge(htp_ready[s], htp_ready.at(r, u + 1))
                        act.wait_ge(mm_ready[s], mm_ready.at(r, u))
                        act.activation(h_t[s][:, :, 0:p], ht_bank[s][:].rearrange("p (j n) -> p j n", j=RPP)[:, :, 0:p],
                                       ACT.Copy).then_inc(ht_ready[s], 1)
                    if tail in ("norm", "norm_ln"):
                        for s in range(2):
                            p = width(u, s)
                            act.wait_ge(sum_ready[s], sum_ready.at(r, u + 1))
                            act.activation(sq[s][0:p], total[s][0:p], ACT.Square).then_inc(sq_ready[s], 1)
                            if tail == "norm_ln":
                                act.activation(t1[s][0:p], total[s][0:p], ACT.Relu).then_inc(t1_ready[s], 1)
                        for s in range(2):
                            p = width(u, s)
                            act.wait_ge(ss_ready[s], ss_ready.at(r, u + 1))
                            act.activation(small[s][0:p, 1, :], small[s][0:p, 0, :], ACT.Sqrt).then_inc(nrm_ready[s], 1)
                    if tail in ("relu", "tr"):
                        for s in range(2):
                            p = width(u, s)
                            act.wait_ge(sum_ready[s], sum_ready.at(r, u + 1))
                            act.wait_ge(stored[s], stored.at(r, u))
                            if tail == "tr":
                                act.wait_ge(hot_ready[s], hot_ready.at(r, u))
                            act.activation(h_out[s][0:p], total[s][0:p], ACT.Relu).then_inc(out_ready[s], 1)
                    if tail == "gat":
                        for s in range(2):
                            p = width(u, s)
                            act.wait_ge(sum_ready[s], sum_ready.at(r, u + 1))
                            act.activation(t1[s][0:p], total[s][0:p], ACT.Relu).then_inc(t1_ready[s], 1)
                        for s in range(2):
                            p = width(u, s)
                            act.wait_ge(gvar_ready[s], gvar_ready.at(r, u + 1))
                            act.activation(small[s][0:p, 1, :], small[s][0:p, 0, :], ACT.Sqrt).then_inc(gsd_ready[s], 1)
                    if tail in ("norm_ln", "relu_ln", "gat"):
                        for s in range(2):
                            roots(u, s, r)
                    for s in range(2):
                        store(u, s, r, h_to)

                def roots(u, s, r):
                    p = width(u, s)
                    act.wait_ge(var_ready[s], var_ready.at(r, u + 1))
                    act.activation(small[s][0:p, 4, :], small[s][0:p, 3, :], ACT.Sqrt).then_inc(sd_ready[s], 1)

                schedule(act, r, {SAGE: sage_pair, GAT: gat_pair, TR: tr_pair}[kind], lambda i: None, unit)

            act.wait_ge(bn_var, 1)
            act.activation(bn_work[:, 3:4], bn_work[:, 2:3], ACT.Sqrt).then_inc(prep_act, 1)

            r = R_OUT

            def out_unit(u):
                for s in range(2):
                    roots(u, s, r)
                for s in range(2):
                    store(u, s, r, out)

            with act.Fori(0, UNITS) as u:
                out_unit(u)
            out_unit(UNITS)
            for s in range(2):
                act.wait_ge(stored[s], stored.at(r, UNITS + 1))

        @block.vector
        def _(dve):
            NW = NOWHERE
            for t, v in ((dst_i[:], NW), (src_i[:], NW), (wt_f[:], 0.0), (zeros[:], 0.0), (ones_row[:], 1.0),
                         (score_ones[:], float(D) ** -0.5), (head_mask[:], 0.0), (head_pick[:], 0.0), (start_neg[:], 0.0)):
                dve.memset(t, v).then_inc(filled, 1)
            dve.wait_ge(filled, FILLS)
            n = [0]

            def done(instruction):
                instruction.then_inc(prep, 1)
                n[0] += 1
                dve.wait_ge(prep, n[0])

            for h in range(HEADS):
                dve.memset(head_mask[h * HDIM:(h + 1) * HDIM, h * HDIM:(h + 1) * HDIM], 1.0)
                dve.memset(head_pick[h * HDIM:h * HDIM + 1, h:h + 1], 1.0)
            for q in range(2):
                for t in (run[q], seg_max[q], den[q]):
                    dve.memset(t[:], 0.0)
                dve.memset(unit_end[q][:], 0)
                dve.memset(idx[q][:, BLOCKS:BLOCKS + 2, :], 0)
            dve.memset(before_f[:], float(NW + 1))
            dve.memset(after_f[:], float(NW))
            dve.memset(all_ones[:], 1.0)
            dve.memset(no_ones[:], 0.0)
            dve.memset(carry[:], 0.0)
            dve.memset(rec_t[:], 0.0)
            done(dve.memset(carry_row[:], 0.0))
            dve.wait_ge(loaded, 16 * len(LOADS))
            done(dve.tensor_scalar(att_rep[:], head_mask[:], cols[:, C_ATT:C_ATT + 1], None, ALU.mult))
            dve.sem_inc(att_ready, 1)
            dve.wait_ge(prep_pool, 8)
            dve.tensor_copy(iota_f[:], iota_i[:])
            dve.tensor_copy(pos_f[:], place_i[:])
            dve.tensor_copy(key_f[:], dst_i[:])
            done(dve.tensor_copy(other_f[:], src_i[:]))

            def by_block(bank):
                return bank[:, 0:CPB * BLOCKS].rearrange("p (k b) -> p b k", k=CPB)

            def build_tables(t):
                dve.sem_inc(key_ready, 1)
                dve.wait_ge(ends_in, 32 * (t + 1))
                dve.tensor_tensor(keep_f[:, 1:BLOCK], key_f[:, 1:BLOCK], key_f[:, 0:BLOCK - 1], ALU.is_equal)
                done(dve.tensor_tensor(keep_f[:, 0:1], key_f[:, 0:1], before_f[:], ALU.is_equal))
                if t == 1:
                    dve.wait_ge(keep_out, 16)
                done(dve.tensor_copy(keep_u[:], keep_f[:]))
                dve.sem_inc(keep_ready, 1)
                dve.tensor_tensor(scat_f[:, 0:BLOCK - 1], key_f[:, 0:BLOCK - 1], key_f[:, 1:BLOCK], ALU.is_equal)
                done(dve.tensor_tensor(scat_f[:, BLOCK - 1:BLOCK], key_f[:, BLOCK - 1:BLOCK], after_f[:], ALU.is_equal))
                dve.scalar_tensor_tensor(scat_f[:], scat_f[:], float(NW), key_f[:], ALU.mult, ALU.add)
                dve.tensor_scalar(keyc_f[:], key_f[:], float(N - 1), None, ALU.min)
                done(dve.tensor_scalar(otherc_f[:], other_f[:], float(N - 1), None, ALU.min))
                if t == 0:
                    done(dve.tensor_tensor(start_f[:], keep_f[:], pos_f[:], ALU.mult))
                    done(dve.tensor_tensor(start_f[:], pos_f[:], start_f[:], ALU.subtract))
                    done(dve.tensor_reduce(carry_col[:], start_f[:], AX_X, ALU.max))
                    dve.sem_inc(last_start, 1)
                    dve.wait_ge(last_start_t, 1)
                    done(dve.tensor_tensor_scan(carry_row[:, 1:BLOCKS + 1], zeros[0:1, 0:BLOCKS],
                                                pe_bank[0][0:1, 0:BLOCKS], 0.0, ALU.add, ALU.max))
                    dve.sem_inc(first_start, 1)
                    dve.wait_ge(first_start_t, 1)
                    done(dve.tensor_copy(carry_col[:], pe_bank[1][0:BLOCKS, 0:1]))
                    done(dve.tensor_tensor_scan(inv_f[:], start_f[:], start_f[:], carry_col[:], ALU.max, ALU.max))
                    done(dve.tensor_tensor(inv_f[:], pos_f[:], inv_f[:], ALU.subtract))
                    done(dve.tensor_scalar(inv_f[:], inv_f[:], 1.0, None, ALU.add))
                    done(dve.reciprocal(inv_f[:], inv_f[:]))
                dve.sem_inc(tab_ready, 1)
                dve.wait_ge(tab_t, t + 1)
                dve.tensor_copy(idx[t][:, 0:BLOCKS, 0:CPB], by_block(ht_bank[0]))
                dve.tensor_copy(idx[t][:, 0:BLOCKS, CPB:2 * CPB], by_block(ht_bank[1]))
                dve.tensor_copy(idx[t][:, 0:BLOCKS, 2 * CPB:3 * CPB], by_block(o_bank[1]))
                if t == 0:
                    dve.tensor_copy(inv[:], by_block(pe_bank[0]))
                end = unit_end[t][0:1, 1:PAIRS + 1]
                done(dve.tensor_copy(end, pe_bank[1][0:1, 0:BLOCKS].rearrange("o (i q) -> o i q", q=2)[:, :, 0]))
                done(dve.tensor_scalar(end, end, SHIFT, None, ALU.logical_shift_right))
                done(dve.tensor_scalar(end, end, float(UNITS - 1), None, ALU.min))
                dve.sem_inc(tab_used, 1)

            build_tables(0)
            for n_pass in range(2):
                if n_pass == 0:
                    done(dve.tensor_scalar(digit_i[:], src_i[:], DIGITS - 1, None, ALU.bitwise_and))
                else:
                    dve.wait_ge(rec_in, 16)
                    done(dve.tensor_copy(src_i[:], rec_f[:, :, 0]))
                    done(dve.tensor_scalar(digit_i[:], src_i[:], LOW_BITS, None, ALU.logical_shift_right))
                done(dve.tensor_copy(digit_f[:], digit_i[:]))
                dve.sem_inc(sort_ready, 1)
                dve.wait_ge(sort_t, n_pass + 1)
                for c, bank in enumerate((ht_bank[0], ht_bank[1], o_bank[1])):
                    dve.tensor_copy(rec_t[:, :, :, c], by_block(bank))
                done(dve.tensor_copy(digit_t[:], by_block(pe_bank[0])))
                dve.sem_inc(sort_used, 1)
                loop = 2 * n_pass * BLOCKS
                with dve.Fori(0, BLOCKS) as b:
                    for k in range(CPB):
                        dve.wait_ge(counted[k], b + loop)
                        dve.tensor_scalar(onehot[k][:], iota_f[:], digit_t[:, bass.ds(b, 1), k], None, ALU.is_gt).then_inc(hot, 1)
                loop += BLOCKS
                with dve.Fori(0, PAIRS) as i:
                    for q in range(2):
                        b = 2 * i + q
                        for k in range(CPB):
                            dve.wait_ge(counted[k], b + loop)
                            dve.tensor_scalar(onehot[k][:], iota_f[:], digit_t[:, bass.ds(b, 1), k], None, ALU.is_equal).then_inc(hot, 1)
                        for k in range(CPB):
                            dve.wait_ge(hot, (b + loop) * CPB + k + 1)
                            dve.wait_ge(ranked, (b + n_pass * BLOCKS) * CPB + k + 1)
                            dve.tensor_tensor_reduce(picked[:], onehot[k][:], pe_bank[2][:], 1.0, 0.0, ALU.mult, ALU.add,
                                                     place_f[:, k:k + 1]).then_inc(placed, 1)
                            dve.wait_ge(placed, (b + n_pass * BLOCKS) * CPB + k + 1)
                        dve.wait_ge(rec_out[q], (i + n_pass * PAIRS) * CPB * 16)
                        dve.tensor_copy(place_idx[q][:], place_f[:])
                        dve.tensor_copy(rec_rows[q][:], rec_t[:, bass.ds(b, 1), :, :].rearrange("p o k c -> p (o k) c")
                                        ).then_inc(slot_ready[q], 1)
            dve.wait_ge(rec_in, 32)
            dve.tensor_copy(key_f[:], rec_f[:, :, 0])
            dve.tensor_copy(other_f[:], rec_f[:, :, 1])
            done(dve.tensor_copy(wt_f[:], rec_f[:, :, 2]))
            build_tables(1)
            dve.wait_ge(prep_act, 9)
            dve.sem_inc(tables_done, 1)

            esteps, usteps = 0, 0
            for r in range(NR):
                kind, tail = ROUNDS[r][0:2]
                eper = {SAGE: 0, GAT: 2 * 10, TR: 2 * 8}[kind]
                uper = {"norm": 2 * 2, "norm_ln": 2 * 5, "relu": 0, "relu_ln": 2 * 3, "gat": 2 * 8, "tr": 0}[tail]

                dve.wait_ge(keep_in, 16 * len([x for x in keep_loads if x <= r]))
                for q in range(2):
                    dve.wait_ge(gathered[q], gathered.at(r, 0))
                    dve.tensor_copy(g_idx[q][:], idx[order(r)][:, q, 0:2 * CPB]).then_inc(gidx_ready[q], 1)

                def next_gather(i, q, r):
                    dve.wait_ge(gathered[q], gathered.at(r, i + 1))
                    if ROUNDS[r][0] == TR:
                        dve.wait_ge(gathered_d[q], gathered_d.at(r, i + 1))
                    dve.tensor_copy(g_idx[q][:], idx[order(r)][:, bass.ds(2 * i + 2 + q, 1), 0:2 * CPB].rearrange("p o k -> p (o k)")
                                    ).then_inc(gidx_ready[q], 1)

                def next_scatter(i, q, r):
                    dve.wait_ge(scattered[q], scattered.at(r, i))
                    dve.tensor_copy(s_idx[q][:], idx[order(r)][:, bass.ds(2 * i + q, 1), 2 * CPB:3 * CPB].rearrange("p o k -> p (o k)")
                                    ).then_inc(sidx_ready[q], 1)

                def keep_of(i, q):
                    return keep[:, bass.ds((2 * i + q) * BLOCK, BLOCK)]

                def sage_pair(i, r=r):
                    for q in range(2):
                        next_gather(i, q, r)
                        dve.wait_ge(gt_ready[q], gt_ready.at(r, i + 1))
                        dve.wait_ge(yp_ready[q], yp_ready.at(r, i))
                        dve.wait_ge(run_ready[1 - q], run_ready.at(r, i + q))
                        dve.tensor_tensor_scan(run[q][:], keep_of(i, q), pe_bank[q][:], run[1 - q][:, BLOCK - 1:BLOCK],
                                               ALU.mult, ALU.add).then_inc(run_ready[q], 1)
                        next_scatter(i, q, r)

                def softmax_sums(i, q, r, st, logits, values, bias_col, weighted_by):
                    before = 1 - q
                    dve.wait_ge(neg_ready[q], neg_ready.at(r, i + 1))
                    st.done(dve.tensor_tensor_scan(seg_max[q][:], start_neg[:, 0:BLOCK], logits, seg_max[before][:, BLOCK - 1:BLOCK],
                                                   ALU.add, ALU.max))
                    st.done(dve.tensor_tensor_scan(full_max[:, ::-1], start_neg[:, BLOCK:0:-1], seg_max[q][:, ::-1], -BIG,
                                                   ALU.add, ALU.max))
                    st.done(dve.tensor_scalar(carry[:, 0:1], seg_max[before][:, BLOCK - 1:BLOCK], full_max[:, 0:1], 0.0,
                                              ALU.subtract, ALU.min))
                    st.mark(dve.tensor_tensor(shifted[:], logits, full_max[:], ALU.subtract))
                    st.wait()
                    dve.sem_inc(shift_ready[q], 1)
                    dve.wait_ge(exp_ready[q], exp_ready.at(r, i + 1))
                    e = expd
                    if weighted_by is not None:
                        dve.wait_ge(extra_in[q], extra_in.at(r, i + 1))
                        st.done(dve.tensor_tensor(weighted[:], expd[:], weighted_by, ALU.mult))
                        e = weighted
                    st.mark(dve.tensor_scalar(carry[:, 2:3], den[before][:, BLOCK - 1:BLOCK], carry[:, 1:2], None, ALU.mult))
                    dve.tensor_scalar(carry[:, 3:4], num[before][:, BLOCK - 1:BLOCK], carry[:, 1:2], None, ALU.mult)
                    st.done(dve.scalar_tensor_tensor(msg[:], values, bias_col, e[:], ALU.add, ALU.mult))
                    dve.tensor_tensor_scan(den[q][:], keep_of(i, q), e[:], carry[:, 2:3], ALU.mult, ALU.add)
                    dve.tensor_tensor_scan(num[q][:], keep_of(i, q), msg[:], carry[:, 3:4], ALU.mult,
                                           ALU.add).then_inc(sums_ready[q], 1)

                def divided_rows(i, q, r, st, bank, den_bank):
                    dve.wait_ge(yp_ready[q], yp_ready.at(r, i + 1))
                    st.done(dve.tensor_scalar(den_inv[:, 0], den_bank[:, 0:CPB * HEADS], 1e-10, None, ALU.max))
                    st.done(dve.reciprocal(den_inv[:, 1], den_inv[:, 0]))
                    dve.wait_ge(scattered[q], scattered.at(r, i))
                    dve.tensor_tensor(y_rows[q][:].rearrange("p k (h d) -> p (k h) d", h=HEADS),
                                      bank[:].rearrange("p (n d) -> p n d", d=HDIM),
                                      den_inv[:, 1].unsqueeze(2).to_broadcast([P, CPB * HEADS, HDIM]),
                                      ALU.mult).then_inc(y_ready[q], 1)

                def gat_pair(i, r=r, base=esteps, per=eper):
                    st = Steps(dve, edge_steps, base, per, i)
                    for q in range(2):
                        next_gather(i, q, r)
                        dve.wait_ge(raw_ready[q], raw_ready.at(r, i + 1))
                        st.done(dve.scalar_tensor_tensor(logit[:], logit_raw[:], 0.2, logit_raw[:], ALU.mult, ALU.max))
                        softmax_sums(i, q, r, st, logit[:], pe_bank[2][:], cols[:, C_B0:C_B0 + 1], wt_bc[q][:])
                        divided_rows(i, q, r, st, pe_bank[0], pe_bank[3])
                        next_scatter(i, q, r)
                    st.end()

                def tr_pair(i, r=r, base=esteps, per=eper):
                    st = Steps(dve, edge_steps, base, per, i)
                    for q in range(2):
                        next_gather(i, q, r)
                        dve.wait_ge(raw_ready[q], raw_ready.at(r, i + 1))
                        dve.scalar_tensor_tensor(prod[:], pe_bank[0][:], cols[:, C_BQ:C_BQ + 1], logit_raw[:], ALU.add,
                                                 ALU.mult).then_inc(prod_ready[q], 1)
                        dve.wait_ge(score_ready[q], score_ready.at(r, i + 1))
                        softmax_sums(i, q, r, st, pe_bank[3][:], pe_bank[1][:], cols[:, C_BV:C_BV + 1], None)
                        divided_rows(i, q, r, st, pe_bank[2], pe_bank[3])
                        next_scatter(i, q, r)
                    st.end()

                def statistics(st, s, p, of):
                    for j in range(RPP):
                        last = dve.bn_stats(st6[s][0:p, j, :], of[0:p, j, :])
                    st.done(last)
                    dve.sem_inc(dve_turn, 1)
                    for j in range(RPP):
                        last = dve.bn_aggr(mv[s][0:p, j, :], st6[s][0:p, j, :])
                    st.done(last)

                def layer_norm(st, u, r, to, stage):
                    for s in range(2):
                        p = width(u, s)
                        statistics(st, s, p, t2[s])
                        dve.tensor_scalar(small[s][0:p, 3, :], mv[s][0:p, :, 1], LN_EPS, None, ALU.add).then_inc(var_ready[s], 1)
                    for s in range(2):
                        p = width(u, s)
                        dve.wait_ge(sd_ready[s], sd_ready.at(r, u + 1))
                        st.done(dve.reciprocal(small[s][0:p, 5, :], small[s][0:p, 4, :]))
                        dve.wait_ge(stored[s], stored.at(r, u))
                        for j in range(RPP):
                            last = dve.tensor_scalar(h_out[s][0:p, j, :], t2[s][0:p, j, :], mv[s][0:p, j, 0:1],
                                                     small[s][0:p, 5, j:j + 1], ALU.subtract, ALU.mult)
                        last.then_inc(out_ready[s], 1)

                def unit(u, r=r, tail=tail, base=usteps, per=uper):
                    st = Steps(dve, unit_steps, base, per, u)
                    for s in range(2):
                        p = width(u, s)
                        dve.wait_ge(mm_ready[s], mm_ready.at(r, u + 1))
                        dve.wait_ge(agg_loaded[s], agg_loaded.at(r, u + 1))
                        dve.wait_ge(out_ready[s], out_ready.at(r, u))
                        dve.tensor_tensor(flat(total[s], p), o_bank[s][0:p, :], flat(agg_in[s], p), ALU.add).then_inc(sum_ready[s], 1)
                    if tail in ("norm", "norm_ln"):
                        for s in range(2):
                            p = width(u, s)
                            dve.wait_ge(sq_ready[s], sq_ready.at(r, u + 1))
                            dve.tensor_reduce(small[s][0:p, 0, :], sq[s][0:p], AX_X, ALU.add).then_inc(ss_ready[s], 1)
                        for s in range(2):
                            p = width(u, s)
                            dve.wait_ge(nrm_ready[s], nrm_ready.at(r, u + 1))
                            st.done(dve.tensor_scalar(small[s][0:p, 2, :], small[s][0:p, 1, :], 1e-12, None, ALU.max))
                            st.done(dve.reciprocal(small[s][0:p, 5, :], small[s][0:p, 2, :]))
                            if tail == "norm":
                                dve.wait_ge(stored[s], stored.at(r, u))
                                for j in range(RPP):
                                    last = dve.tensor_scalar(h_out[s][0:p, j, :], total[s][0:p, j, :], small[s][0:p, 5, j:j + 1],
                                                             0.0, ALU.mult, ALU.max)
                                last.then_inc(out_ready[s], 1)
                            else:
                                dve.wait_ge(t1_ready[s], t1_ready.at(r, u + 1))
                                dve.wait_ge(res_loaded[s], res_loaded.at(r, u + 1))
                                for j in range(RPP):
                                    last = dve.scalar_tensor_tensor(t2[s][0:p, j, :], t1[s][0:p, j, :], small[s][0:p, 5, j:j + 1],
                                                                    res_in[s][0:p, j, :], ALU.mult, ALU.add)
                                last.then_inc(t2_ready[s], 1)
                    if tail == "relu_ln":
                        for s in range(2):
                            p = width(u, s)
                            dve.wait_ge(res_loaded[s], res_loaded.at(r, u + 1))
                            dve.wait_ge(sum_ready[s], sum_ready.at(r, u + 1))
                            dve.scalar_tensor_tensor(flat(t2[s], p), flat(total[s], p), 0.0, flat(res_in[s], p), ALU.max,
                                                     ALU.add).then_inc(t2_ready[s], 1)
                    if tail == "gat":
                        for s in range(2):
                            p = width(u, s)
                            dve.wait_ge(t1_ready[s], t1_ready.at(r, u + 1))
                            statistics(st, s, p, t1[s])
                            dve.tensor_scalar(small[s][0:p, 0, :], mv[s][0:p, :, 1], 1e-9, None, ALU.add).then_inc(gvar_ready[s], 1)
                        for s in range(2):
                            p = width(u, s)
                            dve.wait_ge(gsd_ready[s], gsd_ready.at(r, u + 1))
                            st.done(dve.reciprocal(small[s][0:p, 2, :], small[s][0:p, 1, :]))
                            for j in range(RPP):
                                last = dve.tensor_scalar(t2[s][0:p, j, :], t1[s][0:p, j, :], mv[s][0:p, j, 0:1],
                                                         small[s][0:p, 2, j:j + 1], ALU.subtract, ALU.mult)
                            st.done(last)
                            st.done(dve.tensor_tensor(t2[s][0:p], t2[s][0:p], bc_rows(scale_bc, p), ALU.mult))
                            dve.tensor_tensor(t2[s][0:p], t2[s][0:p], bc_rows(offset_bc, p), ALU.add).then_inc(gat_off[s], 1)
                            dve.wait_ge(gat_off[s], gat_off.at(r, u + 1))
                            dve.tensor_tensor(t2[s][0:p], t2[s][0:p], h_in[s][0:p], ALU.add).then_inc(t2_ready[s], 1)
                    if tail in ("norm_ln", "relu_ln", "gat"):
                        for s in range(2):
                            dve.wait_ge(t2_ready[s], t2_ready.at(r, u + 1))
                        layer_norm(st, u, r, h_out, None)
                    if tail == "tr":
                        for s in range(2):
                            p = width(u, s)
                            g = 2 * u + s
                            dve.wait_ge(hot_ready[s], hot_ready.at(r, u + 1))
                            place = bn_stat[:, g, :] if isinstance(u, int) else bn_stat[:, bass.ds(g, 1), :].rearrange("p o c -> p (o c)")
                            dve.bn_stats(place, ht_bank[s][:].rearrange("p (j n) -> p j n", j=RPP)[:, :, 0:p]).then_inc(bn_ready[s], 1)
                    st.end()

                schedule(dve, r, {SAGE: sage_pair, GAT: gat_pair, TR: tr_pair}[kind], lambda i: None, unit)
                esteps += eper * PAIRS
                usteps += uper * (UNITS + 1)

            for s in range(2):
                dve.wait_ge(bn_ready[s], bn_ready.at(R_TR, UNITS + 1))
            done(dve.bn_aggr(bn_work[:, 0:2], bn_stat[:].rearrange("p g c -> p (g c)")))
            done(dve.tensor_scalar(bn_work[:, 2:3], bn_work[:, 1:2], 1e-5, None, ALU.add))
            dve.sem_inc(bn_var, 1)
            dve.wait_ge(prep_act, 10)
            done(dve.reciprocal(bn_work[:, 6:7], bn_work[:, 3:4]))
            done(dve.tensor_tensor(bn_work[:, 4:5], cols[:, C_GAMMA:C_GAMMA + 1], bn_work[:, 6:7], ALU.mult))
            done(dve.tensor_tensor(bn_work[:, 7:8], bn_work[:, 0:1], bn_work[:, 4:5], ALU.mult))
            done(dve.tensor_tensor(bn_work[:, 5:6], cols[:, C_BETA:C_BETA + 1], bn_work[:, 7:8], ALU.subtract))
            dve.sem_inc(bn_coef, 1)
            dve.wait_ge(prep_pe, 9)
            done(dve.tensor_copy(bn_a[:], o_bank[0][:, 0:P]))
            done(dve.tensor_copy(bn_b[:], o_bank[1][:, 0:P]))

            r = R_OUT
            oper = 2 * (2 + 3)

            def out_unit(u):
                st = Steps(dve, unit_steps, usteps, oper, u)
                for s in range(2):
                    p = width(u, s)
                    dve.wait_ge(h_loaded[s], h_loaded.at(r, u + 1))
                    dve.wait_ge(agg_loaded[s], agg_loaded.at(r, u + 1))
                    dve.wait_ge(out_ready[s], out_ready.at(r, u))
                    st.done(dve.tensor_tensor(t1[s][0:p], agg_in[s][0:p], bc_rows(bn_a, p), ALU.mult))
                    st.done(dve.tensor_tensor(t1[s][0:p], t1[s][0:p], bc_rows(bn_b, p), ALU.add))
                    dve.tensor_tensor(t2[s][0:p], t1[s][0:p], h_in[s][0:p], ALU.add).then_inc(t2_ready[s], 1)
                for s in range(2):
                    dve.wait_ge(t2_ready[s], t2_ready.at(r, u + 1))
                layer_norm(st, u, r, h_out, None)
                st.end()

            with dve.Fori(0, UNITS) as u:
                out_unit(u)
            out_unit(UNITS)


_INS = ["x", "src", "dst", "edge_attr_10", "edge_weight", "L0_gnn_W1_l", "L0_gnn_b1_l", "L0_gnn_W1_r", "L0_gnn_W2_l",
        "L0_gnn_b2_l", "L0_gnn_W2_r", "L1_gnn_Wl", "L1_gnn_Wr", "L1_gnn_b", "L2_gnn_W0", "L2_gnn_b0", "L2_gnn_W1",
        "L2_gnn_b1", "L2_gnn_att", "L2_gnn_scale", "L2_gnn_offset", "L3_gnn_Wq", "L3_gnn_bq", "L3_gnn_Wk", "L3_gnn_bk",
        "L3_gnn_Wv", "L3_gnn_bv", "L3_gnn_We", "L3_gnn_Wskip", "L3_gnn_bskip", "L3_gnn_gamma", "L3_gnn_beta"]


def kernel(**inputs):
    import numpy as _np
    import concourse.bacc as _bacc
    from concourse.bass_utils import run_bass_kernel_spmd as _run

    nc = _bacc.Bacc("TRN2", target_bir_lowering=False, num_devices=1)
    arrays, io = {}, {}
    for name in _INS:
        a = _np.ascontiguousarray(inputs[name])
        arrays[f"in_{name}_dram"] = a
        io[name] = nc.dram_tensor(f"in_{name}_dram", a.shape, mybir.dt.from_np(a.dtype), kind="ExternalInput").ap()
    out = nc.dram_tensor("out_0_dram", inputs["x"].shape, F32, kind="ExternalOutput").ap()
    gnn_kernel(nc, io, out)
    r = _run(nc, [arrays], core_ids=[0])
    return r.results[0]["out_0_dram"]
```

```python
from contextlib import ExitStack

import concourse.bass as bass
from concourse import mybir

F32 = mybir.dt.float32
I32 = mybir.dt.int32
U8 = mybir.dt.uint8
BF16 = mybir.dt.bfloat16
ALU = mybir.AluOpType
ACT = mybir.ActivationFunctionType
AX_X = mybir.AxisListType.X

P = 128
RPP = 4
GROUP = P * RPP
UNIT = 2 * GROUP
CPB = 4
BLOCK = P * CPB
BIG = 1e30
LN_EPS = 1e-5
LOW_BITS = 9
DIGITS = 1 << LOW_BITS
REC = 4


class Stage:

    def __init__(self, sems, rounds, per_round, step=1):
        self.sems, self.rounds, self.per_round, self.step = sems, rounds, per_round, step

    def __getitem__(self, slot):
        return self.sems[slot]

    def at(self, r, n):
        before = len([x for x in self.rounds if x < r]) * self.per_round
        return (n + before) * self.step


def gnn_kernel(nc, io, out):
    N = io["x"].shape[0]
    E = io["src"].shape[0]
    D = io["x"].shape[1]
    EDIM = io["edge_attr_10"].shape[1]
    HEADS, HDIM = io["L2_gnn_att"].shape
    assert D == P and HEADS * HDIM == D
    UNITS = N // UNIT
    TAILP = (N - UNITS * UNIT - GROUP) // RPP
    assert UNITS * UNIT + GROUP + TAILP * RPP == N and 0 < TAILP <= P
    BLOCKS = -(-E // BLOCK)
    BLOCKS += BLOCKS % 2
    PAIRS = BLOCKS // 2
    EPAD = BLOCKS * BLOCK
    FULLB = E // BLOCK
    RESTE = E - FULLB * BLOCK
    assert FULLB == BLOCKS - 1 and 1 < RESTE < BLOCK
    NOWHERE = 1 << 17
    assert N <= NOWHERE and NOWHERE >> LOW_BITS < DIGITS
    SHIFT = UNIT.bit_length() - 1

    SAGE, GAT, TR = "sage", "gat", "tr"
    dram = {n: nc.dram_tensor(n, [N, D], F32).ap() for n in ("node_a", "node_b", "node_x", "agg0", "agg1")}
    x_in, node_a, node_b, node_x = io["x"], dram["node_a"], dram["node_b"], dram["node_x"]
    agg = [dram["agg0"], dram["agg1"]]
    w1 = [io["L1_gnn_Wl"][k] for k in range(4)]
    v1 = [io["L1_gnn_Wr"][k] for k in range(4)]
    c1 = [io["L1_gnn_b"][k:k + 1, :] for k in range(4)]

    def row(v):
        return v.unsqueeze(0)

    ROUNDS = [
        (SAGE, "norm", x_in, None, node_a, io["L0_gnn_W1_l"], io["L0_gnn_W1_r"], row(io["L0_gnn_b1_l"])),
        (SAGE, "norm_ln", node_a, x_in, node_x, io["L0_gnn_W2_l"], io["L0_gnn_W2_r"], row(io["L0_gnn_b2_l"])),
        (SAGE, "relu", node_x, None, node_a, w1[0], v1[0], c1[0]),
        (SAGE, "relu", node_a, None, node_b, w1[1], v1[1], c1[1]),
        (SAGE, "relu", node_b, None, node_a, w1[2], v1[2], c1[2]),
        (SAGE, "relu_ln", node_a, node_x, node_b, w1[3], v1[3], c1[3]),
        (GAT, "gat", node_b, node_b, node_x, None, io["L2_gnn_W1"], row(io["L2_gnn_b1"])),
        (TR, "tr", node_x, None, node_a, None, io["L3_gnn_Wskip"], row(io["L3_gnn_bskip"])),
    ]
    NR = len(ROUNDS)
    R_GAT, R_TR, R_OUT = 6, 7, 8
    sage_rounds = [r for r in range(NR) if ROUNDS[r][0] == SAGE]
    soft_rounds = [R_GAT, R_TR]
    all_edges = list(range(NR))
    all_dense = list(range(NR))
    all_store = list(range(NR + 1))
    tails = {k: [r for r in range(NR) if ROUNDS[r][1] == k] for k in ("norm", "norm_ln", "relu", "relu_ln", "gat", "tr")}
    norm_rounds = tails["norm"] + tails["norm_ln"]
    t1_rounds = tails["norm_ln"] + tails["gat"]
    ln_rounds = sorted(tails["norm_ln"] + tails["relu_ln"] + tails["gat"] + [R_OUT])
    res_rounds = sorted(tails["norm_ln"] + tails["relu_ln"] + tails["gat"])

    with ExitStack() as ctx:
        def sb(name, shape, dt=F32):
            return ctx.enter_context(nc.sbuf_tensor(name, shape, dt))

        def sb2(name, shape, dt=F32):
            return [sb(f"{name}{k}", shape, dt) for k in range(2)]

        def sem(name):
            return ctx.enter_context(nc.semaphore(name))

        def edge_stage(name, rounds, step=1):
            return Stage([sem(f"{name}{k}") for k in range(2)], rounds, PAIRS, step)

        def unit_stage(name, rounds, step=1):
            return Stage([sem(f"{name}{k}") for k in range(2)], rounds, UNITS + 1, step)

        keep_dram = [nc.dram_tensor(f"keep_dram{t}", [EPAD], U8).ap() for t in range(2)]
        weight_dram = nc.dram_tensor("weight_dram", [EPAD], F32).ap()
        rec_dram = [nc.dram_tensor(f"rec_dram{t}", [EPAD, REC], F32).ap() for t in range(2)]
        attr_dram = nc.dram_tensor("attr_dram", [EPAD, EDIM], F32).ap()

        ident = sb("ident", [P, P])
        ones_row = sb("ones_row", [1, P])
        score_ones = sb("score_ones", [P, P])
        head_mask = sb("head_mask", [P, P])
        head_pick = sb("head_pick", [P, HEADS])
        keep = sb("keep", [P, EPAD], U8)
        idx = [sb(f"idx{t}", [P, BLOCKS + 2, 3 * CPB], I32) for t in range(2)]
        inv = sb("inv", [P, BLOCKS, CPB])
        unit_end = [sb(f"unit_end{t}", [1, PAIRS + 1], I32) for t in range(2)]
        zeros = sb("zeros", [P, 16 * P])
        w_l = {r: sb(f"w_l{r}", [P, P]) for r in sage_rounds}
        w_r = {r: sb(f"w_r{r}", [P, P]) for r in range(NR)}
        b_row = {r: sb(f"b_row{r}", [1, P]) for r in range(NR)}
        natural = {n: sb(f"nat_{n}", [P, P]) for n in ("W0", "W1", "Wq", "Wk", "Wv", "Wskip")}
        we_nat = sb("we_nat", [P, EDIM])
        w0_t, wq_t, wk_t, wv_t = sb("w0_t", [P, P]), sb("wq_t", [P, P]), sb("wk_t", [P, P]), sb("wv_t", [P, P])
        we_t = sb("we_t", [EDIM, P])
        att_rep = sb("att_rep", [P, P])
        w_att = sb("w_att", [P, P])
        cols = sb("cols", [P, 8])
        C_ATT, C_B0, C_BQ, C_BK, C_BV, C_GAMMA, C_BETA, C_BATT = range(8)
        scale_bc, offset_bc = sb("scale_bc", [P, P]), sb("offset_bc", [P, P])
        bn_stat = sb("bn_stat", [P, 2 * (UNITS + 1), 6])
        bn_work = sb("bn_work", [P, 8])
        bn_a, bn_b = sb("bn_a", [P, P]), sb("bn_b", [P, P])
        arena_at = [0]

        def in_arena(parts, shape, dt=F32):
            count = 1
            for size in shape:
                count *= size
            nbytes = count * mybir.dt.size(dt)
            at = arena_at[0]
            arena_at[0] += -(-nbytes // 32) * 32
            assert arena_at[0] <= EPAD
            t = keep[0:parts, at:at + nbytes].bitcast(dt)
            if len(shape) == 2:
                t = t.rearrange("p (a b) -> p a b", a=shape[0])
            if len(shape) == 3:
                t = t.rearrange("p (a b c) -> p a b c", a=shape[0], b=shape[1])
            return t

        def block_table(dt=F32):
            return in_arena(BLOCKS, [BLOCK], dt)

        src_i, digit_i, keep_u = block_table(I32), block_table(I32), block_table(U8)
        key_f, other_f, wt_f, keep_f, scat_f, keyc_f, otherc_f = (block_table() for _ in range(7))
        inv_f = digit_f = block_table()
        arena_rec = arena_at[0]
        dst_i, place_i, pos_f, start_f = block_table(I32), block_table(I32), block_table(), block_table()
        arena_at[0] = arena_rec
        rec_f = in_arena(BLOCKS, [BLOCK, REC])
        before_f, after_f = sb("before_f", [BLOCKS, 1]), sb("after_f", [BLOCKS, 1])
        carry_col, carry_row = sb("carry_col", [BLOCKS, 1]), sb("carry_row", [1, BLOCKS + 1])
        rec_t = in_arena(P, [BLOCKS, CPB, REC])
        digit_t = in_arena(P, [BLOCKS, CPB])
        iota_i, iota_f = in_arena(P, [DIGITS], I32), in_arena(P, [DIGITS])
        onehot = [in_arena(P, [DIGITS], BF16) for k in range(CPB)]
        picked = in_arena(P, [DIGITS])
        before_ones, rest_ones = sb("before_ones", [P, P], BF16), sb("rest_ones", [P, P], BF16)
        all_ones, no_ones = sb("all_ones", [P, P], BF16), sb("no_ones", [P, P], BF16)
        place_f = sb("place_f", [P, CPB])
        place_idx, rec_rows = sb2("place_idx", [P, CPB], I32), sb2("rec_rows", [P, CPB, REC])
        g_idx = sb2("g_idx", [P, 2 * CPB], I32)
        s_idx = sb2("s_idx", [P, CPB], I32)
        gath = sb2("gath", [P, CPB, P])
        gath_d = sb2("gath_d", [P, CPB, P])
        run = sb2("run", [P, BLOCK])
        y_rows = sb2("y_rows", [P, CPB, P])
        seg_max, den, num = sb2("seg_max", [P, BLOCK]), sb2("den", [P, BLOCK]), run
        gsrc_t = sb2("gsrc_t", [P, BLOCK])
        attr = sb2("attr", [P, CPB, EDIM])
        attr_t = sb2("attr_t", [EDIM, BLOCK])
        wt_bc = sb2("wt_bc", [P, BLOCK])
        start_neg = sb2("start_neg", [P, BLOCK + 1])
        logit_raw = sb2("logit_raw", [P, BLOCK])
        logit = sb2("logit", [P, BLOCK])
        gdst_t = prod = logit
        full_max = sb2("full_max", [P, BLOCK])
        msg = full_max
        expd = sb2("expd", [P, BLOCK])
        carry = sb2("carry", [P, 4])
        den_inv = sb2("den_inv", [P, 2, CPB * HEADS])
        h_in, agg_in, res_in = sb2("h_in", [P, RPP, P]), sb2("agg_in", [P, RPP, P]), sb2("res_in", [P, RPP, P])
        h_t = sb2("h_t", [P, RPP, P])
        total, t2 = sb2("total", [P, RPP, P]), sb2("t2", [P, RPP, P])
        t1, sq = ([zeros[:, (2 * n + k) * GROUP:(2 * n + k + 1) * GROUP].rearrange("p (j f) -> p j f", j=RPP)
                   for k in range(2)] for n in range(2))
        h_out = sb2("h_out", [P, RPP, P])
        small = sb2("small", [P, 6, RPP])
        small2 = sb2("small2", [P, 2, RPP])
        st6, mv = sb2("st6", [P, RPP, 6]), sb2("mv", [P, RPP, 2])
        pe_bank = [ctx.enter_context(nc.psum_tensor(f"edge_bank{k}", [P, BLOCK], F32)) for k in range(4)]
        ht_bank = [ctx.enter_context(nc.psum_tensor(f"ht_bank{k}", [P, GROUP], F32)) for k in range(2)]
        o_bank = [ctx.enter_context(nc.psum_tensor(f"o_bank{k}", [P, GROUP], F32)) for k in range(2)]

        filled, loaded, prep, prep_pe, prep_act, prep_pool = (sem(n) for n in ("filled", "loaded", "prep", "prep_pe", "prep_act", "prep_pool"))
        zeroed, keep_out, keep_in, padded, tables_done = (sem(n) for n in ("zeroed", "keep_out", "keep_in", "padded", "tables_done"))
        key_ready = sem("key_ready")
        ends_in = sem("ends_in")
        keep_ready = sem("keep_ready")
        att_ready = sem("att_ready")
        last_start, first_start = sem("last_start"), sem("first_start")
        last_start_t, first_start_t = sem("last_start_t"), sem("first_start_t")
        tab_ready, tab_t = sem("tab_ready"), sem("tab_t")
        tab_used = sem("tab_used")
        sort_ready, sort_t, sort_used = sem("sort_ready"), sem("sort_t"), sem("sort_used")
        hot = sem("hot")
        counted = [sem(f"counted{k}") for k in range(CPB)]
        ranked, placed = sem("ranked"), sem("placed")
        slot_ready = [sem(f"slot_ready{q}") for q in range(2)]
        rec_out = [sem(f"rec_out{q}") for q in range(2)]
        rec_in = sem("rec_in")
        bn_var, bn_coef = sem("bn_var"), sem("bn_coef")
        pool_turn, sp_turn, dve_turn = sem("pool_turn"), sem("sp_turn"), sem("dve_turn")
        gidx_ready = Stage([sem(f"gidx_ready{q}") for q in range(2)], all_edges, PAIRS + 1)
        sidx_ready = edge_stage("sidx_ready", all_edges)
        gathered = edge_stage("gathered", all_edges, 16 * CPB)
        gathered_d = edge_stage("gathered_d", [R_TR], 16 * CPB)
        scattered = edge_stage("scattered", all_edges, 16 * CPB)
        gt_ready = edge_stage("gt_ready", all_edges)
        run_ready = edge_stage("run_ready", sage_rounds)
        yp_ready = edge_stage("yp_ready", all_edges)
        y_ready = edge_stage("y_ready", all_edges)
        gts_ready = edge_stage("gts_ready", soft_rounds)
        lin_ready = edge_stage("lin_ready", soft_rounds)
        raw_ready = edge_stage("raw_ready", soft_rounds)
        neg_ready = edge_stage("neg_ready", soft_rounds)
        prod_ready = edge_stage("prod_ready", [R_TR])
        score_ready = edge_stage("score_ready", [R_TR])
        at_ready = edge_stage("at_ready", [R_TR])
        ats_ready = edge_stage("ats_ready", [R_TR])
        val_ready = edge_stage("val_ready", [R_TR])
        shift_ready = edge_stage("shift_ready", soft_rounds)
        exp_ready = edge_stage("exp_ready", soft_rounds)
        sums_ready = edge_stage("sums_ready", soft_rounds)
        extra_in = edge_stage("extra_in", soft_rounds, 16)
        h_loaded = unit_stage("h_loaded", all_store, 16)
        agg_loaded = unit_stage("agg_loaded", all_store, 16)
        res_loaded = unit_stage("res_loaded", res_rounds, 16)
        htp_ready = unit_stage("htp_ready", all_dense)
        ht_ready = unit_stage("ht_ready", all_dense)
        mm_ready = unit_stage("mm_ready", all_dense)
        sum_ready = unit_stage("sum_ready", all_dense)
        sq_ready = unit_stage("sq_ready", norm_rounds)
        ss_ready = unit_stage("ss_ready", norm_rounds)
        nrm_ready = unit_stage("nrm_ready", norm_rounds)
        t1_ready = unit_stage("t1_ready", t1_rounds)
        t2_ready = unit_stage("t2_ready", ln_rounds)
        var_ready = unit_stage("var_ready", ln_rounds)
        sd_ready = unit_stage("sd_ready", ln_rounds)
        gvar_ready = unit_stage("gvar_ready", tails["gat"])
        gsd_ready = unit_stage("gsd_ready", tails["gat"])
        grs_ready = unit_stage("grs_ready", tails["gat"])
        gln_ready = unit_stage("gln_ready", tails["gat"])
        rs_ready = unit_stage("rs_ready", tails["gat"])
        out_ready = unit_stage("out_ready", all_store)
        stored = unit_stage("stored", all_store, 16)
        hot_ready = unit_stage("hot_ready", [R_TR])
        bn_ready = unit_stage("bn_ready", [R_TR])
        edge_steps = sem("edge_steps")
        unit_steps = sem("unit_steps")

        class Steps:

            def __init__(self, dve, semaphore, base, per, iteration):
                self.dve, self.sem, self.value, self.n, self.per = dve, semaphore, base + iteration * per, 0, per

            def mark(self, instruction):
                instruction.then_inc(self.sem, 1)
                self.n += 1

            def wait(self):
                self.dve.wait_ge(self.sem, self.value + self.n)

            def done(self, instruction):
                self.mark(instruction)
                self.wait()

            def end(self):
                assert self.n == self.per

        def unit_rows(t):
            return t[0:UNITS * UNIT].rearrange("(u h p j) f -> u h p (j f)", h=2, p=P, j=RPP)

        def group_dram(t, u, s):
            if isinstance(u, int):
                first = u * UNIT + s * GROUP
                p = width(u, s)
                return t[first:first + p * RPP].rearrange("(p j) f -> p (j f)", j=RPP)
            return unit_rows(t)[bass.ds(u, 1), s].rearrange("o p f -> (o p) f")

        def width(u, s):
            return TAILP if isinstance(u, int) and u == UNITS and s == 1 else P

        def flat(t, p=P):
            return t[0:p].rearrange("p j f -> p (j f)")

        def bc_rows(t, p):
            return t[0:p].unsqueeze(1).to_broadcast([p, RPP, P])

        def order(r):
            return 1 if ROUNDS[r][0] == GAT else 0

        def schedule(eng, r, edge_pair, before_units, unit):
            end = unit_end[order(r)]
            with eng.Fori(0, PAIRS) as i:
                edge_pair(i)
                before_units(i)
                lo = eng.value_load(end[0:1, bass.ds(i, 1)], min_val=0, max_val=UNITS - 3)
                hi = eng.value_load(end[0:1, bass.ds(i + 1, 1)], min_val=0, max_val=UNITS - 3)
                with eng.If(lo < hi):
                    with eng.Fori(lo, hi) as u:
                        unit(u)
            before_units(PAIRS)
            lo = eng.value_load(end[0:1, PAIRS:PAIRS + 1], min_val=0, max_val=UNITS - 3)
            with eng.Fori(lo, UNITS - 2) as u:
                unit(u)
            for u in range(UNITS - 2, UNITS + 1):
                unit(u)

        PREP_W = [("W0", pe_bank[0], 0), ("W1", pe_bank[0], P), ("Wq", pe_bank[1], 0), ("Wk", pe_bank[1], P),
                  ("Wv", pe_bank[2], 0), ("Wskip", pe_bank[2], P)]
        big_zero = [(n * P * 16, P, 16) for n in range(N // (P * 16))]
        at_zero = len(big_zero) * P * 16
        while at_zero < N:
            big_zero.append((at_zero, min(P, (N - at_zero) // RPP), RPP))
            at_zero += big_zero[-1][1] * RPP
        ZERO_DMAS = 2 * len(big_zero)

        ctx.enter_context(nc.allow_non_contiguous_dma(reason="vectors as columns and every 1024th destination, once"))
        block = ctx.enter_context(nc.Block())

        FILLS = 10
        LOADS = []
        keep_loads = [r for r in range(NR) if r == 0 or order(r) != order(r - 1)]

        @block.sync
        def _(sp):
            sp.wait_ge(filled, FILLS)
            dst, src = io["dst"], io["src"]

            def load(to, of):
                sp.dma_start(to, of).then_inc(loaded, 16)
                LOADS.append(1)

            load(dst_i[0:FULLB], dst[0:FULLB * BLOCK].rearrange("(p j) -> p j", j=BLOCK))
            load(dst_i[FULLB:FULLB + 1, 0:RESTE], row(dst[FULLB * BLOCK:E]))
            load(src_i[0:FULLB], src[0:FULLB * BLOCK].rearrange("(p j) -> p j", j=BLOCK))
            load(src_i[FULLB:FULLB + 1, 0:RESTE], row(src[FULLB * BLOCK:E]))
            load(wt_f[0:FULLB], io["edge_weight"][0:FULLB * BLOCK].rearrange("(p j) -> p j", j=BLOCK))
            load(wt_f[FULLB:FULLB + 1, 0:RESTE], row(io["edge_weight"][FULLB * BLOCK:E]))
            for r in range(NR):
                _, _, _, _, _, wl, wr, b = ROUNDS[r]
                if wl is not None:
                    load(w_l[r][:], wl)
                    load(w_r[r][:], wr)
                load(b_row[r][:], b)
            for n, t in (("W0", "L2_gnn_W0"), ("W1", "L2_gnn_W1"), ("Wq", "L3_gnn_Wq"), ("Wk", "L3_gnn_Wk"),
                         ("Wv", "L3_gnn_Wv"), ("Wskip", "L3_gnn_Wskip")):
                load(natural[n][:], io[t])
            load(we_nat[:], io["L3_gnn_We"])
            load(cols[:, C_ATT:C_ATT + 1], io["L2_gnn_att"].rearrange("h d -> (h d)").unsqueeze(1))
            for c, t in ((C_B0, "L2_gnn_b0"), (C_BQ, "L3_gnn_bq"), (C_BK, "L3_gnn_bk"), (C_BV, "L3_gnn_bv"),
                         (C_GAMMA, "L3_gnn_gamma"), (C_BETA, "L3_gnn_beta")):
                load(cols[:, c:c + 1], io[t].unsqueeze(1))
            load(scale_bc[:], row(io["L2_gnn_scale"]).to_broadcast([P, P]))
            load(offset_bc[:], row(io["L2_gnn_offset"]).to_broadcast([P, P]))
            sp.dma_start(attr_dram[0:E].rearrange("(a b) f -> a (b f)", a=16),
                         io["edge_attr_10"].rearrange("(a b) f -> a (b f)", a=16)).then_inc(padded, 16)
            sp.dma_start(row(attr_dram[E:EPAD].rearrange("a f -> (a f)")),
                         zeros[0:1, 0:(EPAD - E) * EDIM]).then_inc(padded, 16)
            for t in range(2):
                if t == 1:
                    for n in range(2):
                        for q in range(2):
                            sp.wait_ge(rec_out[q], (n + 1) * PAIRS * CPB * 16)
                        if n == 1:
                            sp.wait_ge(sort_ready, 2)
                        sp.dma_start(rec_f[:].rearrange("p j c -> p (j c)"),
                                     rec_dram[n].rearrange("(p j) c -> p (j c)", j=BLOCK)).then_inc(rec_in, 16)
                sp.wait_ge(key_ready, t + 1)
                sp.dma_start(before_f[1:BLOCKS], key_f[0:BLOCKS - 1, BLOCK - 1:BLOCK]).then_inc(ends_in, 16)
                sp.dma_start(after_f[0:BLOCKS - 1], key_f[1:BLOCKS, 0:1]).then_inc(ends_in, 16)
                sp.wait_ge(keep_ready, t + 1)
                sp.dma_start(keep_dram[t].rearrange("(p j) -> p j", j=BLOCK), keep_u[:]).then_inc(keep_out, 16)
            sp.dma_start(weight_dram.rearrange("(p j) -> p j", j=BLOCK), wt_f[:]).then_inc(padded, 16)
            sp.wait_ge(keep_out, 32)
            sp.wait_ge(padded, 48)
            sp.wait_ge(tables_done, 1)

            weight_v = weight_dram.rearrange("(i q e) -> i q e", q=2, e=BLOCK)
            attr_v = attr_dram.rearrange("(i q k p) f -> i q p k f", q=2, k=CPB, p=P)
            for r in range(NR):
                kind, tail, h_of, res_of, _, _, _, _ = ROUNDS[r]
                if r > 0:
                    for s in range(2):
                        sp.wait_ge(stored[s], stored.at(r, 0))
                        sp.sem_inc(sp_turn, 1)
                if r in keep_loads:
                    sp.dma_start(keep[:], row(keep_dram[order(r)]).to_broadcast([P, EPAD])).then_inc(keep_in, 16)

                def edge_pair(i, r=r, kind=kind):
                    if kind == GAT:
                        for q in range(2):
                            sp.wait_ge(sums_ready[q], sums_ready.at(r, i))
                            sp.sem_inc(sp_turn, 1)
                            sp.dma_start(wt_bc[q][:], weight_v[bass.ds(i, 1), q].to_broadcast([P, BLOCK])).then_inc(extra_in[q], 16)
                    if kind == TR:
                        for q in range(2):
                            sp.wait_ge(sums_ready[q], sums_ready.at(r, i))
                            sp.sem_inc(sp_turn, 1)
                            sp.dma_start(attr[q][:], attr_v[bass.ds(i, 1), q].rearrange("o p k f -> (o p) k f")).then_inc(extra_in[q], 16)

                def before_units(i, r=r):
                    for q in range(2):
                        sp.wait_ge(scattered[q], scattered.at(r, i))
                    sp.sem_inc(sp_turn, 1)

                def load_h(u, r=r, h_of=h_of):
                    for s in range(2):
                        sp.wait_ge(htp_ready[s], htp_ready.at(r, u))
                        sp.sem_inc(sp_turn, 1)
                        sp.dma_start(flat(h_in[s], width(u, s)), group_dram(h_of, u, s)).then_inc(h_loaded[s], 16)

                def unit(u, r=r, res_of=res_of):
                    for s in range(2):
                        sp.wait_ge(sum_ready[s], sum_ready.at(r, u))
                        sp.sem_inc(sp_turn, 1)
                        sp.dma_start(flat(agg_in[s], width(u, s)), group_dram(agg[order(r)], u, s)).then_inc(agg_loaded[s], 16)
                    if res_of is not None:
                        for s in range(2):
                            sp.wait_ge(t2_ready[s], t2_ready.at(r, u))
                            sp.sem_inc(sp_turn, 1)
                            sp.dma_start(flat(res_in[s], width(u, s)), group_dram(res_of, u, s)).then_inc(res_loaded[s], 16)
                    if not isinstance(u, int) or u + 2 <= UNITS:
                        load_h(u + 2)

                load_h(0)
                load_h(1)
                schedule(sp, r, edge_pair, before_units, unit)

            r = R_OUT
            for s in range(2):
                sp.wait_ge(stored[s], stored.at(r, 0))
                sp.sem_inc(sp_turn, 1)

            def out_unit(u):
                for s in range(2):
                    p = width(u, s)
                    sp.wait_ge(t2_ready[s], t2_ready.at(r, u))
                    sp.sem_inc(sp_turn, 1)
                    sp.dma_start(flat(h_in[s], p), group_dram(node_x, u, s)).then_inc(h_loaded[s], 16)
                    sp.sem_inc(sp_turn, 1)
                    sp.dma_start(flat(agg_in[s], p), group_dram(node_a, u, s)).then_inc(agg_loaded[s], 16)

            with sp.Fori(0, UNITS) as u:
                out_unit(u)
            out_unit(UNITS)

        @block.gpsimd
        def _(pool):
            pool.memset(ident[:], 0.0).then_inc(prep_pool, 1)
            pool.memset(before_ones[:], 0.0).then_inc(prep_pool, 1)
            pool.memset(rest_ones[:], 1.0).then_inc(prep_pool, 1)
            pool.iota(place_i[:], pattern=[[1, BLOCK]], base=0, channel_multiplier=BLOCK).then_inc(prep_pool, 1)
            pool.iota(iota_i[:], pattern=[[1, DIGITS]], base=0, channel_multiplier=0).then_inc(prep_pool, 1)
            pool.wait_ge(prep_pool, 5)
            pool.affine_select(out=ident[:], in_=ident[:], compare_op=ALU.not_equal, fill=1.0, base=0,
                               pattern=[[-1, P]], channel_multiplier=1).then_inc(prep_pool, 1)
            pool.affine_select(out=before_ones[:], in_=before_ones[:], compare_op=ALU.is_ge, fill=1.0, base=0,
                               pattern=[[-1, P]], channel_multiplier=1).then_inc(prep_pool, 1)
            pool.affine_select(out=rest_ones[:], in_=rest_ones[:], compare_op=ALU.is_ge, fill=0.0, base=0,
                               pattern=[[-1, P]], channel_multiplier=1).then_inc(prep_pool, 1)
            for n in range(2):
                with pool.Fori(0, PAIRS) as i:
                    for q in range(2):
                        pool.wait_ge(slot_ready[q], n * PAIRS + i + 1)
                        pool.sem_inc(pool_turn, 1)
                        for k in range(CPB):
                            pool.indirect_dma_start(rec_dram[n], bass.IndirectOffsetOnAxis(place_idx[q][:, k:k + 1], 0),
                                                    rec_rows[q][:, k, :], None).then_inc(rec_out[q], 16)
            pool.wait_ge(tables_done, 1)
            pool.wait_ge(zeroed, ZERO_DMAS * 16)
            for r in range(NR):
                kind, _, h_of, _, _, _, _, _ = ROUNDS[r]
                if r > 0:
                    for s in range(2):
                        pool.wait_ge(stored[s], stored.at(r, 0))

                def gathers(q, r=r, kind=kind, h_of=h_of):
                    for k in range(CPB):
                        pool.indirect_dma_start(gath[q][:, k, :], None, h_of,
                                                bass.IndirectOffsetOnAxis(g_idx[q][:, k:k + 1], 0)).then_inc(gathered[q], 16)
                    if kind == TR:
                        for k in range(CPB):
                            pool.indirect_dma_start(gath_d[q][:, k, :], None, h_of,
                                                    bass.IndirectOffsetOnAxis(g_idx[q][:, CPB + k:CPB + k + 1], 0)).then_inc(gathered_d[q], 16)

                def scatters(q, r=r):
                    for k in range(CPB):
                        pool.indirect_dma_start(agg[order(r)], bass.IndirectOffsetOnAxis(s_idx[q][:, k:k + 1], 0), y_rows[q][:, k, :],
                                                None, bounds_check=N - 1, oob_is_err=False).then_inc(scattered[q], 16)

                for q in range(2):
                    pool.wait_ge(gidx_ready[q], gidx_ready.at(r, 1))
                    gathers(q)
                with pool.Fori(0, PAIRS - 1) as i:
                    for q in range(2):
                        pool.wait_ge(gt_ready[q], gt_ready.at(r, i + 1))
                        pool.wait_ge(gidx_ready[q], gidx_ready.at(r, i + 2))
                        pool.sem_inc(pool_turn, 1)
                        gathers(q)
                        pool.wait_ge(sidx_ready[q], sidx_ready.at(r, i + 1))
                        pool.wait_ge(y_ready[q], y_ready.at(r, i + 1))
                        pool.sem_inc(pool_turn, 1)
                        scatters(q)
                for q in range(2):
                    pool.wait_ge(sidx_ready[q], sidx_ready.at(r, PAIRS))
                    pool.wait_ge(y_ready[q], y_ready.at(r, PAIRS))
                    scatters(q)

        @block.tensor
        def _(pe):
            pe.wait_ge(prep_pool, 8)
            pe.wait_ge(loaded, 16 * len(LOADS))
            for name, bank, col in PREP_W:
                pe.transpose(bank[:, col:col + P], natural[name][:], ident[:]).then_inc(prep_pe, 1)
            pe.transpose(pe_bank[3][0:EDIM, 0:P], we_nat[:], ident[:]).then_inc(prep_pe, 1)
            pe.wait_ge(att_ready, 1)
            pe.matmul(o_bank[0][:, 0:P], natural["W0"][:], att_rep[:], start=True, stop=True)
            pe.matmul(o_bank[0][:, P:P + 1], att_rep[:], cols[:, C_B0:C_B0 + 1], start=True, stop=True,
                      skip_group_check=True).then_inc(prep_pe, 1)
            pe.wait_ge(prep_act, 9)

            def transposed(tables, semaphore):
                for t, bank in tables:
                    for k in range(CPB):
                        last = pe.transpose(bank[:, k * BLOCKS:(k + 1) * BLOCKS], t[:, k * P:(k + 1) * P],
                                            ident[0:BLOCKS, 0:BLOCKS])
                last.then_inc(semaphore, 1)

            pe.wait_ge(last_start, 1)
            pe.transpose(pe_bank[0][0:1, 0:BLOCKS], carry_col[:], ident[0:BLOCKS, 0:BLOCKS]).then_inc(last_start_t, 1)
            pe.wait_ge(first_start, 1)
            pe.transpose(pe_bank[1][0:BLOCKS, 0:1], carry_row[:, 0:BLOCKS], ident[0:1, 0:1]).then_inc(first_start_t, 1)
            for t in range(2):
                pe.wait_ge(tab_ready, t + 1)
                pe.transpose(pe_bank[1][0:1, 0:BLOCKS], key_f[:, 0:1], ident[0:BLOCKS, 0:BLOCKS])
                transposed([(otherc_f, ht_bank[0]), (keyc_f, ht_bank[1]), (scat_f, o_bank[1])]
                           + ([(inv_f, pe_bank[0])] if t == 0 else []), tab_t)
                if t == 1:
                    break
                for n in range(2):
                    pe.wait_ge(sort_ready, n + 1)
                    pe.wait_ge(tab_used, 1)
                    transposed([(rec_f[:, :, 0] if n else other_f, ht_bank[0]), (rec_f[:, :, 1] if n else key_f, ht_bank[1]),
                                (rec_f[:, :, 2] if n else wt_f, o_bank[1]), (digit_f, pe_bank[0])], sort_t)
                    pe.wait_ge(sort_used, n + 1)
                    rank = pe_bank[2]
                    loop = 2 * n * BLOCKS
                    for k in range(DIGITS // P):
                        pe.matmul(rank[:, k * P:(k + 1) * P], no_ones[:], no_ones[:], start=k == 0, stop=False,
                                  skip_group_check=True)
                    with pe.Fori(0, BLOCKS) as b:
                        for k in range(CPB):
                            pe.wait_ge(hot, (b + loop) * CPB + k + 1)
                            pe.matmul(rank[:], all_ones[:], onehot[k][:], start=False, stop=False,
                                      skip_group_check=True).then_inc(counted[k], 1)
                    loop += BLOCKS
                    with pe.Fori(0, BLOCKS) as b:
                        for k in range(CPB):
                            pe.wait_ge(hot, (b + loop) * CPB + k + 1)
                            pe.matmul(rank[:], before_ones[:], onehot[k][:], start=False, stop=False,
                                      skip_group_check=True).then_inc(ranked, 1)
                            pe.wait_ge(placed, (b + n * BLOCKS) * CPB + k + 1)
                            pe.matmul(rank[:], rest_ones[:], onehot[k][:], start=False, stop=False,
                                      skip_group_check=True).then_inc(counted[k], 1)
            pe.wait_ge(tables_done, 1)

            for r in range(NR):
                kind, tail = ROUNDS[r][0:2]

                def sage_pair(i, r=r):
                    for q in range(2):
                        pe.wait_ge(gathered[q], gathered.at(r, i + 1))
                        pe.wait_ge(run_ready[q], run_ready.at(r, i))
                        for k in range(CPB):
                            last = pe.transpose(pe_bank[q][:, k * P:(k + 1) * P], gath[q][:, k, :], ident[:])
                        last.then_inc(gt_ready[q], 1)
                    for q in range(2):
                        pe.wait_ge(run_ready[q], run_ready.at(r, i + 1))
                        pe.wait_ge(y_ready[q], y_ready.at(r, i))
                        for k in range(CPB):
                            last = pe.matmul(pe_bank[2 + q][:, k * P:(k + 1) * P], run[q][:, k * P:(k + 1) * P],
                                             w_l[r][:], start=True, stop=True, skip_group_check=True)
                        last.then_inc(yp_ready[q], 1)

                def rows_out(i, q, r):
                    pe.wait_ge(sums_ready[q], sums_ready.at(r, i + 1))
                    for k in range(CPB):
                        pe.transpose(pe_bank[q][:, k * P:(k + 1) * P], num[q][:, k * P:(k + 1) * P], ident[:])
                    for k in range(CPB):
                        last = pe.matmul(pe_bank[2 + q][:, k * HEADS:(k + 1) * HEADS], den[q][:, k * P:(k + 1) * P],
                                         head_pick[:], start=True, stop=True, skip_group_check=True)
                    last.then_inc(yp_ready[q], 1)

                def gat_pair(i, r=r):
                    for q in range(2):
                        pe.wait_ge(gathered[q], gathered.at(r, i + 1))
                        pe.wait_ge(y_ready[q], y_ready.at(r, i))
                        for k in range(CPB):
                            last = pe.transpose(pe_bank[q][:, k * P:(k + 1) * P], gath[q][:, k, :], ident[:])
                        last.then_inc(gt_ready[q], 1)
                    for q in range(2):
                        pe.wait_ge(gts_ready[q], gts_ready.at(r, i + 1))
                        pe.matmul(pe_bank[q][:], w_att[:], gsrc_t[q][:], start=True, stop=True)
                        pe.matmul(pe_bank[2 + q][:], w0_t[:], gsrc_t[q][:], start=True, stop=True).then_inc(lin_ready[q], 1)
                    for q in range(2):
                        rows_out(i, q, r)

                def tr_pair(i, r=r):
                    for q in range(2):
                        pe.wait_ge(gathered[q], gathered.at(r, i + 1))
                        pe.wait_ge(gathered_d[q], gathered_d.at(r, i + 1))
                        pe.wait_ge(y_ready[q], y_ready.at(r, i))
                        for k in range(CPB):
                            pe.transpose(pe_bank[q][:, k * P:(k + 1) * P], gath[q][:, k, :], ident[:])
                        for k in range(CPB):
                            last = pe.transpose(pe_bank[2 + q][:, k * P:(k + 1) * P], gath_d[q][:, k, :], ident[:])
                        last.then_inc(gt_ready[q], 1)
                    for q in range(2):
                        pe.wait_ge(extra_in[q], extra_in.at(r, i + 1))
                        pe.wait_ge(gts_ready[q], gts_ready.at(r, i + 1))
                        for k in range(CPB):
                            last = pe.transpose(pe_bank[q][0:EDIM, k * P:(k + 1) * P], attr[q][:, k, :], ident[:])
                        last.then_inc(at_ready[q], 1)
                    for q in range(2):
                        pe.matmul(pe_bank[2 + q][:], wq_t[:], gdst_t[q][:], start=True, stop=True)
                        pe.wait_ge(ats_ready[q], ats_ready.at(r, i + 1))
                        pe.matmul(pe_bank[q][:], wk_t[:], gsrc_t[q][:], start=True, stop=False)
                        pe.matmul(pe_bank[q][:], we_t[:], attr_t[q][:], start=False, stop=True).then_inc(lin_ready[q], 1)
                    for q in range(2):
                        pe.wait_ge(prod_ready[q], prod_ready.at(r, i + 1))
                        pe.matmul(pe_bank[q][:], score_ones[:], prod[q][:], start=True, stop=True).then_inc(score_ready[q], 1)
                        pe.matmul(pe_bank[2 + q][:], wv_t[:], gsrc_t[q][:], start=True, stop=False)
                        pe.matmul(pe_bank[2 + q][:], we_t[:], attr_t[q][:], start=False, stop=True).then_inc(val_ready[q], 1)
                    for q in range(2):
                        rows_out(i, q, r)

                def front(u, r=r, tail=tail):
                    for s in range(2):
                        p = width(u, s)
                        pe.wait_ge(h_loaded[s], h_loaded.at(r, u + 1))
                        pe.wait_ge(ht_ready[s], ht_ready.at(r, u))
                        if tail == "tr" and not (isinstance(u, int) and u == 0):
                            pe.wait_ge(bn_ready[s], bn_ready.at(r, u - 1))
                        for j in range(RPP):
                            last = pe.transpose(ht_bank[s][:, j * P:j * P + p], h_in[s][0:p, j, :], ident[0:p, 0:p])
                        last.then_inc(htp_ready[s], 1)
                    for s in range(2):
                        p = width(u, s)
                        pe.wait_ge(ht_ready[s], ht_ready.at(r, u + 1))
                        pe.wait_ge(sum_ready[s], sum_ready.at(r, u))
                        pe.matmul(o_bank[s][0:p, :], ones_row[:, 0:p], b_row[r][:].unsqueeze(1).to_broadcast([1, RPP, P]),
                                  start=True, stop=False, skip_group_check=True)
                        for j in range(RPP):
                            last = pe.matmul(o_bank[s][0:p, j * P:(j + 1) * P], h_t[s][:, j, 0:p], w_r[r][:],
                                             start=False, stop=j == RPP - 1, skip_group_check=True)
                        last.then_inc(mm_ready[s], 1)

                def unit(u, r=r, tail=tail):
                    if not isinstance(u, int) or u + 1 <= UNITS:
                        front(u + 1)
                    if tail == "tr":
                        for s in range(2):
                            p = width(u, s)
                            pe.wait_ge(out_ready[s], out_ready.at(r, u + 1))
                            if not isinstance(u, int) or u + 1 <= UNITS:
                                pe.wait_ge(ht_ready[s], ht_ready.at(r, u + 2))
                            for j in range(RPP):
                                last = pe.transpose(ht_bank[s][:, j * P:j * P + p], h_out[s][0:p, j, :], ident[0:p, 0:p])
                            last.then_inc(hot_ready[s], 1)

                front(0)
                schedule(pe, r, {SAGE: sage_pair, GAT: gat_pair, TR: tr_pair}[kind], lambda i: None, unit)

            pe.wait_ge(bn_coef, 1)
            for bank, c in ((o_bank[0], 4), (o_bank[1], 5)):
                last = pe.matmul(bank[:, 0:P], bn_work[:, c:c + 1].to_broadcast([P, P]), ident[:], start=True, stop=True)
            last.then_inc(prep_pe, 1)

        @block.scalar
        def _(act):
            act.wait_ge(filled, FILLS)
            for t, first, p, j in [(t, *z) for t in range(2) for z in big_zero]:
                act.dma_start(agg[t][first:first + p * j].rearrange("(p j) f -> p (j f)", j=j),
                              zeros[0:p, 0:j * P]).then_inc(zeroed, 16)
            for to, bank, col in ([(w0_t, pe_bank[0], 0), (w_r[R_GAT], pe_bank[0], P), (wq_t, pe_bank[1], 0),
                                                 (wk_t, pe_bank[1], P), (wv_t, pe_bank[2], 0), (w_r[R_TR], pe_bank[2], P)]):
                act.wait_ge(prep_pe, 7)
                act.activation(to[:], bank[:, col:col + P], ACT.Copy).then_inc(prep_act, 1)
            act.activation(we_t[:], pe_bank[3][0:EDIM, 0:P], ACT.Copy).then_inc(prep_act, 1)
            act.wait_ge(prep_pe, 8)
            act.activation(w_att[:], o_bank[0][:, 0:P], ACT.Copy).then_inc(prep_act, 1)
            act.activation(cols[:, C_BATT:C_BATT + 1], o_bank[0][:, P:P + 1], ACT.Copy).then_inc(prep_act, 1)
            act.wait_ge(tables_done, 1)

            for r in range(NR):
                kind, tail, _, _, h_to, _, _, _ = ROUNDS[r]
                act.wait_ge(keep_in, 16 * len([x for x in keep_loads if x <= r]))

                def sage_pair(i, r=r):
                    for q in range(2):
                        act.wait_ge(yp_ready[q], yp_ready.at(r, i + 1))
                        act.wait_ge(scattered[q], scattered.at(r, i))
                        for k in range(CPB):
                            last = act.activation(y_rows[q][:, k, :], pe_bank[2 + q][:, k * P:(k + 1) * P], ACT.Copy,
                                                  scale=inv[:, bass.ds(2 * i + q, 1), k])
                        last.then_inc(y_ready[q], 1)

                def start_marks(i, q, r):
                    act.wait_ge(shift_ready[q], shift_ready.at(r, i))
                    act.activation(start_neg[q][:, 0:BLOCK], keep[:, bass.ds((2 * i + q) * BLOCK, BLOCK)], ACT.Copy,
                                   scale=BIG, bias=-BIG).then_inc(neg_ready[q], 1)

                def exponentials(i, q, r):
                    act.wait_ge(shift_ready[q], shift_ready.at(r, i + 1))
                    act.activation(carry[q][:, 1:2], carry[q][:, 0:1], ACT.Exp)
                    act.activation(expd[q][:], expd[q][:], ACT.Exp).then_inc(exp_ready[q], 1)

                def gat_pair(i, r=r):
                    for q in range(2):
                        start_marks(i, q, r)
                    for q in range(2):
                        act.wait_ge(gt_ready[q], gt_ready.at(r, i + 1))
                        act.wait_ge(lin_ready[q], lin_ready.at(r, i))
                        act.activation(gsrc_t[q][:], pe_bank[q][:], ACT.Copy).then_inc(gts_ready[q], 1)
                    for q in range(2):
                        act.wait_ge(lin_ready[q], lin_ready.at(r, i + 1))
                        act.activation(logit_raw[q][:], pe_bank[q][:], ACT.Identity,
                                       bias=cols[:, C_BATT:C_BATT + 1]).then_inc(raw_ready[q], 1)
                    for q in range(2):
                        exponentials(i, q, r)

                def tr_pair(i, r=r):
                    for q in range(2):
                        start_marks(i, q, r)
                    for q in range(2):
                        act.wait_ge(gt_ready[q], gt_ready.at(r, i + 1))
                        act.wait_ge(val_ready[q], val_ready.at(r, i))
                        act.wait_ge(score_ready[q], score_ready.at(r, i))
                        act.activation(gsrc_t[q][:], pe_bank[q][:], ACT.Copy)
                        act.activation(gdst_t[q][:], pe_bank[2 + q][:], ACT.Copy).then_inc(gts_ready[q], 1)
                    for q in range(2):
                        act.wait_ge(at_ready[q], at_ready.at(r, i + 1))
                        act.activation(attr_t[q][:], pe_bank[q][0:EDIM, :], ACT.Copy).then_inc(ats_ready[q], 1)
                    for q in range(2):
                        act.wait_ge(lin_ready[q], lin_ready.at(r, i + 1))
                        act.activation(logit_raw[q][:], pe_bank[q][:], ACT.Identity,
                                       bias=cols[:, C_BK:C_BK + 1]).then_inc(raw_ready[q], 1)
                    for q in range(2):
                        exponentials(i, q, r)

                def store(u, s, r, h_to):
                    act.wait_ge(out_ready[s], out_ready.at(r, u + 1))
                    act.dma_start(group_dram(h_to, u, s), flat(h_out[s], width(u, s))).then_inc(stored[s], 16)

                def front(u, r=r):
                    for s in range(2):
                        p = width(u, s)
                        act.wait_ge(htp_ready[s], htp_ready.at(r, u + 1))
                        act.wait_ge(mm_ready[s], mm_ready.at(r, u))
                        act.activation(h_t[s][:, :, 0:p], ht_bank[s][:].rearrange("p (j n) -> p j n", j=RPP)[:, :, 0:p],
                                       ACT.Copy).then_inc(ht_ready[s], 1)

                def unit(u, r=r, tail=tail, h_to=h_to):
                    if not isinstance(u, int) or u + 1 <= UNITS:
                        front(u + 1)
                    if tail in ("norm", "norm_ln"):
                        for s in range(2):
                            p = width(u, s)
                            act.wait_ge(sum_ready[s], sum_ready.at(r, u + 1))
                            act.activation(sq[s][0:p], total[s][0:p], ACT.Square).then_inc(sq_ready[s], 1)
                            if tail == "norm_ln":
                                act.activation(t1[s][0:p], total[s][0:p], ACT.Relu).then_inc(t1_ready[s], 1)
                        for s in range(2):
                            p = width(u, s)
                            act.wait_ge(ss_ready[s], ss_ready.at(r, u + 1))
                            act.activation(small[s][0:p, 1, :], small[s][0:p, 0, :], ACT.Sqrt).then_inc(nrm_ready[s], 1)
                    if tail in ("relu", "tr"):
                        for s in range(2):
                            p = width(u, s)
                            act.wait_ge(sum_ready[s], sum_ready.at(r, u + 1))
                            act.wait_ge(stored[s], stored.at(r, u))
                            if tail == "tr":
                                act.wait_ge(hot_ready[s], hot_ready.at(r, u))
                            act.activation(h_out[s][0:p], total[s][0:p], ACT.Relu).then_inc(out_ready[s], 1)
                    if tail == "gat":
                        for s in range(2):
                            p = width(u, s)
                            act.wait_ge(sum_ready[s], sum_ready.at(r, u + 1))
                            act.activation(t1[s][0:p], total[s][0:p], ACT.Relu).then_inc(t1_ready[s], 1)
                        for s in range(2):
                            p = width(u, s)
                            act.wait_ge(gvar_ready[s], gvar_ready.at(r, u + 1))
                            act.activation(small[s][0:p, 1, :], small[s][0:p, 0, :], ACT.Sqrt).then_inc(gsd_ready[s], 1)
                        for s in range(2):
                            p = width(u, s)
                            act.wait_ge(grs_ready[s], grs_ready.at(r, u + 1))
                            for j in range(RPP):
                                last = act.activation(t2[s][0:p, j, :], t1[s][0:p, j, :], ACT.Identity,
                                                      scale=small[s][0:p, 2, j:j + 1], bias=small2[s][0:p, 0, j:j + 1])
                            last.then_inc(gln_ready[s], 1)
                    if tail in ("norm_ln", "relu_ln", "gat"):
                        for s in range(2):
                            roots(u, s, r)
                    if tail == "gat":
                        for s in range(2):
                            p = width(u, s)
                            act.wait_ge(rs_ready[s], rs_ready.at(r, u + 1))
                            act.wait_ge(stored[s], stored.at(r, u))
                            for j in range(RPP):
                                last = act.activation(h_out[s][0:p, j, :], t2[s][0:p, j, :], ACT.Identity,
                                                      scale=small[s][0:p, 5, j:j + 1], bias=small2[s][0:p, 1, j:j + 1])
                            last.then_inc(out_ready[s], 1)
                    for s in range(2):
                        store(u, s, r, h_to)

                def roots(u, s, r):
                    p = width(u, s)
                    act.wait_ge(var_ready[s], var_ready.at(r, u + 1))
                    act.activation(small[s][0:p, 4, :], small[s][0:p, 3, :], ACT.Sqrt).then_inc(sd_ready[s], 1)

                if r == 0:
                    act.wait_ge(zeroed, ZERO_DMAS * 16)
                front(0)
                schedule(act, r, {SAGE: sage_pair, GAT: gat_pair, TR: tr_pair}[kind], lambda i: None, unit)

            act.wait_ge(bn_var, 1)
            act.activation(bn_work[:, 3:4], bn_work[:, 2:3], ACT.Sqrt).then_inc(prep_act, 1)

            r = R_OUT

            def out_unit(u):
                for s in range(2):
                    roots(u, s, r)
                for s in range(2):
                    store(u, s, r, out)

            with act.Fori(0, UNITS) as u:
                out_unit(u)
            out_unit(UNITS)
            for s in range(2):
                act.wait_ge(stored[s], stored.at(r, UNITS + 1))

        @block.vector
        def _(dve):
            NW = NOWHERE
            for t, v in ((dst_i[:], NW), (src_i[:], NW), (wt_f[:], 0.0), (zeros[:], 0.0), (ones_row[:], 1.0),
                         (score_ones[:], float(D) ** -0.5), (head_mask[:], 0.0), (head_pick[:], 0.0), (start_neg[0][:], 0.0),
                         (start_neg[1][:], 0.0)):
                dve.memset(t, v).then_inc(filled, 1)
            dve.wait_ge(filled, FILLS)
            n = [0]

            def done(instruction):
                instruction.then_inc(prep, 1)
                n[0] += 1
                dve.wait_ge(prep, n[0])

            for h in range(HEADS):
                dve.memset(head_mask[h * HDIM:(h + 1) * HDIM, h * HDIM:(h + 1) * HDIM], 1.0)
                dve.memset(head_pick[h * HDIM:h * HDIM + 1, h:h + 1], 1.0)
            for q in range(2):
                for t in (run[q], seg_max[q], den[q]):
                    dve.memset(t[:], 0.0)
                dve.memset(unit_end[q][:], 0)
                dve.memset(idx[q][:, BLOCKS:BLOCKS + 2, :], 0)
            dve.memset(before_f[:], float(NW + 1))
            dve.memset(after_f[:], float(NW))
            dve.memset(all_ones[:], 1.0)
            dve.memset(no_ones[:], 0.0)
            dve.memset(carry[0][:], 0.0)
            dve.memset(carry[1][:], 0.0)
            dve.memset(rec_t[:], 0.0)
            done(dve.memset(carry_row[:], 0.0))
            dve.wait_ge(loaded, 16 * len(LOADS))
            done(dve.tensor_scalar(att_rep[:], head_mask[:], cols[:, C_ATT:C_ATT + 1], None, ALU.mult))
            dve.sem_inc(att_ready, 1)
            dve.wait_ge(prep_pool, 8)
            dve.tensor_copy(iota_f[:], iota_i[:])
            dve.tensor_copy(pos_f[:], place_i[:])
            dve.tensor_copy(key_f[:], dst_i[:])
            done(dve.tensor_copy(other_f[:], src_i[:]))

            def by_block(bank):
                return bank[:, 0:CPB * BLOCKS].rearrange("p (k b) -> p b k", k=CPB)

            def build_tables(t):
                dve.sem_inc(key_ready, 1)
                dve.wait_ge(ends_in, 32 * (t + 1))
                dve.tensor_tensor(keep_f[:, 1:BLOCK], key_f[:, 1:BLOCK], key_f[:, 0:BLOCK - 1], ALU.is_equal)
                done(dve.tensor_tensor(keep_f[:, 0:1], key_f[:, 0:1], before_f[:], ALU.is_equal))
                if t == 1:
                    dve.wait_ge(keep_out, 16)
                done(dve.tensor_copy(keep_u[:], keep_f[:]))
                dve.sem_inc(keep_ready, 1)
                dve.tensor_tensor(scat_f[:, 0:BLOCK - 1], key_f[:, 0:BLOCK - 1], key_f[:, 1:BLOCK], ALU.is_equal)
                done(dve.tensor_tensor(scat_f[:, BLOCK - 1:BLOCK], key_f[:, BLOCK - 1:BLOCK], after_f[:], ALU.is_equal))
                dve.scalar_tensor_tensor(scat_f[:], scat_f[:], float(NW), key_f[:], ALU.mult, ALU.add)
                dve.tensor_scalar(keyc_f[:], key_f[:], float(N - 1), None, ALU.min)
                done(dve.tensor_scalar(otherc_f[:], other_f[:], float(N - 1), None, ALU.min))
                if t == 0:
                    done(dve.tensor_tensor(start_f[:], keep_f[:], pos_f[:], ALU.mult))
                    done(dve.tensor_tensor(start_f[:], pos_f[:], start_f[:], ALU.subtract))
                    done(dve.tensor_reduce(carry_col[:], start_f[:], AX_X, ALU.max))
                    dve.sem_inc(last_start, 1)
                    dve.wait_ge(last_start_t, 1)
                    done(dve.tensor_tensor_scan(carry_row[:, 1:BLOCKS + 1], zeros[0:1, 0:BLOCKS],
                                                pe_bank[0][0:1, 0:BLOCKS], 0.0, ALU.add, ALU.max))
                    dve.sem_inc(first_start, 1)
                    dve.wait_ge(first_start_t, 1)
                    done(dve.tensor_copy(carry_col[:], pe_bank[1][0:BLOCKS, 0:1]))
                    done(dve.tensor_tensor_scan(inv_f[:], start_f[:], start_f[:], carry_col[:], ALU.max, ALU.max))
                    done(dve.tensor_tensor(inv_f[:], pos_f[:], inv_f[:], ALU.subtract))
                    done(dve.tensor_scalar(inv_f[:], inv_f[:], 1.0, None, ALU.add))
                    done(dve.reciprocal(inv_f[:], inv_f[:]))
                dve.sem_inc(tab_ready, 1)
                dve.wait_ge(tab_t, t + 1)
                dve.tensor_copy(idx[t][:, 0:BLOCKS, 0:CPB], by_block(ht_bank[0]))
                dve.tensor_copy(idx[t][:, 0:BLOCKS, CPB:2 * CPB], by_block(ht_bank[1]))
                dve.tensor_copy(idx[t][:, 0:BLOCKS, 2 * CPB:3 * CPB], by_block(o_bank[1]))
                if t == 0:
                    dve.tensor_copy(inv[:], by_block(pe_bank[0]))
                end = unit_end[t][0:1, 1:PAIRS + 1]
                done(dve.tensor_copy(end, pe_bank[1][0:1, 0:BLOCKS].rearrange("o (i q) -> o i q", q=2)[:, :, 0]))
                done(dve.tensor_scalar(end, end, SHIFT, None, ALU.logical_shift_right))
                done(dve.tensor_scalar(end, end, float(UNITS - 3), None, ALU.min))
                dve.sem_inc(tab_used, 1)

            build_tables(0)
            for n_pass in range(2):
                if n_pass == 0:
                    done(dve.tensor_scalar(digit_i[:], src_i[:], DIGITS - 1, None, ALU.bitwise_and))
                else:
                    dve.wait_ge(rec_in, 16)
                    done(dve.tensor_copy(src_i[:], rec_f[:, :, 0]))
                    done(dve.tensor_scalar(digit_i[:], src_i[:], LOW_BITS, None, ALU.logical_shift_right))
                done(dve.tensor_copy(digit_f[:], digit_i[:]))
                dve.sem_inc(sort_ready, 1)
                dve.wait_ge(sort_t, n_pass + 1)
                for c, bank in enumerate((ht_bank[0], ht_bank[1], o_bank[1])):
                    dve.tensor_copy(rec_t[:, :, :, c], by_block(bank))
                done(dve.tensor_copy(digit_t[:], by_block(pe_bank[0])))
                dve.sem_inc(sort_used, 1)
                loop = 2 * n_pass * BLOCKS
                with dve.Fori(0, BLOCKS) as b:
                    for k in range(CPB):
                        dve.wait_ge(counted[k], b + loop)
                        dve.tensor_scalar(onehot[k][:], iota_f[:], digit_t[:, bass.ds(b, 1), k], None, ALU.is_gt).then_inc(hot, 1)
                loop += BLOCKS
                with dve.Fori(0, PAIRS) as i:
                    for q in range(2):
                        b = 2 * i + q
                        for k in range(CPB):
                            dve.wait_ge(counted[k], b + loop)
                            dve.tensor_scalar(onehot[k][:], iota_f[:], digit_t[:, bass.ds(b, 1), k], None, ALU.is_equal).then_inc(hot, 1)
                        for k in range(CPB):
                            dve.wait_ge(hot, (b + loop) * CPB + k + 1)
                            dve.wait_ge(ranked, (b + n_pass * BLOCKS) * CPB + k + 1)
                            dve.tensor_tensor_reduce(picked[:], onehot[k][:], pe_bank[2][:], 1.0, 0.0, ALU.mult, ALU.add,
                                                     place_f[:, k:k + 1]).then_inc(placed, 1)
                            dve.wait_ge(placed, (b + n_pass * BLOCKS) * CPB + k + 1)
                        dve.wait_ge(rec_out[q], (i + n_pass * PAIRS) * CPB * 16)
                        dve.tensor_copy(place_idx[q][:], place_f[:])
                        dve.tensor_copy(rec_rows[q][:], rec_t[:, bass.ds(b, 1), :, :].rearrange("p o k c -> p (o k) c")
                                        ).then_inc(slot_ready[q], 1)
            dve.wait_ge(rec_in, 32)
            dve.tensor_copy(key_f[:], rec_f[:, :, 0])
            dve.tensor_copy(other_f[:], rec_f[:, :, 1])
            done(dve.tensor_copy(wt_f[:], rec_f[:, :, 2]))
            build_tables(1)
            dve.wait_ge(prep_act, 9)
            dve.sem_inc(tables_done, 1)

            esteps, usteps = 0, 0
            for r in range(NR):
                kind, tail = ROUNDS[r][0:2]
                eper = {SAGE: 0, GAT: 2 * 8, TR: 2 * 6}[kind]
                uper = {"norm": 2 * 2, "norm_ln": 2 * 5, "relu": 0, "relu_ln": 2 * 3, "gat": 2 * 8, "tr": 0}[tail]

                dve.wait_ge(keep_in, 16 * len([x for x in keep_loads if x <= r]))
                for q in range(2):
                    dve.wait_ge(gathered[q], gathered.at(r, 0))
                    dve.tensor_copy(g_idx[q][:], idx[order(r)][:, q, 0:2 * CPB]).then_inc(gidx_ready[q], 1)

                def next_gather(i, q, r):
                    dve.wait_ge(gathered[q], gathered.at(r, i + 1))
                    if ROUNDS[r][0] == TR:
                        dve.wait_ge(gathered_d[q], gathered_d.at(r, i + 1))
                    dve.tensor_copy(g_idx[q][:], idx[order(r)][:, bass.ds(2 * i + 2 + q, 1), 0:2 * CPB].rearrange("p o k -> p (o k)")
                                    ).then_inc(gidx_ready[q], 1)

                def next_scatter(i, q, r):
                    dve.wait_ge(scattered[q], scattered.at(r, i))
                    dve.tensor_copy(s_idx[q][:], idx[order(r)][:, bass.ds(2 * i + q, 1), 2 * CPB:3 * CPB].rearrange("p o k -> p (o k)")
                                    ).then_inc(sidx_ready[q], 1)

                def keep_of(i, q):
                    return keep[:, bass.ds((2 * i + q) * BLOCK, BLOCK)]

                def sage_pair(i, r=r):
                    for q in range(2):
                        next_gather(i, q, r)
                        dve.wait_ge(gt_ready[q], gt_ready.at(r, i + 1))
                        dve.wait_ge(yp_ready[q], yp_ready.at(r, i))
                        dve.wait_ge(run_ready[1 - q], run_ready.at(r, i + q))
                        dve.tensor_tensor_scan(run[q][:], keep_of(i, q), pe_bank[q][:], run[1 - q][:, BLOCK - 1:BLOCK],
                                               ALU.mult, ALU.add).then_inc(run_ready[q], 1)
                        next_scatter(i, q, r)

                def maxima(i, q, r, st, logits):
                    before = 1 - q
                    dve.wait_ge(neg_ready[q], neg_ready.at(r, i + 1))
                    st.wait()
                    st.done(dve.tensor_tensor_scan(seg_max[q][:], start_neg[q][:, 0:BLOCK], logits,
                                                   seg_max[before][:, BLOCK - 1:BLOCK], ALU.add, ALU.max))
                    st.done(dve.tensor_tensor_scan(full_max[q][:, ::-1], start_neg[q][:, BLOCK:0:-1], seg_max[q][:, ::-1], -BIG,
                                                   ALU.add, ALU.max))
                    st.mark(dve.tensor_scalar(carry[q][:, 0:1], seg_max[before][:, BLOCK - 1:BLOCK], full_max[q][:, 0:1], 0.0,
                                              ALU.subtract, ALU.min))
                    dve.tensor_tensor(expd[q][:], logits, full_max[q][:], ALU.subtract).then_inc(shift_ready[q], 1)

                def sums(i, q, r, st, values, bias_col, weighted_by):
                    before = 1 - q
                    dve.wait_ge(exp_ready[q], exp_ready.at(r, i + 1))
                    if weighted_by is not None:
                        dve.wait_ge(extra_in[q], extra_in.at(r, i + 1))
                        st.done(dve.tensor_tensor(expd[q][:], expd[q][:], weighted_by, ALU.mult))
                    if q == 0:
                        dve.wait_ge(sums_ready[1], sums_ready.at(r, i))
                    else:
                        dve.wait_ge(sums_ready[0], sums_ready.at(r, i + 1))
                    dve.tensor_scalar(carry[q][:, 2:3], den[before][:, BLOCK - 1:BLOCK], carry[q][:, 1:2], None, ALU.mult)
                    dve.tensor_scalar(carry[q][:, 3:4], num[before][:, BLOCK - 1:BLOCK], carry[q][:, 1:2], None, ALU.mult)
                    st.done(dve.scalar_tensor_tensor(msg[q][:], values, bias_col, expd[q][:], ALU.add, ALU.mult))
                    dve.wait_ge(yp_ready[q], yp_ready.at(r, i))
                    dve.tensor_tensor_scan(den[q][:], keep_of(i, q), expd[q][:], carry[q][:, 2:3], ALU.mult, ALU.add)
                    dve.tensor_tensor_scan(num[q][:], keep_of(i, q), msg[q][:], carry[q][:, 3:4], ALU.mult,
                                           ALU.add).then_inc(sums_ready[q], 1)

                def divided_rows(i, q, r, st):
                    dve.wait_ge(yp_ready[q], yp_ready.at(r, i + 1))
                    st.done(dve.tensor_scalar(den_inv[q][:, 0], pe_bank[2 + q][:, 0:CPB * HEADS], 1e-10, None, ALU.max))
                    st.done(dve.reciprocal(den_inv[q][:, 1], den_inv[q][:, 0]))
                    dve.wait_ge(scattered[q], scattered.at(r, i))
                    dve.tensor_tensor(y_rows[q][:].rearrange("p k (h d) -> p (k h) d", h=HEADS),
                                      pe_bank[q][:].rearrange("p (n d) -> p n d", d=HDIM),
                                      den_inv[q][:, 1].unsqueeze(2).to_broadcast([P, CPB * HEADS, HDIM]),
                                      ALU.mult).then_inc(y_ready[q], 1)

                def gat_pair(i, r=r, base=esteps, per=eper):
                    st = Steps(dve, edge_steps, base, per, i)
                    for q in range(2):
                        next_gather(i, q, r)
                        dve.wait_ge(raw_ready[q], raw_ready.at(r, i + 1))
                        st.done(dve.scalar_tensor_tensor(logit[q][:], logit_raw[q][:], 0.2, logit_raw[q][:], ALU.mult, ALU.max))
                        maxima(i, q, r, st, logit[q][:])
                    for q in range(2):
                        sums(i, q, r, st, pe_bank[2 + q][:], cols[:, C_B0:C_B0 + 1], wt_bc[q][:])
                    for q in range(2):
                        divided_rows(i, q, r, st)
                        next_scatter(i, q, r)
                    st.end()

                def tr_pair(i, r=r, base=esteps, per=eper):
                    st = Steps(dve, edge_steps, base, per, i)
                    for q in range(2):
                        next_gather(i, q, r)
                        dve.wait_ge(raw_ready[q], raw_ready.at(r, i + 1))
                        dve.scalar_tensor_tensor(prod[q][:], pe_bank[2 + q][:], cols[:, C_BQ:C_BQ + 1], logit_raw[q][:],
                                                 ALU.add, ALU.mult).then_inc(prod_ready[q], 1)
                    for q in range(2):
                        dve.wait_ge(score_ready[q], score_ready.at(r, i + 1))
                        maxima(i, q, r, st, pe_bank[q][:])
                    for q in range(2):
                        dve.wait_ge(val_ready[q], val_ready.at(r, i + 1))
                        sums(i, q, r, st, pe_bank[2 + q][:], cols[:, C_BV:C_BV + 1], None)
                    for q in range(2):
                        divided_rows(i, q, r, st)
                        next_scatter(i, q, r)
                    st.end()

                def statistics(st, s, p, of):
                    for j in range(RPP):
                        last = dve.bn_stats(st6[s][0:p, j, :], of[0:p, j, :])
                    st.done(last)
                    dve.sem_inc(dve_turn, 1)
                    for j in range(RPP):
                        last = dve.bn_aggr(mv[s][0:p, j, :], st6[s][0:p, j, :])
                    st.done(last)

                def layer_norm(st, u, r, on_act=False):
                    for s in range(2):
                        p = width(u, s)
                        statistics(st, s, p, t2[s])
                        dve.tensor_scalar(small[s][0:p, 3, :], mv[s][0:p, :, 1], LN_EPS, None, ALU.add).then_inc(var_ready[s], 1)
                    for s in range(2):
                        p = width(u, s)
                        dve.wait_ge(sd_ready[s], sd_ready.at(r, u + 1))
                        st.done(dve.reciprocal(small[s][0:p, 5, :], small[s][0:p, 4, :]))
                        if on_act:
                            dve.scalar_tensor_tensor(small2[s][0:p, 1, :], mv[s][0:p, :, 0], -1.0, small[s][0:p, 5, :],
                                                     ALU.mult, ALU.mult).then_inc(rs_ready[s], 1)
                            continue
                        dve.wait_ge(stored[s], stored.at(r, u))
                        for j in range(RPP):
                            last = dve.tensor_scalar(h_out[s][0:p, j, :], t2[s][0:p, j, :], mv[s][0:p, j, 0:1],
                                                     small[s][0:p, 5, j:j + 1], ALU.subtract, ALU.mult)
                        last.then_inc(out_ready[s], 1)

                def unit(u, r=r, tail=tail, base=usteps, per=uper):
                    st = Steps(dve, unit_steps, base, per, u)
                    for s in range(2):
                        p = width(u, s)
                        dve.wait_ge(mm_ready[s], mm_ready.at(r, u + 1))
                        dve.wait_ge(agg_loaded[s], agg_loaded.at(r, u + 1))
                        dve.wait_ge(out_ready[s], out_ready.at(r, u))
                        dve.tensor_tensor(flat(total[s], p), o_bank[s][0:p, :], flat(agg_in[s], p), ALU.add).then_inc(sum_ready[s], 1)
                    if tail in ("norm", "norm_ln"):
                        for s in range(2):
                            p = width(u, s)
                            dve.wait_ge(sq_ready[s], sq_ready.at(r, u + 1))
                            dve.tensor_reduce(small[s][0:p, 0, :], sq[s][0:p], AX_X, ALU.add).then_inc(ss_ready[s], 1)
                        for s in range(2):
                            p = width(u, s)
                            dve.wait_ge(nrm_ready[s], nrm_ready.at(r, u + 1))
                            st.done(dve.tensor_scalar(small[s][0:p, 2, :], small[s][0:p, 1, :], 1e-12, None, ALU.max))
                            st.done(dve.reciprocal(small[s][0:p, 5, :], small[s][0:p, 2, :]))
                            if tail == "norm":
                                dve.wait_ge(stored[s], stored.at(r, u))
                                for j in range(RPP):
                                    last = dve.tensor_scalar(h_out[s][0:p, j, :], total[s][0:p, j, :], small[s][0:p, 5, j:j + 1],
                                                             0.0, ALU.mult, ALU.max)
                                last.then_inc(out_ready[s], 1)
                            else:
                                dve.wait_ge(t1_ready[s], t1_ready.at(r, u + 1))
                                dve.wait_ge(res_loaded[s], res_loaded.at(r, u + 1))
                                for j in range(RPP):
                                    last = dve.scalar_tensor_tensor(t2[s][0:p, j, :], t1[s][0:p, j, :], small[s][0:p, 5, j:j + 1],
                                                                    res_in[s][0:p, j, :], ALU.mult, ALU.add)
                                last.then_inc(t2_ready[s], 1)
                    if tail == "relu_ln":
                        for s in range(2):
                            p = width(u, s)
                            dve.wait_ge(res_loaded[s], res_loaded.at(r, u + 1))
                            dve.wait_ge(sum_ready[s], sum_ready.at(r, u + 1))
                            dve.scalar_tensor_tensor(flat(t2[s], p), flat(total[s], p), 0.0, flat(res_in[s], p), ALU.max,
                                                     ALU.add).then_inc(t2_ready[s], 1)
                    if tail == "gat":
                        for s in range(2):
                            p = width(u, s)
                            dve.wait_ge(t1_ready[s], t1_ready.at(r, u + 1))
                            statistics(st, s, p, t1[s])
                            dve.tensor_scalar(small[s][0:p, 0, :], mv[s][0:p, :, 1], 1e-9, None, ALU.add).then_inc(gvar_ready[s], 1)
                        for s in range(2):
                            p = width(u, s)
                            dve.wait_ge(gsd_ready[s], gsd_ready.at(r, u + 1))
                            st.done(dve.reciprocal(small[s][0:p, 2, :], small[s][0:p, 1, :]))
                            dve.scalar_tensor_tensor(small2[s][0:p, 0, :], mv[s][0:p, :, 0], -1.0, small[s][0:p, 2, :],
                                                     ALU.mult, ALU.mult).then_inc(grs_ready[s], 1)
                        for s in range(2):
                            p = width(u, s)
                            dve.wait_ge(res_loaded[s], res_loaded.at(r, u + 1))
                            st.mark(dve.tensor_tensor(res_in[s][0:p], res_in[s][0:p], bc_rows(offset_bc, p), ALU.add))
                        for s in range(2):
                            p = width(u, s)
                            dve.wait_ge(gln_ready[s], gln_ready.at(r, u + 1))
                            st.done(dve.tensor_tensor(t2[s][0:p], t2[s][0:p], bc_rows(scale_bc, p), ALU.mult))
                            dve.tensor_tensor(t2[s][0:p], t2[s][0:p], res_in[s][0:p], ALU.add).then_inc(t2_ready[s], 1)
                    if tail in ("norm_ln", "relu_ln", "gat"):
                        for s in range(2):
                            dve.wait_ge(t2_ready[s], t2_ready.at(r, u + 1))
                        layer_norm(st, u, r, on_act=tail == "gat")
                    if tail == "tr":
                        for s in range(2):
                            p = width(u, s)
                            g = 2 * u + s
                            dve.wait_ge(hot_ready[s], hot_ready.at(r, u + 1))
                            place = bn_stat[:, g, :] if isinstance(u, int) else bn_stat[:, bass.ds(g, 1), :].rearrange("p o c -> p (o c)")
                            dve.bn_stats(place, ht_bank[s][:].rearrange("p (j n) -> p j n", j=RPP)[:, :, 0:p]).then_inc(bn_ready[s], 1)
                    st.end()

                schedule(dve, r, {SAGE: sage_pair, GAT: gat_pair, TR: tr_pair}[kind], lambda i: None, unit)
                esteps += eper * PAIRS
                usteps += uper * (UNITS + 1)

            for s in range(2):
                dve.wait_ge(bn_ready[s], bn_ready.at(R_TR, UNITS + 1))
            done(dve.bn_aggr(bn_work[:, 0:2], bn_stat[:].rearrange("p g c -> p (g c)")))
            done(dve.tensor_scalar(bn_work[:, 2:3], bn_work[:, 1:2], 1e-5, None, ALU.add))
            dve.sem_inc(bn_var, 1)
            dve.wait_ge(prep_act, 10)
            done(dve.reciprocal(bn_work[:, 6:7], bn_work[:, 3:4]))
            done(dve.tensor_tensor(bn_work[:, 4:5], cols[:, C_GAMMA:C_GAMMA + 1], bn_work[:, 6:7], ALU.mult))
            done(dve.tensor_tensor(bn_work[:, 7:8], bn_work[:, 0:1], bn_work[:, 4:5], ALU.mult))
            done(dve.tensor_tensor(bn_work[:, 5:6], cols[:, C_BETA:C_BETA + 1], bn_work[:, 7:8], ALU.subtract))
            dve.sem_inc(bn_coef, 1)
            dve.wait_ge(prep_pe, 9)
            done(dve.tensor_copy(bn_a[:], o_bank[0][:, 0:P]))
            done(dve.tensor_copy(bn_b[:], o_bank[1][:, 0:P]))

            r = R_OUT
            oper = 2 * (2 + 3)

            def out_unit(u):
                st = Steps(dve, unit_steps, usteps, oper, u)
                for s in range(2):
                    p = width(u, s)
                    dve.wait_ge(h_loaded[s], h_loaded.at(r, u + 1))
                    dve.wait_ge(agg_loaded[s], agg_loaded.at(r, u + 1))
                    dve.wait_ge(out_ready[s], out_ready.at(r, u))
                    st.done(dve.tensor_tensor(t1[s][0:p], agg_in[s][0:p], bc_rows(bn_a, p), ALU.mult))
                    st.done(dve.tensor_tensor(t1[s][0:p], t1[s][0:p], bc_rows(bn_b, p), ALU.add))
                    dve.tensor_tensor(t2[s][0:p], t1[s][0:p], h_in[s][0:p], ALU.add).then_inc(t2_ready[s], 1)
                for s in range(2):
                    dve.wait_ge(t2_ready[s], t2_ready.at(r, u + 1))
                layer_norm(st, u, r)
                st.end()

            with dve.Fori(0, UNITS) as u:
                out_unit(u)
            out_unit(UNITS)


_INS = ["x", "src", "dst", "edge_attr_10", "edge_weight", "L0_gnn_W1_l", "L0_gnn_b1_l", "L0_gnn_W1_r", "L0_gnn_W2_l",
        "L0_gnn_b2_l", "L0_gnn_W2_r", "L1_gnn_Wl", "L1_gnn_Wr", "L1_gnn_b", "L2_gnn_W0", "L2_gnn_b0", "L2_gnn_W1",
        "L2_gnn_b1", "L2_gnn_att", "L2_gnn_scale", "L2_gnn_offset", "L3_gnn_Wq", "L3_gnn_bq", "L3_gnn_Wk", "L3_gnn_bk",
        "L3_gnn_Wv", "L3_gnn_bv", "L3_gnn_We", "L3_gnn_Wskip", "L3_gnn_bskip", "L3_gnn_gamma", "L3_gnn_beta"]


def kernel(**inputs):
    import numpy as _np
    import concourse.bacc as _bacc
    from concourse.bass_utils import run_bass_kernel_spmd as _run

    nc = _bacc.Bacc("TRN2", target_bir_lowering=False, num_devices=1)
    arrays, io = {}, {}
    for name in _INS:
        a = _np.ascontiguousarray(inputs[name])
        arrays[f"in_{name}_dram"] = a
        io[name] = nc.dram_tensor(f"in_{name}_dram", a.shape, mybir.dt.from_np(a.dtype), kind="ExternalInput").ap()
    out = nc.dram_tensor("out_0_dram", inputs["x"].shape, F32, kind="ExternalOutput").ap()
    gnn_kernel(nc, io, out)
    r = _run(nc, [arrays], core_ids=[0])
    return r.results[0]["out_0_dram"]
```

```python
from contextlib import ExitStack

import concourse.bass as bass
from concourse import mybir

F32 = mybir.dt.float32
I32 = mybir.dt.int32
U8 = mybir.dt.uint8
BF16 = mybir.dt.bfloat16
F16 = mybir.dt.float16
ALU = mybir.AluOpType
ACT = mybir.ActivationFunctionType
AX_X = mybir.AxisListType.X

P = 128
RPP = 4
GROUP = P * RPP
UNIT = 2 * GROUP
CPB = 4
BLOCK = P * CPB
BIG = 1e30
LN_EPS = 1e-5
LOW_BITS = 9
DIGITS = 1 << LOW_BITS
REC = 4


class Stage:

    every = []

    def __init__(self, sems, rounds, per_round, step=1):
        self.sems, self.rounds, self.per_round, self.step = sems, rounds, per_round, step
        Stage.every.append(self)

    def __getitem__(self, slot):
        return self.sems[slot]

    def at(self, r, n):
        before = len([x for x in self.rounds if x < r]) * self.per_round
        return (n + before) * self.step + (self.step == 1)


def gnn_kernel(nc, io, out):
    N = io["x"].shape[0]
    E = io["src"].shape[0]
    D = io["x"].shape[1]
    EDIM = io["edge_attr_10"].shape[1]
    HEADS, HDIM = io["L2_gnn_att"].shape
    assert D == P and HEADS * HDIM == D
    Stage.every = []
    UNITS = N // UNIT
    TAILP = (N - UNITS * UNIT - GROUP) // RPP
    assert UNITS * UNIT + GROUP + TAILP * RPP == N and 0 < TAILP <= P
    BLOCKS = -(-E // BLOCK)
    BLOCKS += BLOCKS % 2
    PAIRS = BLOCKS // 2
    EPAD = BLOCKS * BLOCK
    FULLB = E // BLOCK
    RESTE = E - FULLB * BLOCK
    assert FULLB == BLOCKS - 1 and 1 < RESTE < BLOCK
    NOWHERE = 1 << 17
    assert N <= NOWHERE and NOWHERE >> LOW_BITS < DIGITS
    WIDTHS = [DIGITS, (NOWHERE >> LOW_BITS) + 8]
    SHIFT = UNIT.bit_length() - 1

    SAGE, GAT, TR = "sage", "gat", "tr"
    dram = {n: nc.dram_tensor(n, [N, D], F32).ap() for n in ("node_a", "node_b", "node_x", "agg0", "agg1")}
    x_in, node_a, node_b, node_x = io["x"], dram["node_a"], dram["node_b"], dram["node_x"]
    agg = [dram["agg0"], dram["agg1"]]
    w1 = [io["L1_gnn_Wl"][k] for k in range(4)]
    v1 = [io["L1_gnn_Wr"][k] for k in range(4)]
    c1 = [io["L1_gnn_b"][k:k + 1, :] for k in range(4)]

    def row(v):
        return v.unsqueeze(0)

    ROUNDS = [
        (SAGE, "norm", x_in, None, node_a, io["L0_gnn_W1_l"], io["L0_gnn_W1_r"], row(io["L0_gnn_b1_l"])),
        (SAGE, "norm_ln", node_a, x_in, node_x, io["L0_gnn_W2_l"], io["L0_gnn_W2_r"], row(io["L0_gnn_b2_l"])),
        (SAGE, "relu", node_x, None, node_a, w1[0], v1[0], c1[0]),
        (SAGE, "relu", node_a, None, node_b, w1[1], v1[1], c1[1]),
        (SAGE, "relu", node_b, None, node_a, w1[2], v1[2], c1[2]),
        (SAGE, "relu_ln", node_a, node_x, node_b, w1[3], v1[3], c1[3]),
        (GAT, "gat", node_b, node_b, node_x, None, io["L2_gnn_W1"], row(io["L2_gnn_b1"])),
        (TR, "tr", node_x, None, node_a, None, io["L3_gnn_Wskip"], row(io["L3_gnn_bskip"])),
    ]
    NR = len(ROUNDS)
    R_GAT, R_TR, R_OUT = 6, 7, 8
    sage_rounds = [r for r in range(NR) if ROUNDS[r][0] == SAGE]
    soft_rounds = [R_GAT, R_TR]
    all_edges = list(range(NR))
    all_dense = list(range(NR))
    all_store = list(range(NR + 1))
    tails = {k: [r for r in range(NR) if ROUNDS[r][1] == k] for k in ("norm", "norm_ln", "relu", "relu_ln", "gat", "tr")}
    norm_rounds = tails["norm"] + tails["norm_ln"]
    t1_rounds = tails["norm_ln"] + tails["gat"]
    ln_rounds = sorted(tails["norm_ln"] + tails["relu_ln"] + tails["gat"] + [R_OUT])
    res_rounds = sorted(tails["norm_ln"] + tails["relu_ln"] + tails["gat"])

    with ExitStack() as ctx:
        def sb(name, shape, dt=F32):
            return ctx.enter_context(nc.sbuf_tensor(name, shape, dt))

        def sb2(name, shape, dt=F32):
            return [sb(f"{name}{k}", shape, dt) for k in range(2)]

        def sem(name):
            return ctx.enter_context(nc.semaphore(name))

        def edge_stage(name, rounds, step=1):
            return Stage([sem(f"{name}{k}") for k in range(2)], rounds, PAIRS, step)

        def unit_stage(name, rounds, step=1):
            return Stage([sem(f"{name}{k}") for k in range(2)], rounds, UNITS + 1, step)

        keep_dram = [nc.dram_tensor(f"keep_dram{t}", [EPAD], U8).ap() for t in range(2)]
        weight_dram = nc.dram_tensor("weight_dram", [EPAD], F32).ap()
        rec_dram = [nc.dram_tensor(f"rec_dram{t}", [EPAD, REC], F32).ap() for t in range(2)]
        attr_dram = nc.dram_tensor("attr_dram", [EPAD, EDIM], F32).ap()

        ident = sb("ident", [P, P])
        score_ones = sb("score_ones", [P, P])
        head_mask = sb("head_mask", [P, P])
        head_pick = sb("head_pick", [P, HEADS])
        keep = sb("keep", [P, EPAD], U8)
        idx = [sb(f"idx{t}", [P, BLOCKS + 2, 3 * CPB], I32) for t in range(2)]
        inv = sb("inv", [P, BLOCKS, CPB])
        unit_end = [sb(f"unit_end{t}", [1, PAIRS + 1], I32) for t in range(2)]
        zeros = sb("zeros", [P, 16 * P])
        w_l = {r: sb(f"w_l{r}", [P, P]) for r in sage_rounds}
        w_r = {r: sb(f"w_r{r}", [P, P]) for r in range(NR)}
        b_rep = sb("b_rep", [3, NR, P])
        b_parts = sb("b_parts", [3, NR, P], BF16)
        ones_parts = sb("ones_parts", [3, P], BF16)
        natural = {n: sb(f"nat_{n}", [P, P]) for n in ("W0", "W1", "Wq", "Wk", "Wv", "Wskip")}
        we_nat = sb("we_nat", [P, EDIM])
        w0_t, wq_t, wk_t, wv_t = sb("w0_t", [P, P]), sb("wq_t", [P, P]), sb("wk_t", [P, P]), sb("wv_t", [P, P])
        we_t = sb("we_t", [EDIM, P])
        att_rep = sb("att_rep", [P, P])
        w_att = sb("w_att", [P, P])
        cols = sb("cols", [P, 8])
        C_ATT, C_B0, C_BQ, C_BK, C_BV, C_GAMMA, C_BETA, C_BATT = range(8)
        scale_bc, offset_bc = sb("scale_bc", [P, P]), sb("offset_bc", [P, P])
        bn_stat = sb("bn_stat", [P, 2 * (UNITS + 1), 6])
        bn_work = sb("bn_work", [P, 8])
        arena_at = [0]

        def in_arena(parts, shape, dt=F32):
            count = 1
            for size in shape:
                count *= size
            nbytes = count * mybir.dt.size(dt)
            at = arena_at[0]
            arena_at[0] += -(-nbytes // 32) * 32
            assert arena_at[0] <= EPAD
            t = keep[0:parts, at:at + nbytes].bitcast(dt)
            if len(shape) == 2:
                t = t.rearrange("p (a b) -> p a b", a=shape[0])
            if len(shape) == 3:
                t = t.rearrange("p (a b c) -> p a b c", a=shape[0], b=shape[1])
            return t

        def block_table(dt=F32):
            return in_arena(BLOCKS, [BLOCK], dt)

        src_i, digit_i, keep_u = block_table(I32), block_table(I32), block_table(U8)
        key_f, other_f, wt_f, keep_f, scat_f, keyc_f, otherc_f = (block_table() for _ in range(7))
        inv_f = digit_f = block_table()
        arena_rec = arena_at[0]
        dst_i, place_i, pos_f, start_f = block_table(I32), block_table(I32), block_table(), block_table()
        arena_at[0] = arena_rec
        rec_f = in_arena(BLOCKS, [BLOCK, REC])
        before_f, after_f = sb("before_f", [BLOCKS, 1]), sb("after_f", [BLOCKS, 1])
        carry_col, carry_row = sb("carry_col", [BLOCKS, 1]), sb("carry_row", [1, BLOCKS + 1])
        rec_t = in_arena(P, [BLOCKS, CPB, REC])
        digit_t = in_arena(P, [BLOCKS, CPB])
        iota_i, iota_f = in_arena(P, [DIGITS], I32), in_arena(P, [DIGITS], F16)
        b_wide_at = arena_at[0]
        onehot = [in_arena(P, [DIGITS], BF16) for k in range(CPB)]
        b_low_at = arena_at[0]
        picked = in_arena(P, [DIGITS])
        assert 4 * NR * P <= CPB * 2 * DIGITS and 2 * NR * P <= 4 * DIGITS
        b_wide = keep[0:3, b_wide_at:b_wide_at + 4 * NR * P].bitcast(F32).rearrange("p (r f) -> p r f", r=NR)
        b_low = keep[0:3, b_low_at:b_low_at + 2 * NR * P].bitcast(BF16).rearrange("p (r f) -> p r f", r=NR)
        before_ones, rest_ones = sb("before_ones", [P, P], BF16), sb("rest_ones", [P, P], BF16)
        all_ones, no_ones = sb("all_ones", [P, P], BF16), sb("no_ones", [P, P], BF16)
        place_f = sb("place_f", [P, CPB])
        place_idx, rec_rows = sb2("place_idx", [P, CPB], I32), sb2("rec_rows", [P, CPB, REC])
        g_idx = sb2("g_idx", [P, 2 * CPB], I32)
        s_idx = sb2("s_idx", [P, CPB], I32)
        gath = sb2("gath", [P, CPB, P])
        gath_d = sb2("gath_d", [P, CPB, P])
        run = sb2("run", [P, BLOCK])
        y_rows = sb2("y_rows", [P, CPB, P])
        seg_max, den, num = sb2("seg_max", [P, BLOCK]), sb2("den", [P, BLOCK]), run
        gsrc_t = sb2("gsrc_t", [P, BLOCK])
        attr = sb2("attr", [P, CPB, EDIM])
        attr_t = sb2("attr_t", [EDIM, BLOCK])
        wt_bc = sb2("wt_bc", [P, BLOCK])
        start_neg = sb2("start_neg", [P, BLOCK + 1])
        logit_raw = sb2("logit_raw", [P, BLOCK])
        logit = sb2("logit", [P, BLOCK])
        gdst_t = prod = logit
        full_max = sb2("full_max", [P, BLOCK])
        msg = full_max
        expd = sb2("expd", [P, BLOCK])
        carry = sb2("carry", [P, 4])
        den_inv = sb2("den_inv", [P, 2, CPB * HEADS])
        h_in, agg_in, res_in = sb2("h_in", [P, RPP, P]), sb2("agg_in", [P, RPP, P]), sb2("res_in", [P, RPP, P])
        h_t = sb2("h_t", [P, RPP, P])
        total, t2 = sb2("total", [P, RPP, P]), sb2("t2", [P, RPP, P])
        t1, sq = ([zeros[:, (2 * n + k) * GROUP:(2 * n + k + 1) * GROUP].rearrange("p (j f) -> p j f", j=RPP)
                   for k in range(2)] for n in range(2))
        h_out = sb2("h_out", [P, RPP, P])
        small = sb2("small", [P, 6, RPP])
        small2 = sb2("small2", [P, 6, RPP])
        spark = sb("spark", [1, 2])
        st6, mv = sb2("st6", [P, RPP, 6]), sb2("mv", [P, RPP, 2])
        pe_bank = [ctx.enter_context(nc.psum_tensor(f"edge_bank{k}", [P, BLOCK], F32)) for k in range(4)]
        ht_bank = [ctx.enter_context(nc.psum_tensor(f"ht_bank{k}", [P, GROUP], F32)) for k in range(2)]
        o_bank = [ctx.enter_context(nc.psum_tensor(f"o_bank{k}", [P, GROUP], F32)) for k in range(2)]

        filled, loaded, prep, prep_pe, prep_act, prep_pool = (sem(n) for n in ("filled", "loaded", "prep", "prep_pe", "prep_act", "prep_pool"))
        zeroed, keep_out, keep_in, padded, tables_done = (sem(n) for n in ("zeroed", "keep_out", "keep_in", "padded", "tables_done"))
        key_ready = sem("key_ready")
        ends_in = sem("ends_in")
        keep_ready = sem("keep_ready")
        att_ready = sem("att_ready")
        last_start, first_start = sem("last_start"), sem("first_start")
        last_start_t, first_start_t = sem("last_start_t"), sem("first_start_t")
        tab_ready, tab_t = sem("tab_ready"), sem("tab_t")
        tab_used = sem("tab_used")
        sort_ready, sort_t, sort_used = sem("sort_ready"), sem("sort_t"), sem("sort_used")
        hot = sem("hot")
        counted = [sem(f"counted{k}") for k in range(CPB)]
        ranked, placed = sem("ranked"), sem("placed")
        slot_ready = [sem(f"slot_ready{q}") for q in range(2)]
        rec_out = [sem(f"rec_out{q}") for q in range(2)]
        rec_in = sem("rec_in")
        bn_var, bn_coef = sem("bn_var"), sem("bn_coef")
        pool_turn, sp_turn, dve_turn = sem("pool_turn"), sem("sp_turn"), sem("dve_turn")
        gidx_ready = Stage([sem(f"gidx_ready{q}") for q in range(2)], all_edges, PAIRS + 1)
        sidx_ready = edge_stage("sidx_ready", all_edges)
        gathered = edge_stage("gathered", all_edges, 16 * CPB)
        gathered_d = edge_stage("gathered_d", [R_TR], 16 * CPB)
        scattered = edge_stage("scattered", all_edges, 16 * CPB)
        gt_ready = edge_stage("gt_ready", all_edges)
        run_ready = edge_stage("run_ready", sage_rounds)
        yp_ready = edge_stage("yp_ready", all_edges)
        y_ready = edge_stage("y_ready", all_edges)
        gts_ready = edge_stage("gts_ready", soft_rounds)
        lin_ready = edge_stage("lin_ready", soft_rounds)
        raw_ready = edge_stage("raw_ready", soft_rounds)
        neg_ready = edge_stage("neg_ready", soft_rounds)
        prod_ready = edge_stage("prod_ready", [R_TR])
        score_ready = edge_stage("score_ready", [R_TR])
        at_ready = edge_stage("at_ready", [R_TR])
        ats_ready = edge_stage("ats_ready", [R_TR])
        val_ready = edge_stage("val_ready", soft_rounds)
        shift_ready = edge_stage("shift_ready", soft_rounds)
        exp_ready = edge_stage("exp_ready", soft_rounds)
        sums_ready = edge_stage("sums_ready", soft_rounds)
        extra_in = edge_stage("extra_in", soft_rounds, 16)
        h_loaded = unit_stage("h_loaded", all_store, 16)
        agg_loaded = unit_stage("agg_loaded", all_store, 16)
        res_loaded = unit_stage("res_loaded", res_rounds, 16)
        htp_ready = unit_stage("htp_ready", all_store)
        ht_ready = unit_stage("ht_ready", all_store)
        mm_ready = unit_stage("mm_ready", all_store)
        sum_ready = unit_stage("sum_ready", all_dense)
        sq_ready = unit_stage("sq_ready", norm_rounds)
        ss_ready = unit_stage("ss_ready", norm_rounds)
        nrm_ready = unit_stage("nrm_ready", norm_rounds)
        t1_ready = unit_stage("t1_ready", t1_rounds)
        t2_ready = unit_stage("t2_ready", ln_rounds)
        var_ready = unit_stage("var_ready", ln_rounds)
        sd_ready = unit_stage("sd_ready", ln_rounds)
        gvar_ready = unit_stage("gvar_ready", tails["gat"])
        gsd_ready = unit_stage("gsd_ready", tails["gat"])
        grs_ready = unit_stage("grs_ready", tails["gat"])
        gln_ready = unit_stage("gln_ready", tails["gat"])
        rs_ready = unit_stage("rs_ready", ln_rounds)
        out_ready = unit_stage("out_ready", all_store)
        stored = unit_stage("stored", all_store, 16)
        hot_ready = unit_stage("hot_ready", [R_TR])
        bn_ready = unit_stage("bn_ready", [R_TR])
        fetched = sem("fetched")
        edge_steps = sem("edge_steps")
        unit_steps = sem("unit_steps")

        class Steps:

            def __init__(self, dve, semaphore, base, per, iteration):
                self.dve, self.sem, self.value, self.n, self.per = dve, semaphore, base + iteration * per, 0, per

            def mark(self, instruction):
                instruction.then_inc(self.sem, 1)
                self.n += 1

            def wait(self):
                self.dve.wait_ge(self.sem, self.value + self.n)

            def done(self, instruction):
                self.mark(instruction)
                self.wait()

            def end(self):
                assert self.n == self.per

        def unit_rows(t):
            return t[0:UNITS * UNIT].rearrange("(u h p j) f -> u h p (j f)", h=2, p=P, j=RPP)

        def group_dram(t, u, s):
            if isinstance(u, int):
                first = u * UNIT + s * GROUP
                p = width(u, s)
                return t[first:first + p * RPP].rearrange("(p j) f -> p (j f)", j=RPP)
            return unit_rows(t)[bass.ds(u, 1), s].rearrange("o p f -> (o p) f")

        def width(u, s):
            return TAILP if isinstance(u, int) and u == UNITS and s == 1 else P

        def flat(t, p=P):
            return t[0:p].rearrange("p j f -> p (j f)")

        def bc_rows(t, p):
            return t[0:p].unsqueeze(1).to_broadcast([p, RPP, P])

        def order(r):
            return 1 if ROUNDS[r][0] == GAT else 0

        def schedule(eng, r, edge_pair, before_units, unit):
            end = unit_end[order(r)]
            with eng.Fori(0, PAIRS - 1) as i:
                edge_pair(i)
                before_units(i)
                lo = eng.value_load(end[0:1, bass.ds(i, 1)], min_val=0, max_val=UNITS - 3)
                hi = eng.value_load(end[0:1, bass.ds(i + 1, 1)], min_val=0, max_val=UNITS - 3)
                with eng.If(lo < hi):
                    with eng.Fori(lo, hi) as u:
                        unit(u)
            edge_pair(PAIRS - 1)
            before_units(PAIRS)
            lo = eng.value_load(end[0:1, PAIRS - 1:PAIRS], min_val=0, max_val=UNITS - 3)
            with eng.Fori(lo, UNITS - 2) as u:
                unit(u)
            for u in range(UNITS - 2, UNITS + 1):
                unit(u)

        def out_units(eng, out_unit):
            twos = (UNITS - 2) // 2
            with eng.Fori(0, twos) as n:
                out_unit(2 * n, 0)
                out_unit(2 * n + 1, 1)
            for u in range(2 * twos, UNITS + 1):
                out_unit(u, u % 2)

        PREP_W = [("W0", pe_bank[0], 0), ("W1", pe_bank[0], P), ("Wq", pe_bank[1], 0), ("Wk", pe_bank[1], P),
                  ("Wv", pe_bank[2], 0), ("Wskip", pe_bank[2], P)]
        big_zero = [(n * P * 16, P, 16) for n in range(N // (P * 16))]
        at_zero = len(big_zero) * P * 16
        while at_zero < N:
            big_zero.append((at_zero, min(P, (N - at_zero) // RPP), RPP))
            at_zero += big_zero[-1][1] * RPP
        ZERO_DMAS = 2 * len(big_zero)

        ctx.enter_context(nc.allow_non_contiguous_dma(reason="vectors as columns and every 1024th destination, once"))
        block = ctx.enter_context(nc.Block())

        FILLS = 10
        LOADS = []
        keep_loads = [r for r in range(NR) if r == 0 or order(r) != order(r - 1)]

        @block.sync
        def _(sp):
            sp.wait_ge(filled, FILLS)
            dst, src = io["dst"], io["src"]

            def load(to, of):
                sp.dma_start(to, of).then_inc(loaded, 16)
                LOADS.append(1)

            load(dst_i[0:FULLB], dst[0:FULLB * BLOCK].rearrange("(p j) -> p j", j=BLOCK))
            load(dst_i[FULLB:FULLB + 1, 0:RESTE], row(dst[FULLB * BLOCK:E]))
            load(src_i[0:FULLB], src[0:FULLB * BLOCK].rearrange("(p j) -> p j", j=BLOCK))
            load(src_i[FULLB:FULLB + 1, 0:RESTE], row(src[FULLB * BLOCK:E]))
            load(wt_f[0:FULLB], io["edge_weight"][0:FULLB * BLOCK].rearrange("(p j) -> p j", j=BLOCK))
            load(wt_f[FULLB:FULLB + 1, 0:RESTE], row(io["edge_weight"][FULLB * BLOCK:E]))
            for r in range(NR):
                _, _, _, _, _, wl, wr, b = ROUNDS[r]
                if wl is not None:
                    load(w_l[r][:], wl)
                    load(w_r[r][:], wr)
                load(b_rep[:, r, :], b.to_broadcast([3, P]))
            for n, t in (("W0", "L2_gnn_W0"), ("W1", "L2_gnn_W1"), ("Wq", "L3_gnn_Wq"), ("Wk", "L3_gnn_Wk"),
                         ("Wv", "L3_gnn_Wv"), ("Wskip", "L3_gnn_Wskip")):
                load(natural[n][:], io[t])
            load(we_nat[:], io["L3_gnn_We"])
            load(cols[:, C_ATT:C_ATT + 1], io["L2_gnn_att"].rearrange("h d -> (h d)").unsqueeze(1))
            for c, t in ((C_B0, "L2_gnn_b0"), (C_BQ, "L3_gnn_bq"), (C_BK, "L3_gnn_bk"), (C_BV, "L3_gnn_bv"),
                         (C_GAMMA, "L3_gnn_gamma"), (C_BETA, "L3_gnn_beta")):
                load(cols[:, c:c + 1], io[t].unsqueeze(1))
            load(scale_bc[:], row(io["L2_gnn_scale"]).to_broadcast([P, P]))
            load(offset_bc[:], row(io["L2_gnn_offset"]).to_broadcast([P, P]))
            sp.dma_start(attr_dram[0:E].rearrange("(a b) f -> a (b f)", a=16),
                         io["edge_attr_10"].rearrange("(a b) f -> a (b f)", a=16)).then_inc(padded, 16)
            sp.dma_start(row(attr_dram[E:EPAD].rearrange("a f -> (a f)")),
                         zeros[0:1, 0:(EPAD - E) * EDIM]).then_inc(padded, 16)
            for t in range(2):
                if t == 1:
                    for n in range(2):
                        for q in range(2):
                            sp.wait_ge(rec_out[q], (n + 1) * PAIRS * CPB * 16)
                        if n == 1:
                            sp.wait_ge(sort_ready, 2)
                        sp.dma_start(rec_f[:].rearrange("p j c -> p (j c)"),
                                     rec_dram[n].rearrange("(p j) c -> p (j c)", j=BLOCK)).then_inc(rec_in, 16)
                sp.wait_ge(key_ready, t + 1)
                sp.dma_start(before_f[1:BLOCKS], key_f[0:BLOCKS - 1, BLOCK - 1:BLOCK]).then_inc(ends_in, 16)
                sp.dma_start(after_f[0:BLOCKS - 1], key_f[1:BLOCKS, 0:1]).then_inc(ends_in, 16)
                sp.wait_ge(keep_ready, t + 1)
                sp.dma_start(keep_dram[t].rearrange("(p j) -> p j", j=BLOCK), keep_u[:]).then_inc(keep_out, 16)
            sp.dma_start(weight_dram.rearrange("(p j) -> p j", j=BLOCK), wt_f[:]).then_inc(padded, 16)
            sp.wait_ge(keep_out, 32)
            sp.wait_ge(padded, 48)
            sp.wait_ge(tables_done, 1)

            weight_v = weight_dram.rearrange("(i q e) -> i q e", q=2, e=BLOCK)
            attr_v = attr_dram.rearrange("(i q k p) f -> i q p k f", q=2, k=CPB, p=P)
            for r in range(NR):
                kind, tail, h_of, res_of, _, _, _, _ = ROUNDS[r]
                if r > 0:
                    for s in range(2):
                        sp.wait_ge(stored[s], stored.at(r, 0))
                        sp.sem_inc(sp_turn, 1)
                if r in keep_loads:
                    sp.dma_start(keep[:], row(keep_dram[order(r)]).to_broadcast([P, EPAD])).then_inc(keep_in, 16)

                def edge_pair(i, r=r, kind=kind):
                    if kind == GAT:
                        for q in range(2):
                            sp.wait_ge(sums_ready[q], sums_ready.at(r, i))
                            sp.sem_inc(sp_turn, 1)
                            sp.dma_start(wt_bc[q][:], weight_v[bass.ds(i, 1), q].to_broadcast([P, BLOCK])).then_inc(extra_in[q], 16)
                    if kind == TR and not (isinstance(i, int) and i == PAIRS - 1):
                        load_attr(i + 1)

                def load_attr(i, r=r):
                    for q in range(2):
                        sp.wait_ge(at_ready[q], at_ready.at(r, i))
                        sp.sem_inc(sp_turn, 1)
                        sp.dma_start(attr[q][:], attr_v[bass.ds(i, 1), q].rearrange("o p k f -> (o p) k f")).then_inc(extra_in[q], 16)

                def before_units(i, r=r):
                    for q in range(2):
                        sp.wait_ge(scattered[q], scattered.at(r, i))
                    sp.sem_inc(sp_turn, 1)

                def load_h(u, r=r, h_of=h_of):
                    for s in range(2):
                        sp.wait_ge(htp_ready[s], htp_ready.at(r, u))
                        sp.sem_inc(sp_turn, 1)
                        sp.dma_start(flat(h_in[s], width(u, s)), group_dram(h_of, u, s)).then_inc(h_loaded[s], 16)

                def unit(u, r=r, res_of=res_of):
                    for s in range(2):
                        sp.wait_ge(sum_ready[s], sum_ready.at(r, u))
                        sp.sem_inc(sp_turn, 1)
                        sp.dma_start(flat(agg_in[s], width(u, s)), group_dram(agg[order(r)], u, s)).then_inc(agg_loaded[s], 16)
                    if res_of is not None:
                        for s in range(2):
                            sp.wait_ge(t2_ready[s], t2_ready.at(r, u))
                            sp.sem_inc(sp_turn, 1)
                            sp.dma_start(flat(res_in[s], width(u, s)), group_dram(res_of, u, s)).then_inc(res_loaded[s], 16)
                    if not isinstance(u, int) or u + 2 <= UNITS:
                        load_h(u + 2)

                if kind == TR:
                    load_attr(0)
                load_h(0)
                load_h(1)
                schedule(sp, r, edge_pair, before_units, unit)

            r = R_OUT
            for s in range(2):
                sp.wait_ge(stored[s], stored.at(r, 0))
                sp.sem_inc(sp_turn, 1)

            def out_unit(u, turn):
                for s in range(2):
                    sp.wait_ge(t2_ready[s], t2_ready.at(r, u))
                    sp.sem_inc(sp_turn, 1)
                    sp.dma_start(flat(agg_in[s], width(u, s)), group_dram(node_x, u, s)).then_inc(agg_loaded[s], 16)
                if not isinstance(u, int) or u + 2 <= UNITS:
                    load_h(u + 2, r, node_a)

            load_h(0, r, node_a)
            load_h(1, r, node_a)
            out_units(sp, out_unit)

        @block.gpsimd
        def _(pool):
            pool.memset(ident[:], 0.0).then_inc(prep_pool, 1)
            pool.memset(before_ones[:], 0.0).then_inc(prep_pool, 1)
            pool.memset(rest_ones[:], 1.0).then_inc(prep_pool, 1)
            pool.iota(place_i[:], pattern=[[1, BLOCK]], base=0, channel_multiplier=BLOCK).then_inc(prep_pool, 1)
            pool.iota(iota_i[:], pattern=[[1, DIGITS]], base=0, channel_multiplier=0).then_inc(prep_pool, 1)
            pool.wait_ge(prep_pool, 5)
            pool.affine_select(out=ident[:], in_=ident[:], compare_op=ALU.not_equal, fill=1.0, base=0,
                               pattern=[[-1, P]], channel_multiplier=1).then_inc(prep_pool, 1)
            pool.affine_select(out=before_ones[:], in_=before_ones[:], compare_op=ALU.is_ge, fill=1.0, base=0,
                               pattern=[[-1, P]], channel_multiplier=1).then_inc(prep_pool, 1)
            pool.affine_select(out=rest_ones[:], in_=rest_ones[:], compare_op=ALU.is_ge, fill=0.0, base=0,
                               pattern=[[-1, P]], channel_multiplier=1).then_inc(prep_pool, 1)
            for n in range(2):
                with pool.Fori(0, PAIRS) as i:
                    for q in range(2):
                        pool.wait_ge(slot_ready[q], n * PAIRS + i + 2)
                        pool.sem_inc(pool_turn, 1)
                        for k in range(CPB):
                            pool.indirect_dma_start(rec_dram[n], bass.IndirectOffsetOnAxis(place_idx[q][:, k:k + 1], 0),
                                                    rec_rows[q][:, k, :], None).then_inc(rec_out[q], 16)
            pool.wait_ge(tables_done, 1)
            pool.wait_ge(zeroed, ZERO_DMAS * 16)
            for r in range(NR):
                kind, _, h_of, _, _, _, _, _ = ROUNDS[r]
                if r > 0:
                    for s in range(2):
                        pool.wait_ge(stored[s], stored.at(r, 0))

                def gathers(q, r=r, kind=kind, h_of=h_of):
                    for k in range(CPB):
                        pool.indirect_dma_start(gath[q][:, k, :], None, h_of,
                                                bass.IndirectOffsetOnAxis(g_idx[q][:, k:k + 1], 0)).then_inc(gathered[q], 16)
                    if kind == TR:
                        for k in range(CPB):
                            pool.indirect_dma_start(gath_d[q][:, k, :], None, h_of,
                                                    bass.IndirectOffsetOnAxis(g_idx[q][:, CPB + k:CPB + k + 1], 0)).then_inc(gathered_d[q], 16)

                def scatters(q, r=r):
                    for k in range(CPB):
                        pool.indirect_dma_start(agg[order(r)], bass.IndirectOffsetOnAxis(s_idx[q][:, k:k + 1], 0), y_rows[q][:, k, :],
                                                None, bounds_check=N - 1, oob_is_err=False).then_inc(scattered[q], 16)

                for q in range(2):
                    pool.wait_ge(gidx_ready[q], gidx_ready.at(r, 1))
                    gathers(q)
                with pool.Fori(0, PAIRS - 1) as i:
                    for step, q in ((gathers, 0), (gathers, 1), (scatters, 0), (scatters, 1)) if kind != SAGE else (
                            (gathers, 0), (scatters, 0), (gathers, 1), (scatters, 1)):
                        if step == gathers:
                            pool.wait_ge(gt_ready[q], gt_ready.at(r, i + 1))
                            pool.wait_ge(gidx_ready[q], gidx_ready.at(r, i + 2))
                        else:
                            pool.wait_ge(sidx_ready[q], sidx_ready.at(r, i + 1))
                            pool.wait_ge(y_ready[q], y_ready.at(r, i + 1))
                        pool.sem_inc(pool_turn, 1)
                        step(q)
                for q in range(2):
                    pool.wait_ge(sidx_ready[q], sidx_ready.at(r, PAIRS))
                    pool.wait_ge(y_ready[q], y_ready.at(r, PAIRS))
                    scatters(q)

        @block.tensor
        def _(pe):
            pe.wait_ge(prep_pool, 8)
            pe.wait_ge(loaded, 16 * len(LOADS))
            for name, bank, col in PREP_W:
                pe.transpose(bank[:, col:col + P], natural[name][:], ident[:]).then_inc(prep_pe, 1)
            pe.transpose(pe_bank[3][0:EDIM, 0:P], we_nat[:], ident[:]).then_inc(prep_pe, 1)
            pe.wait_ge(att_ready, 1)
            pe.matmul(o_bank[0][:, 0:P], natural["W0"][:], att_rep[:], start=True, stop=True)
            pe.matmul(o_bank[0][:, P:P + 1], att_rep[:], cols[:, C_B0:C_B0 + 1], start=True, stop=True,
                      skip_group_check=True).then_inc(prep_pe, 1)
            pe.wait_ge(prep_act, 9)

            def transposed(tables, semaphore):
                for t, bank in tables:
                    for k in range(CPB):
                        last = pe.transpose(bank[:, k * BLOCKS:(k + 1) * BLOCKS], t[:, k * P:(k + 1) * P],
                                            ident[0:BLOCKS, 0:BLOCKS])
                last.then_inc(semaphore, 1)

            pe.wait_ge(last_start, 1)
            pe.transpose(pe_bank[0][0:1, 0:BLOCKS], carry_col[:], ident[0:BLOCKS, 0:BLOCKS]).then_inc(last_start_t, 1)
            pe.wait_ge(first_start, 1)
            pe.transpose(pe_bank[1][0:BLOCKS, 0:1], carry_row[:, 0:BLOCKS], ident[0:1, 0:1]).then_inc(first_start_t, 1)
            for t in range(2):
                pe.wait_ge(tab_ready, t + 1)
                pe.transpose(pe_bank[1][0:1, 0:BLOCKS], key_f[:, 0:1], ident[0:BLOCKS, 0:BLOCKS])
                transposed([(otherc_f, ht_bank[0]), (keyc_f, ht_bank[1]), (scat_f, o_bank[1])]
                           + ([(inv_f, pe_bank[0])] if t == 0 else []), tab_t)
                if t == 1:
                    break
                for n in range(2):
                    pe.wait_ge(sort_ready, n + 1)
                    pe.wait_ge(tab_used, 1)
                    transposed([(rec_f[:, :, 0] if n else other_f, ht_bank[0]), (rec_f[:, :, 1] if n else key_f, ht_bank[1]),
                                (rec_f[:, :, 2] if n else wt_f, o_bank[1]), (digit_f, pe_bank[0])], sort_t)
                    pe.wait_ge(sort_used, n + 1)
                    rank = pe_bank[2:4]
                    width_n = WIDTHS[n]
                    loop = 2 * n * BLOCKS
                    for m in range(2):
                        for first in range(0, width_n, P):
                            last = min(first + P, width_n)
                            pe.matmul(rank[m][:, first:last], no_ones[:], no_ones[:, 0:last - first], start=first == 0, stop=False,
                                      skip_group_check=True)
                    with pe.Fori(0, BLOCKS) as b:
                        for k in range(CPB):
                            pe.wait_ge(hot, (b + loop) * CPB + k + 1)
                            for m in range(2):
                                count = pe.matmul(rank[m][:, 0:width_n], all_ones[:], onehot[k][:, 0:width_n], start=False,
                                                  stop=False, skip_group_check=True)
                            count.then_inc(counted[k], 1)
                    loop += BLOCKS

                    def earlier(k):
                        pe.matmul(rank[k % 2][:, 0:width_n], before_ones[:], onehot[k][:, 0:width_n], start=False, stop=False,
                                  skip_group_check=True).then_inc(ranked, 1)

                    def the_rest(k, more):
                        pe.matmul(rank[k % 2][:, 0:width_n], rest_ones[:], onehot[k][:, 0:width_n], start=False, stop=False,
                                  skip_group_check=True).then_inc(counted[k], 1)
                        if more:
                            pe.matmul(rank[k % 2][:, 0:width_n], all_ones[:], onehot[(k + 1) % CPB][:, 0:width_n], start=False,
                                      stop=False, skip_group_check=True)

                    def rank_block(b, final):
                        for k in range(CPB):
                            more = not (final and k == CPB - 1)
                            if more:
                                pe.wait_ge(hot, (b + loop) * CPB + k + 2)
                                earlier((k + 1) % CPB)
                            pe.wait_ge(placed, (b + n * BLOCKS) * CPB + k + 2)
                            the_rest(k, more)

                    pe.wait_ge(hot, loop * CPB + 1)
                    earlier(0)
                    pe.matmul(rank[1][:, 0:width_n], all_ones[:], onehot[0][:, 0:width_n], start=False, stop=False,
                              skip_group_check=True)
                    with pe.Fori(0, BLOCKS - 1) as b:
                        rank_block(b, False)
                    rank_block(BLOCKS - 1, True)
            pe.wait_ge(tables_done, 1)

            for r in range(NR):
                kind, tail = ROUNDS[r][0:2]

                def sage_pair(i, r=r):
                    for q in range(2):
                        pe.wait_ge(gathered[q], gathered.at(r, i + 1))
                        pe.wait_ge(run_ready[q], run_ready.at(r, i))
                        for k in range(CPB):
                            last = pe.transpose(pe_bank[q][:, k * P:(k + 1) * P], gath[q][:, k, :], ident[:])
                        last.then_inc(gt_ready[q], 1)
                    for q in range(2):
                        pe.wait_ge(run_ready[q], run_ready.at(r, i + 1))
                        pe.wait_ge(y_ready[q], y_ready.at(r, i))
                        for k in range(CPB):
                            last = pe.matmul(pe_bank[2 + q][:, k * P:(k + 1) * P], run[q][:, k * P:(k + 1) * P],
                                             w_l[r][:], start=True, stop=True, skip_group_check=True)
                        last.then_inc(yp_ready[q], 1)

                def rows_out(i, q, r):
                    pe.wait_ge(sums_ready[q], sums_ready.at(r, i + 1))
                    for k in range(CPB):
                        pe.transpose(pe_bank[q][:, k * P:(k + 1) * P], num[q][:, k * P:(k + 1) * P], ident[:])
                    for k in range(CPB):
                        last = pe.matmul(pe_bank[2 + q][:, k * HEADS:(k + 1) * HEADS], den[q][:, k * P:(k + 1) * P],
                                         head_pick[:], start=True, stop=True, skip_group_check=True)
                    last.then_inc(yp_ready[q], 1)

                def gat_front(i, r=r):
                    for q in range(2):
                        pe.wait_ge(gathered[q], gathered.at(r, i + 1))
                        pe.wait_ge(y_ready[q], y_ready.at(r, i))
                        for k in range(CPB):
                            last = pe.transpose(pe_bank[q][:, k * P:(k + 1) * P], gath[q][:, k, :], ident[:])
                        last.then_inc(gt_ready[q], 1)
                    for q in range(2):
                        pe.wait_ge(gts_ready[q], gts_ready.at(r, i + 1))
                        pe.matmul(pe_bank[q][:], w_att[:], gsrc_t[q][:], start=True, stop=True).then_inc(lin_ready[q], 1)
                    for q in range(2):
                        pe.matmul(pe_bank[2 + q][:], w0_t[:], gsrc_t[q][:], start=True, stop=True).then_inc(val_ready[q], 1)

                def tr_front(i, r=r):
                    for q in range(2):
                        pe.wait_ge(gathered[q], gathered.at(r, i + 1))
                        pe.wait_ge(gathered_d[q], gathered_d.at(r, i + 1))
                        pe.wait_ge(y_ready[q], y_ready.at(r, i))
                        for k in range(CPB):
                            pe.transpose(pe_bank[q][:, k * P:(k + 1) * P], gath[q][:, k, :], ident[:])
                        for k in range(CPB):
                            last = pe.transpose(pe_bank[2 + q][:, k * P:(k + 1) * P], gath_d[q][:, k, :], ident[:])
                        last.then_inc(gt_ready[q], 1)
                    for q in range(2):
                        pe.wait_ge(extra_in[q], extra_in.at(r, i + 1))
                        pe.wait_ge(gts_ready[q], gts_ready.at(r, i + 1))
                        for k in range(CPB):
                            last = pe.transpose(pe_bank[q][0:EDIM, k * P:(k + 1) * P], attr[q][:, k, :], ident[:])
                        last.then_inc(at_ready[q], 1)
                    for q in range(2):
                        pe.matmul(pe_bank[2 + q][:], wq_t[:], gdst_t[q][:], start=True, stop=True)
                        pe.wait_ge(ats_ready[q], ats_ready.at(r, i + 1))
                        pe.matmul(pe_bank[q][:], wk_t[:], gsrc_t[q][:], start=True, stop=False)
                        pe.matmul(pe_bank[q][:], we_t[:], attr_t[q][:], start=False, stop=True).then_inc(lin_ready[q], 1)

                def gat_pair(i, r=r):
                    for q in range(2):
                        rows_out(i, q, r)
                    if not (isinstance(i, int) and i == PAIRS - 1):
                        gat_front(i + 1)

                def tr_pair(i, r=r):
                    for q in range(2):
                        pe.wait_ge(prod_ready[q], prod_ready.at(r, i + 1))
                        pe.matmul(pe_bank[q][:], score_ones[:], prod[q][:], start=True, stop=True).then_inc(score_ready[q], 1)
                    for q in range(2):
                        pe.matmul(pe_bank[2 + q][:], wv_t[:], gsrc_t[q][:], start=True, stop=False)
                        pe.matmul(pe_bank[2 + q][:], we_t[:], attr_t[q][:], start=False, stop=True).then_inc(val_ready[q], 1)
                    for q in range(2):
                        rows_out(i, q, r)
                    if not (isinstance(i, int) and i == PAIRS - 1):
                        tr_front(i + 1)

                def front(u, r=r, tail=tail):
                    for s in range(2):
                        p = width(u, s)
                        pe.wait_ge(h_loaded[s], h_loaded.at(r, u + 1))
                        pe.wait_ge(ht_ready[s], ht_ready.at(r, u))
                        if tail == "tr" and not (isinstance(u, int) and u == 0):
                            pe.wait_ge(bn_ready[s], bn_ready.at(r, u - 1))
                        for j in range(RPP):
                            last = pe.transpose(ht_bank[s][:, j * P:j * P + p], h_in[s][0:p, j, :], ident[0:p, 0:p])
                        last.then_inc(htp_ready[s], 1)
                    for s in range(2):
                        p = width(u, s)
                        pe.wait_ge(ht_ready[s], ht_ready.at(r, u + 1))
                        pe.wait_ge(sum_ready[s], sum_ready.at(r, u))
                        pe.matmul(o_bank[s][0:p, :], ones_parts[:, 0:p], b_parts[:, r, :].unsqueeze(1).to_broadcast([3, RPP, P]),
                                  start=True, stop=False, skip_group_check=True)
                        for j in range(RPP):
                            last = pe.matmul(o_bank[s][0:p, j * P:(j + 1) * P], h_t[s][:, j, 0:p], w_r[r][:],
                                             start=False, stop=j == RPP - 1, skip_group_check=True)
                        last.then_inc(mm_ready[s], 1)

                def unit(u, r=r, tail=tail):
                    if not isinstance(u, int) or u + 1 <= UNITS:
                        front(u + 1)
                    if tail == "tr":
                        for s in range(2):
                            p = width(u, s)
                            pe.wait_ge(out_ready[s], out_ready.at(r, u + 1))
                            if not isinstance(u, int) or u + 1 <= UNITS:
                                pe.wait_ge(ht_ready[s], ht_ready.at(r, u + 2))
                            for j in range(RPP):
                                last = pe.transpose(ht_bank[s][:, j * P:j * P + p], h_out[s][0:p, j, :], ident[0:p, 0:p])
                            last.then_inc(hot_ready[s], 1)

                if kind == GAT:
                    gat_front(0)
                if kind == TR:
                    tr_front(0)
                front(0)
                schedule(pe, r, {SAGE: sage_pair, GAT: gat_pair, TR: tr_pair}[kind], lambda i: None, unit)

            r = R_OUT

            def out_front(u):
                for s in range(2):
                    p = width(u, s)
                    pe.wait_ge(h_loaded[s], h_loaded.at(r, u + 1))
                    pe.wait_ge(ht_ready[s], ht_ready.at(r, u))
                    for j in range(RPP):
                        last = pe.transpose(ht_bank[s][:, j * P:j * P + p], h_in[s][0:p, j, :], ident[0:p, 0:p])
                    last.then_inc(htp_ready[s], 1)
                for s in range(2):
                    p = width(u, s)
                    pe.wait_ge(ht_ready[s], ht_ready.at(r, u + 1))
                    pe.wait_ge(t2_ready[s], t2_ready.at(r, u))
                    for j in range(RPP):
                        last = pe.transpose(o_bank[s][0:p, j * P:(j + 1) * P], h_t[s][:, j, 0:p], ident[:])
                    last.then_inc(mm_ready[s], 1)

            pe.wait_ge(bn_coef, 1)
            out_front(0)
            out_units(pe, lambda u, turn: out_front(u + 1) if not isinstance(u, int) or u < UNITS else None)

        @block.scalar
        def _(act):
            act.wait_ge(filled, FILLS)
            for t, first, p, j in [(t, *z) for t in range(2) for z in big_zero]:
                act.dma_start(agg[t][first:first + p * j].rearrange("(p j) f -> p (j f)", j=j),
                              zeros[0:p, 0:j * P]).then_inc(zeroed, 16)
            for to, bank, col in ([(w0_t, pe_bank[0], 0), (w_r[R_GAT], pe_bank[0], P), (wq_t, pe_bank[1], 0),
                                                 (wk_t, pe_bank[1], P), (wv_t, pe_bank[2], 0), (w_r[R_TR], pe_bank[2], P)]):
                act.wait_ge(prep_pe, 7)
                act.activation(to[:], bank[:, col:col + P], ACT.Copy).then_inc(prep_act, 1)
            act.activation(we_t[:], pe_bank[3][0:EDIM, 0:P], ACT.Copy).then_inc(prep_act, 1)
            act.wait_ge(prep_pe, 8)
            act.activation(w_att[:], o_bank[0][:, 0:P], ACT.Copy).then_inc(prep_act, 1)
            act.activation(cols[:, C_BATT:C_BATT + 1], o_bank[0][:, P:P + 1], ACT.Copy).then_inc(prep_act, 1)
            act.wait_ge(tables_done, 1)

            for r in range(NR):
                kind, tail, _, _, h_to, _, _, _ = ROUNDS[r]
                act.wait_ge(keep_in, 16 * len([x for x in keep_loads if x <= r]))

                def sage_pair(i, r=r):
                    for q in range(2):
                        act.wait_ge(yp_ready[q], yp_ready.at(r, i + 1))
                        act.wait_ge(scattered[q], scattered.at(r, i))
                        for k in range(CPB):
                            last = act.activation(y_rows[q][:, k, :], pe_bank[2 + q][:, k * P:(k + 1) * P], ACT.Copy,
                                                  scale=inv[:, bass.ds(2 * i + q, 1), k])
                        last.then_inc(y_ready[q], 1)

                def start_marks(i, q, r):
                    act.wait_ge(shift_ready[q], shift_ready.at(r, i))
                    act.activation(start_neg[q][:, 0:BLOCK], keep[:, bass.ds((2 * i + q) * BLOCK, BLOCK)], ACT.Copy,
                                   scale=BIG, bias=-BIG).then_inc(neg_ready[q], 1)

                def exponentials(i, q, r):
                    act.wait_ge(shift_ready[q], shift_ready.at(r, i + 1))
                    act.activation(carry[q][:, 1:2], carry[q][:, 0:1], ACT.Exp)
                    act.activation(expd[q][:], expd[q][:], ACT.Exp).then_inc(exp_ready[q], 1)

                def gat_front(i, r=r):
                    for q in range(2):
                        act.wait_ge(gt_ready[q], gt_ready.at(r, i + 1))
                        act.wait_ge(val_ready[q], val_ready.at(r, i))
                        act.activation(gsrc_t[q][:], pe_bank[q][:], ACT.Copy).then_inc(gts_ready[q], 1)
                    for q in range(2):
                        start_marks(i, q, r)
                    for q in range(2):
                        act.wait_ge(lin_ready[q], lin_ready.at(r, i + 1))
                        act.activation(logit_raw[q][:], pe_bank[q][:], ACT.Identity,
                                       bias=cols[:, C_BATT:C_BATT + 1]).then_inc(raw_ready[q], 1)

                def tr_front(i, r=r):
                    for q in range(2):
                        act.wait_ge(gt_ready[q], gt_ready.at(r, i + 1))
                        act.wait_ge(val_ready[q], val_ready.at(r, i))
                        act.wait_ge(score_ready[q], score_ready.at(r, i))
                        act.activation(gsrc_t[q][:], pe_bank[q][:], ACT.Copy)
                        act.activation(gdst_t[q][:], pe_bank[2 + q][:], ACT.Copy).then_inc(gts_ready[q], 1)
                    for q in range(2):
                        act.wait_ge(at_ready[q], at_ready.at(r, i + 1))
                        act.activation(attr_t[q][:], pe_bank[q][0:EDIM, :], ACT.Copy).then_inc(ats_ready[q], 1)
                    for q in range(2):
                        start_marks(i, q, r)
                    for q in range(2):
                        act.wait_ge(lin_ready[q], lin_ready.at(r, i + 1))
                        act.activation(logit_raw[q][:], pe_bank[q][:], ACT.Identity,
                                       bias=cols[:, C_BK:C_BK + 1]).then_inc(raw_ready[q], 1)

                def soft_pair(i, r=r, kind=kind):
                    if kind == GAT:
                        fetch(ACT.Exp, 2 * i + 1)
                    for q in range(2):
                        exponentials(i, q, r)
                    if kind == GAT:
                        fetch(ACT.Sqrt, 2 * i + 2)
                    if not (isinstance(i, int) and i == PAIRS - 1):
                        {GAT: gat_front, TR: tr_front}[kind](i + 1)

                def store(u, s, r, h_to):
                    act.wait_ge(out_ready[s], out_ready.at(r, u + 1))
                    act.dma_start(group_dram(h_to, u, s), flat(h_out[s], width(u, s))).then_inc(stored[s], 16)

                def front(u, r=r):
                    for s in range(2):
                        p = width(u, s)
                        act.wait_ge(htp_ready[s], htp_ready.at(r, u + 1))
                        act.wait_ge(mm_ready[s], mm_ready.at(r, u))
                        act.activation(h_t[s][:, :, 0:p], ht_bank[s][:].rearrange("p (j n) -> p j n", j=RPP)[:, :, 0:p],
                                       ACT.Copy).then_inc(ht_ready[s], 1)

                def unit(u, r=r, tail=tail, h_to=h_to):
                    ahead = not isinstance(u, int) or u + 1 <= UNITS
                    if ahead and tail != "gat":
                        front(u + 1)
                    if tail in ("norm", "norm_ln"):
                        for s in range(2):
                            p = width(u, s)
                            act.wait_ge(sum_ready[s], sum_ready.at(r, u + 1))
                            act.activation(sq[s][0:p], total[s][0:p], ACT.Square).then_inc(sq_ready[s], 1)
                            if tail == "norm_ln":
                                act.activation(t1[s][0:p], total[s][0:p], ACT.Relu).then_inc(t1_ready[s], 1)
                    if tail in ("relu", "tr"):
                        for s in range(2):
                            p = width(u, s)
                            act.wait_ge(sum_ready[s], sum_ready.at(r, u + 1))
                            act.wait_ge(stored[s], stored.at(r, u))
                            if tail == "tr":
                                act.wait_ge(hot_ready[s], hot_ready.at(r, u))
                            act.activation(h_out[s][0:p], total[s][0:p], ACT.Relu).then_inc(out_ready[s], 1)
                    if tail == "gat":
                        for s in range(2):
                            p = width(u, s)
                            act.wait_ge(sum_ready[s], sum_ready.at(r, u + 1))
                            act.activation(t1[s][0:p], total[s][0:p], ACT.Relu).then_inc(t1_ready[s], 1)
                    if ahead and tail == "gat":
                        front(u + 1)
                    if tail in ("norm", "norm_ln"):
                        for s in range(2):
                            p = width(u, s)
                            act.wait_ge(ss_ready[s], ss_ready.at(r, u + 1))
                            act.activation(small[s][0:p, 1, :], small[s][0:p, 0, :], ACT.Sqrt).then_inc(nrm_ready[s], 1)
                    if tail == "gat":
                        for s in range(2):
                            p = width(u, s)
                            act.wait_ge(gvar_ready[s], gvar_ready.at(r, u + 1))
                            act.activation(small[s][0:p, 1, :], small[s][0:p, 0, :], ACT.Sqrt).then_inc(gsd_ready[s], 1)
                        for s in range(2):
                            p = width(u, s)
                            act.wait_ge(grs_ready[s], grs_ready.at(r, u + 1))
                            act.wait_ge(out_ready[s], out_ready.at(r, u))
                            for j in range(RPP):
                                last = act.activation(t2[s][0:p, j, :], t1[s][0:p, j, :], ACT.Identity,
                                                      scale=small[s][0:p, 2, j:j + 1], bias=small2[s][0:p, 0, j:j + 1])
                            last.then_inc(gln_ready[s], 1)
                    if tail in ("norm_ln", "relu_ln", "gat"):
                        for s in range(2):
                            roots(u, s, r)
                        for s in range(2):
                            normalised(u, s, r)
                    for s in range(2):
                        store(u, s, r, h_to)

                def roots(u, s, r):
                    p = width(u, s)
                    act.wait_ge(var_ready[s], var_ready.at(r, u + 1))
                    act.activation(small[s][0:p, 4, :], small[s][0:p, 3, :], ACT.Sqrt).then_inc(sd_ready[s], 1)

                def normalised(u, s, r, of=t2, turn=0):
                    p = width(u, s)
                    act.wait_ge(rs_ready[s], rs_ready.at(r, u + 1))
                    act.wait_ge(stored[s], stored.at(r, u))
                    for j in range(RPP):
                        last = act.activation(h_out[s][0:p, j, :], of[s][0:p, j, :], ACT.Identity,
                                              scale=small2[s][0:p, 2 + 2 * turn, j:j + 1],
                                              bias=small2[s][0:p, 3 + 2 * turn, j:j + 1])
                    last.then_inc(out_ready[s], 1)

                def fetch(function, before):
                    act.wait_ge(fetched, before + 1)
                    act.activation(spark[:, 1:2], spark[:, 0:1], function).then_inc(fetched, 1)

                if r == 0:
                    act.wait_ge(zeroed, ZERO_DMAS * 16)
                    fetch(ACT.Sqrt, 0)
                if kind == TR:
                    fetch(ACT.Exp, 2 * PAIRS + 1)
                    tr_front(0)
                if kind == GAT:
                    gat_front(0)
                front(0)
                schedule(act, r, sage_pair if kind == SAGE else soft_pair, lambda i: None, unit)

            act.wait_ge(bn_var, 1)
            act.activation(bn_work[:, 3:4], bn_work[:, 2:3], ACT.Sqrt).then_inc(prep_act, 1)

            r = R_OUT
            act.wait_ge(bn_coef, 1)

            def out_front(u):
                for s in range(2):
                    p = width(u, s)
                    act.wait_ge(htp_ready[s], htp_ready.at(r, u + 1))
                    act.wait_ge(mm_ready[s], mm_ready.at(r, u))
                    act.activation(h_t[s][:, :, 0:p], ht_bank[s][:].rearrange("p (j n) -> p j n", j=RPP)[:, :, 0:p],
                                   ACT.Identity, scale=bn_work[:, 4:5], bias=bn_work[:, 5:6]).then_inc(ht_ready[s], 1)

            def out_unit(u, turn):
                if not isinstance(u, int) or u < UNITS:
                    out_front(u + 1)
                for s in range(2):
                    roots(u, s, r)
                for s in range(2):
                    normalised(u, s, r, (t2, total)[turn], turn)
                for s in range(2):
                    store(u, s, r, out)

            out_front(0)
            out_units(act, out_unit)
            for s in range(2):
                act.wait_ge(stored[s], stored.at(r, UNITS + 1))

        @block.vector
        def _(dve):
            NW = NOWHERE
            for t, v in ((dst_i[:], NW), (src_i[:], NW), (wt_f[:], 0.0), (zeros[:], 0.0), (ones_parts[:], 1.0),
                         (score_ones[:], float(D) ** -0.5), (head_mask[:], 0.0), (head_pick[:], 0.0), (start_neg[0][:], 0.0),
                         (start_neg[1][:], 0.0)):
                dve.memset(t, v).then_inc(filled, 1)
            dve.wait_ge(filled, FILLS)
            n = [0]

            def done(instruction):
                instruction.then_inc(prep, 1)
                n[0] += 1
                dve.wait_ge(prep, n[0])

            for h in range(HEADS):
                dve.memset(head_mask[h * HDIM:(h + 1) * HDIM, h * HDIM:(h + 1) * HDIM], 1.0)
                dve.memset(head_pick[h * HDIM:h * HDIM + 1, h:h + 1], 1.0)
            for q in range(2):
                for t in (run[q], seg_max[q], den[q]):
                    dve.memset(t[:], 0.0)
                dve.memset(unit_end[q][:], 0)
                dve.memset(idx[q][:, BLOCKS:BLOCKS + 2, :], 0)
            dve.memset(before_f[:], float(NW + 1))
            dve.memset(after_f[:], float(NW))
            dve.memset(all_ones[:], 1.0)
            dve.memset(no_ones[:], 0.0)
            dve.memset(spark[:], 0.0)
            dve.memset(carry[0][:], 0.0)
            dve.memset(carry[1][:], 0.0)
            dve.memset(rec_t[:], 0.0)
            done(dve.memset(carry_row[:], 0.0))
            dve.wait_ge(loaded, 16 * len(LOADS))
            done(dve.tensor_scalar(att_rep[:], head_mask[:], cols[:, C_ATT:C_ATT + 1], None, ALU.mult))
            dve.sem_inc(att_ready, 1)
            dve.wait_ge(prep_pool, 8)
            for part in range(3):
                done(dve.tensor_copy(b_low[:], b_rep[:]))
                done(dve.tensor_copy(b_wide[:], b_low[:]))
                if part == 0:
                    done(dve.tensor_scalar(b_parts[:], b_wide[:], ident[0:3, 0:1], None, ALU.mult))
                else:
                    done(dve.scalar_tensor_tensor(b_parts[:], b_wide[:], ident[0:3, part:part + 1], b_parts[:], ALU.mult, ALU.add))
                done(dve.tensor_tensor(b_rep[:], b_rep[:], b_wide[:], ALU.subtract))
            dve.tensor_copy(iota_f[:], iota_i[:])
            dve.tensor_copy(pos_f[:], place_i[:])
            dve.tensor_copy(key_f[:], dst_i[:])
            done(dve.tensor_copy(other_f[:], src_i[:]))

            def by_block(bank):
                return bank[:, 0:CPB * BLOCKS].rearrange("p (k b) -> p b k", k=CPB)

            def build_tables(t):
                dve.sem_inc(key_ready, 1)
                dve.wait_ge(ends_in, 32 * (t + 1))
                dve.tensor_tensor(keep_f[:, 1:BLOCK], key_f[:, 1:BLOCK], key_f[:, 0:BLOCK - 1], ALU.is_equal)
                done(dve.tensor_tensor(keep_f[:, 0:1], key_f[:, 0:1], before_f[:], ALU.is_equal))
                if t == 1:
                    dve.wait_ge(keep_out, 16)
                done(dve.tensor_copy(keep_u[:], keep_f[:]))
                dve.sem_inc(keep_ready, 1)
                dve.tensor_tensor(scat_f[:, 0:BLOCK - 1], key_f[:, 0:BLOCK - 1], key_f[:, 1:BLOCK], ALU.is_equal)
                done(dve.tensor_tensor(scat_f[:, BLOCK - 1:BLOCK], key_f[:, BLOCK - 1:BLOCK], after_f[:], ALU.is_equal))
                dve.scalar_tensor_tensor(scat_f[:], scat_f[:], float(NW), key_f[:], ALU.mult, ALU.add)
                dve.tensor_scalar(keyc_f[:], key_f[:], float(N - 1), None, ALU.min)
                done(dve.tensor_scalar(otherc_f[:], other_f[:], float(N - 1), None, ALU.min))
                if t == 0:
                    done(dve.tensor_tensor(start_f[:], keep_f[:], pos_f[:], ALU.mult))
                    done(dve.tensor_tensor(start_f[:], pos_f[:], start_f[:], ALU.subtract))
                    done(dve.tensor_reduce(carry_col[:], start_f[:], AX_X, ALU.max))
                    dve.sem_inc(last_start, 1)
                    dve.wait_ge(last_start_t, 1)
                    done(dve.tensor_tensor_scan(carry_row[:, 1:BLOCKS + 1], zeros[0:1, 0:BLOCKS],
                                                pe_bank[0][0:1, 0:BLOCKS], 0.0, ALU.add, ALU.max))
                    dve.sem_inc(first_start, 1)
                    dve.wait_ge(first_start_t, 1)
                    done(dve.tensor_copy(carry_col[:], pe_bank[1][0:BLOCKS, 0:1]))
                    done(dve.tensor_tensor_scan(inv_f[:], start_f[:], start_f[:], carry_col[:], ALU.max, ALU.max))
                    done(dve.tensor_tensor(inv_f[:], pos_f[:], inv_f[:], ALU.subtract))
                    done(dve.tensor_scalar(inv_f[:], inv_f[:], 1.0, None, ALU.add))
                    done(dve.reciprocal(inv_f[:], inv_f[:]))
                dve.sem_inc(tab_ready, 1)
                dve.wait_ge(tab_t, t + 1)
                dve.tensor_copy(idx[t][:, 0:BLOCKS, 0:CPB], by_block(ht_bank[0]))
                dve.tensor_copy(idx[t][:, 0:BLOCKS, CPB:2 * CPB], by_block(ht_bank[1]))
                dve.tensor_copy(idx[t][:, 0:BLOCKS, 2 * CPB:3 * CPB], by_block(o_bank[1]))
                if t == 0:
                    dve.tensor_copy(inv[:], by_block(pe_bank[0]))
                end = unit_end[t][0:1, 1:PAIRS + 1]
                done(dve.tensor_copy(end, pe_bank[1][0:1, 0:BLOCKS].rearrange("o (i q) -> o i q", q=2)[:, :, 0]))
                done(dve.tensor_scalar(end, end, SHIFT, None, ALU.logical_shift_right))
                done(dve.tensor_scalar(end, end, float(UNITS - 3), None, ALU.min))
                dve.sem_inc(tab_used, 1)

            build_tables(0)
            for semaphore in (*counted, placed, *slot_ready):
                dve.sem_inc(semaphore, 1)
            for n_pass in range(2):
                if n_pass == 0:
                    done(dve.tensor_scalar(digit_i[:], src_i[:], DIGITS - 1, None, ALU.bitwise_and))
                else:
                    dve.wait_ge(rec_in, 16)
                    done(dve.tensor_copy(src_i[:], rec_f[:, :, 0]))
                    done(dve.tensor_scalar(digit_i[:], src_i[:], LOW_BITS, None, ALU.logical_shift_right))
                done(dve.tensor_copy(digit_f[:], digit_i[:]))
                dve.sem_inc(sort_ready, 1)
                dve.wait_ge(sort_t, n_pass + 1)
                for c, bank in enumerate((ht_bank[0], ht_bank[1], o_bank[1])):
                    dve.tensor_copy(rec_t[:, :, :, c], by_block(bank))
                done(dve.tensor_copy(digit_t[:], by_block(pe_bank[0])))
                dve.sem_inc(sort_used, 1)
                loop = 2 * n_pass * BLOCKS
                width_n = WIDTHS[n_pass]
                with dve.Fori(0, BLOCKS) as b:
                    for k in range(CPB):
                        dve.wait_ge(counted[k], b + loop + 1)
                        dve.tensor_scalar(onehot[k][:, 0:width_n], iota_f[:, 0:width_n], digit_t[:, bass.ds(b, 1), k], None,
                                          ALU.is_gt).then_inc(hot, 1)
                loop += BLOCKS

                def one_hot(b, k):
                    dve.wait_ge(counted[k], b + loop + 1)
                    dve.tensor_scalar(onehot[k][:, 0:width_n], iota_f[:, 0:width_n], digit_t[:, bass.ds(b, 1), k], None,
                                      ALU.is_equal).then_inc(hot, 1)

                def place_pair(i, final):
                    for q in range(2):
                        b = 2 * i + q
                        for k in range(CPB):
                            dve.wait_ge(hot, (b + loop) * CPB + k + 1)
                            dve.wait_ge(placed, (b + n_pass * BLOCKS) * CPB + k + 1)
                            if k == 0:
                                dve.wait_ge(slot_ready[1 - q], i + q + n_pass * PAIRS + 1)
                            dve.wait_ge(ranked, (b + n_pass * BLOCKS) * CPB + k + 1)
                            dve.tensor_tensor_reduce(picked[:, 0:width_n], onehot[k][:, 0:width_n], pe_bank[2 + k % 2][:, 0:width_n],
                                                     1.0, 0.0, ALU.mult, ALU.add, place_f[:, k:k + 1]).then_inc(placed, 1)
                            if k == 0:
                                one_hot(b, CPB - 1)
                            elif not (final and q == 1):
                                one_hot(b + 1, k - 1)
                        dve.wait_ge(placed, (b + n_pass * BLOCKS) * CPB + CPB + 1)
                        dve.wait_ge(rec_out[q], (i + n_pass * PAIRS) * CPB * 16)
                        dve.tensor_copy(place_idx[q][:], place_f[:])
                        dve.tensor_copy(rec_rows[q][:], rec_t[:, bass.ds(b, 1), :, :].rearrange("p o k c -> p (o k) c")
                                        ).then_inc(slot_ready[q], 1)

                for k in range(CPB - 1):
                    one_hot(0, k)
                with dve.Fori(0, PAIRS - 1) as i:
                    place_pair(i, False)
                place_pair(PAIRS - 1, True)
            dve.wait_ge(rec_in, 32)
            dve.tensor_copy(key_f[:], rec_f[:, :, 0])
            dve.tensor_copy(other_f[:], rec_f[:, :, 1])
            done(dve.tensor_copy(wt_f[:], rec_f[:, :, 2]))
            build_tables(1)
            dve.wait_ge(prep_act, 9)
            for stage in Stage.every:
                for s in range(2):
                    if stage.step == 1:
                        dve.sem_inc(stage[s], 1)
            dve.sem_inc(fetched, 1)
            dve.sem_inc(edge_steps, 1)
            dve.sem_inc(unit_steps, 1)
            dve.sem_inc(tables_done, 1)

            esteps, usteps = 1, 1
            for r in range(NR):
                kind, tail = ROUNDS[r][0:2]
                eper = {SAGE: 0, GAT: 2 * 8, TR: 2 * 6}[kind]
                uper = {"norm": 2 * 2, "norm_ln": 2 * 5, "relu": 0, "relu_ln": 2 * 3, "gat": 2 * 8, "tr": 0}[tail]

                dve.wait_ge(keep_in, 16 * len([x for x in keep_loads if x <= r]))
                for q in range(2):
                    dve.wait_ge(gathered[q], gathered.at(r, 0))
                    dve.tensor_copy(g_idx[q][:], idx[order(r)][:, q, 0:2 * CPB]).then_inc(gidx_ready[q], 1)

                def next_gather(i, q, r):
                    dve.wait_ge(gathered[q], gathered.at(r, i + 1))
                    if ROUNDS[r][0] == TR:
                        dve.wait_ge(gathered_d[q], gathered_d.at(r, i + 1))
                    dve.tensor_copy(g_idx[q][:], idx[order(r)][:, bass.ds(2 * i + 2 + q, 1), 0:2 * CPB].rearrange("p o k -> p (o k)")
                                    ).then_inc(gidx_ready[q], 1)

                def next_scatter(i, q, r):
                    dve.wait_ge(scattered[q], scattered.at(r, i))
                    dve.tensor_copy(s_idx[q][:], idx[order(r)][:, bass.ds(2 * i + q, 1), 2 * CPB:3 * CPB].rearrange("p o k -> p (o k)")
                                    ).then_inc(sidx_ready[q], 1)

                def keep_of(i, q):
                    return keep[:, bass.ds((2 * i + q) * BLOCK, BLOCK)]

                def sage_pair(i, r=r):
                    for q in range(2):
                        next_gather(i, q, r)
                        dve.wait_ge(gt_ready[q], gt_ready.at(r, i + 1))
                        dve.wait_ge(yp_ready[q], yp_ready.at(r, i))
                        dve.wait_ge(run_ready[1 - q], run_ready.at(r, i + q))
                        dve.tensor_tensor_scan(run[q][:], keep_of(i, q), pe_bank[q][:], run[1 - q][:, BLOCK - 1:BLOCK],
                                               ALU.mult, ALU.add).then_inc(run_ready[q], 1)
                        next_scatter(i, q, r)

                def maxima(i, q, r, st, logits):
                    before = 1 - q
                    dve.wait_ge(neg_ready[q], neg_ready.at(r, i + 1))
                    st.wait()
                    st.done(dve.tensor_tensor_scan(seg_max[q][:], start_neg[q][:, 0:BLOCK], logits,
                                                   seg_max[before][:, BLOCK - 1:BLOCK], ALU.add, ALU.max))
                    st.done(dve.tensor_tensor_scan(full_max[q][:, ::-1], start_neg[q][:, BLOCK:0:-1], seg_max[q][:, ::-1], -BIG,
                                                   ALU.add, ALU.max))
                    st.mark(dve.tensor_scalar(carry[q][:, 0:1], seg_max[before][:, BLOCK - 1:BLOCK], full_max[q][:, 0:1], 0.0,
                                              ALU.subtract, ALU.min))
                    dve.tensor_tensor(expd[q][:], logits, full_max[q][:], ALU.subtract).then_inc(shift_ready[q], 1)

                def sums(i, q, r, st, values, bias_col, weighted_by):
                    before = 1 - q
                    dve.wait_ge(exp_ready[q], exp_ready.at(r, i + 1))
                    if weighted_by is not None:
                        dve.wait_ge(extra_in[q], extra_in.at(r, i + 1))
                        st.done(dve.tensor_tensor(expd[q][:], expd[q][:], weighted_by, ALU.mult))
                    if q == 0:
                        dve.wait_ge(sums_ready[1], sums_ready.at(r, i))
                    else:
                        dve.wait_ge(sums_ready[0], sums_ready.at(r, i + 1))
                    dve.tensor_scalar(carry[q][:, 2:3], den[before][:, BLOCK - 1:BLOCK], carry[q][:, 1:2], None, ALU.mult)
                    dve.tensor_scalar(carry[q][:, 3:4], num[before][:, BLOCK - 1:BLOCK], carry[q][:, 1:2], None, ALU.mult)
                    st.done(dve.scalar_tensor_tensor(msg[q][:], values, bias_col, expd[q][:], ALU.add, ALU.mult))
                    dve.wait_ge(yp_ready[q], yp_ready.at(r, i))
                    dve.tensor_tensor_scan(den[q][:], keep_of(i, q), expd[q][:], carry[q][:, 2:3], ALU.mult, ALU.add)
                    dve.tensor_tensor_scan(num[q][:], keep_of(i, q), msg[q][:], carry[q][:, 3:4], ALU.mult,
                                           ALU.add).then_inc(sums_ready[q], 1)

                def divided_rows(i, q, r, st):
                    dve.wait_ge(yp_ready[q], yp_ready.at(r, i + 1))
                    st.done(dve.tensor_scalar(den_inv[q][:, 0], pe_bank[2 + q][:, 0:CPB * HEADS], 1e-10, None, ALU.max))
                    st.done(dve.reciprocal(den_inv[q][:, 1], den_inv[q][:, 0]))
                    dve.wait_ge(scattered[q], scattered.at(r, i))
                    dve.tensor_tensor(y_rows[q][:].rearrange("p k (h d) -> p (k h) d", h=HEADS),
                                      pe_bank[q][:].rearrange("p (n d) -> p n d", d=HDIM),
                                      den_inv[q][:, 1].unsqueeze(2).to_broadcast([P, CPB * HEADS, HDIM]),
                                      ALU.mult).then_inc(y_ready[q], 1)

                def gat_pair(i, r=r, base=esteps, per=eper):
                    st = Steps(dve, edge_steps, base, per, i)
                    for q in range(2):
                        next_gather(i, q, r)
                        dve.wait_ge(raw_ready[q], raw_ready.at(r, i + 1))
                        st.done(dve.scalar_tensor_tensor(logit[q][:], logit_raw[q][:], 0.2, logit_raw[q][:], ALU.mult, ALU.max))
                        maxima(i, q, r, st, logit[q][:])
                    for q in range(2):
                        dve.wait_ge(val_ready[q], val_ready.at(r, i + 1))
                        sums(i, q, r, st, pe_bank[2 + q][:], cols[:, C_B0:C_B0 + 1], wt_bc[q][:])
                    for q in range(2):
                        divided_rows(i, q, r, st)
                        next_scatter(i, q, r)
                    st.end()

                def tr_pair(i, r=r, base=esteps, per=eper):
                    st = Steps(dve, edge_steps, base, per, i)
                    for q in range(2):
                        next_gather(i, q, r)
                        dve.wait_ge(raw_ready[q], raw_ready.at(r, i + 1))
                        dve.scalar_tensor_tensor(prod[q][:], pe_bank[2 + q][:], cols[:, C_BQ:C_BQ + 1], logit_raw[q][:],
                                                 ALU.add, ALU.mult).then_inc(prod_ready[q], 1)
                    for q in range(2):
                        dve.wait_ge(score_ready[q], score_ready.at(r, i + 1))
                        maxima(i, q, r, st, pe_bank[q][:])
                    for q in range(2):
                        dve.wait_ge(val_ready[q], val_ready.at(r, i + 1))
                        sums(i, q, r, st, pe_bank[2 + q][:], cols[:, C_BV:C_BV + 1], None)
                    for q in range(2):
                        divided_rows(i, q, r, st)
                        next_scatter(i, q, r)
                    st.end()

                def statistics(st, s, p, of):
                    for j in range(RPP):
                        last = dve.bn_stats(st6[s][0:p, j, :], of[0:p, j, :])
                    st.done(last)
                    dve.sem_inc(dve_turn, 1)
                    for j in range(RPP):
                        last = dve.bn_aggr(mv[s][0:p, j, :], st6[s][0:p, j, :])
                    st.done(last)

                def layer_norm(st, u, r, of=t2, turn=0):
                    for s in range(2):
                        p = width(u, s)
                        statistics(st, s, p, of[s])
                        dve.tensor_scalar(small[s][0:p, 3, :], mv[s][0:p, :, 1], LN_EPS, None, ALU.add).then_inc(var_ready[s], 1)
                    for s in range(2):
                        p = width(u, s)
                        scale = small2[s][0:p, 2 + 2 * turn, :]
                        dve.wait_ge(sd_ready[s], sd_ready.at(r, u + 1))
                        st.done(dve.reciprocal(scale, small[s][0:p, 4, :]))
                        dve.scalar_tensor_tensor(small2[s][0:p, 3 + 2 * turn, :], mv[s][0:p, :, 0], -1.0, scale,
                                                 ALU.mult, ALU.mult).then_inc(rs_ready[s], 1)

                def unit(u, r=r, tail=tail, base=usteps, per=uper):
                    st = Steps(dve, unit_steps, base, per, u)
                    for s in range(2):
                        p = width(u, s)
                        dve.wait_ge(mm_ready[s], mm_ready.at(r, u + 1))
                        dve.wait_ge(agg_loaded[s], agg_loaded.at(r, u + 1))
                        if r not in ln_rounds:
                            dve.wait_ge(out_ready[s], out_ready.at(r, u))
                        dve.tensor_tensor(flat(total[s], p), o_bank[s][0:p, :], flat(agg_in[s], p), ALU.add).then_inc(sum_ready[s], 1)
                    if tail in ("norm", "norm_ln"):
                        for s in range(2):
                            p = width(u, s)
                            dve.wait_ge(sq_ready[s], sq_ready.at(r, u + 1))
                            dve.tensor_reduce(small[s][0:p, 0, :], sq[s][0:p], AX_X, ALU.add).then_inc(ss_ready[s], 1)
                        for s in range(2):
                            p = width(u, s)
                            dve.wait_ge(nrm_ready[s], nrm_ready.at(r, u + 1))
                            st.done(dve.tensor_scalar(small[s][0:p, 2, :], small[s][0:p, 1, :], 1e-12, None, ALU.max))
                            st.done(dve.reciprocal(small[s][0:p, 5, :], small[s][0:p, 2, :]))
                            if tail == "norm":
                                dve.wait_ge(stored[s], stored.at(r, u))
                                for j in range(RPP):
                                    last = dve.tensor_scalar(h_out[s][0:p, j, :], total[s][0:p, j, :], small[s][0:p, 5, j:j + 1],
                                                             0.0, ALU.mult, ALU.max)
                                last.then_inc(out_ready[s], 1)
                            else:
                                dve.wait_ge(t1_ready[s], t1_ready.at(r, u + 1))
                                dve.wait_ge(res_loaded[s], res_loaded.at(r, u + 1))
                                dve.wait_ge(out_ready[s], out_ready.at(r, u))
                                for j in range(RPP):
                                    last = dve.scalar_tensor_tensor(t2[s][0:p, j, :], t1[s][0:p, j, :], small[s][0:p, 5, j:j + 1],
                                                                    res_in[s][0:p, j, :], ALU.mult, ALU.add)
                                last.then_inc(t2_ready[s], 1)
                    if tail == "relu_ln":
                        for s in range(2):
                            p = width(u, s)
                            dve.wait_ge(res_loaded[s], res_loaded.at(r, u + 1))
                            dve.wait_ge(sum_ready[s], sum_ready.at(r, u + 1))
                            dve.wait_ge(out_ready[s], out_ready.at(r, u))
                            dve.scalar_tensor_tensor(flat(t2[s], p), flat(total[s], p), 0.0, flat(res_in[s], p), ALU.max,
                                                     ALU.add).then_inc(t2_ready[s], 1)
                    if tail == "gat":
                        for s in range(2):
                            p = width(u, s)
                            dve.wait_ge(t1_ready[s], t1_ready.at(r, u + 1))
                            statistics(st, s, p, t1[s])
                            dve.tensor_scalar(small[s][0:p, 0, :], mv[s][0:p, :, 1], 1e-9, None, ALU.add).then_inc(gvar_ready[s], 1)
                        for s in range(2):
                            p = width(u, s)
                            dve.wait_ge(gsd_ready[s], gsd_ready.at(r, u + 1))
                            st.done(dve.reciprocal(small[s][0:p, 2, :], small[s][0:p, 1, :]))
                            dve.scalar_tensor_tensor(small2[s][0:p, 0, :], mv[s][0:p, :, 0], -1.0, small[s][0:p, 2, :],
                                                     ALU.mult, ALU.mult).then_inc(grs_ready[s], 1)
                        for s in range(2):
                            p = width(u, s)
                            dve.wait_ge(res_loaded[s], res_loaded.at(r, u + 1))
                            st.mark(dve.tensor_tensor(res_in[s][0:p], res_in[s][0:p], bc_rows(offset_bc, p), ALU.add))
                        for s in range(2):
                            p = width(u, s)
                            dve.wait_ge(gln_ready[s], gln_ready.at(r, u + 1))
                            st.done(dve.tensor_tensor(t2[s][0:p], t2[s][0:p], bc_rows(scale_bc, p), ALU.mult))
                            dve.tensor_tensor(t2[s][0:p], t2[s][0:p], res_in[s][0:p], ALU.add).then_inc(t2_ready[s], 1)
                    if tail in ("norm_ln", "relu_ln", "gat"):
                        for s in range(2):
                            dve.wait_ge(t2_ready[s], t2_ready.at(r, u + 1))
                        layer_norm(st, u, r)
                    if tail == "tr":
                        for s in range(2):
                            p = width(u, s)
                            g = 2 * u + s
                            dve.wait_ge(hot_ready[s], hot_ready.at(r, u + 1))
                            place = bn_stat[:, g, :] if isinstance(u, int) else bn_stat[:, bass.ds(g, 1), :].rearrange("p o c -> p (o c)")
                            dve.bn_stats(place, ht_bank[s][:].rearrange("p (j n) -> p j n", j=RPP)[:, :, 0:p]).then_inc(bn_ready[s], 1)
                    st.end()

                schedule(dve, r, {SAGE: sage_pair, GAT: gat_pair, TR: tr_pair}[kind], lambda i: None, unit)
                esteps += eper * PAIRS
                usteps += uper * (UNITS + 1)

            for s in range(2):
                dve.wait_ge(bn_ready[s], bn_ready.at(R_TR, UNITS + 1))
            done(dve.bn_aggr(bn_work[:, 0:2], bn_stat[:].rearrange("p g c -> p (g c)")))
            done(dve.tensor_scalar(bn_work[:, 2:3], bn_work[:, 1:2], 1e-5, None, ALU.add))
            dve.sem_inc(bn_var, 1)
            dve.wait_ge(prep_act, 10)
            done(dve.reciprocal(bn_work[:, 6:7], bn_work[:, 3:4]))
            done(dve.tensor_tensor(bn_work[:, 4:5], cols[:, C_GAMMA:C_GAMMA + 1], bn_work[:, 6:7], ALU.mult))
            done(dve.tensor_tensor(bn_work[:, 7:8], bn_work[:, 0:1], bn_work[:, 4:5], ALU.mult))
            done(dve.tensor_tensor(bn_work[:, 5:6], cols[:, C_BETA:C_BETA + 1], bn_work[:, 7:8], ALU.subtract))
            dve.sem_inc(bn_coef, 1)

            r = R_OUT
            oper = 2 * 3

            def out_unit(u, turn):
                st = Steps(dve, unit_steps, usteps, oper, u)
                of = (t2, total)[turn]
                for s in range(2):
                    p = width(u, s)
                    dve.wait_ge(mm_ready[s], mm_ready.at(r, u + 1))
                    dve.wait_ge(agg_loaded[s], agg_loaded.at(r, u + 1))
                    dve.wait_ge(out_ready[s], out_ready.at(r, u - 1))
                    dve.tensor_tensor(flat(of[s], p), o_bank[s][0:p, :], flat(agg_in[s], p), ALU.add).then_inc(t2_ready[s], 1)
                for s in range(2):
                    dve.wait_ge(t2_ready[s], t2_ready.at(r, u + 1))
                layer_norm(st, u, r, of, turn)
                st.end()

            out_units(dve, out_unit)


_INS = ["x", "src", "dst", "edge_attr_10", "edge_weight", "L0_gnn_W1_l", "L0_gnn_b1_l", "L0_gnn_W1_r", "L0_gnn_W2_l",
        "L0_gnn_b2_l", "L0_gnn_W2_r", "L1_gnn_Wl", "L1_gnn_Wr", "L1_gnn_b", "L2_gnn_W0", "L2_gnn_b0", "L2_gnn_W1",
        "L2_gnn_b1", "L2_gnn_att", "L2_gnn_scale", "L2_gnn_offset", "L3_gnn_Wq", "L3_gnn_bq", "L3_gnn_Wk", "L3_gnn_bk",
        "L3_gnn_Wv", "L3_gnn_bv", "L3_gnn_We", "L3_gnn_Wskip", "L3_gnn_bskip", "L3_gnn_gamma", "L3_gnn_beta"]


def kernel(**inputs):
    import numpy as _np
    import concourse.bacc as _bacc
    from concourse.bass_utils import run_bass_kernel_spmd as _run

    nc = _bacc.Bacc("TRN2", target_bir_lowering=False, num_devices=1)
    arrays, io = {}, {}
    for name in _INS:
        a = _np.ascontiguousarray(inputs[name])
        arrays[f"in_{name}_dram"] = a
        io[name] = nc.dram_tensor(f"in_{name}_dram", a.shape, mybir.dt.from_np(a.dtype), kind="ExternalInput").ap()
    out = nc.dram_tensor("out_0_dram", inputs["x"].shape, F32, kind="ExternalOutput").ap()
    gnn_kernel(nc, io, out)
    r = _run(nc, [arrays], core_ids=[0])
    return r.results[0]["out_0_dram"]
```
